# Optimizing a Trainium2 kernel written in Bass

```python
import numpy as np
import jax
import jax.numpy as jnp

def _softmax(x, axis=-1):
    return jax.nn.softmax(x, axis=axis)

def _gelu(x):
    return jax.nn.gelu(x, approximate=True)

def _silu(x):
    return jax.nn.silu(x)

def _sigmoid(x):
    return jax.nn.sigmoid(x)

def _layernorm(x, axis=-1, eps=1e-05):
    m = jnp.mean(x, axis=axis, keepdims=True)
    v = jnp.var(x, axis=axis, keepdims=True)
    return (x - m) / jnp.sqrt(v + eps)

def _scatter_add(tgt, idx, src, axis=0):
    return tgt.at[idx].add(src)

def _segment_sum(src, seg, n):
    return jax.ops.segment_sum(src, seg, n)
kernel_name = 'mk_gnn_resnorm_d4_gnn_r64_42bc26'

def setup_inputs(seed: int=0):
    np.random.seed(seed)
    _w = jnp.asarray

    def _rec_inputs():
        import jax
        import jax.numpy as jnp
        _gk = jax.random.key(seed)
        x = -0.000202 + 1 * jax.random.normal(jax.random.fold_in(_gk, 1), (100000, 64), jnp.float32)
        src = jax.random.randint(jax.random.fold_in(_gk, 2), (25000,), 0, 100000, jnp.int32)
        dst = jax.random.randint(jax.random.fold_in(_gk, 3), (25000,), 0, 100000, jnp.int32)
        _o = jnp.argsort(dst, stable=True)
        src = src[_o]
        dst = dst[_o]
        edge_weight = jax.random.uniform(jax.random.fold_in(_gk, 12), (25000,), jnp.float32, 0.0, 0.999999)
        return (x, src, dst, edge_weight)
    x, src, dst, edge_weight = _rec_inputs()

    def _L0_gnn_setup():
        import jax, jax.numpy as jnp
        import numpy as np
        N_NODES = 100000
        key = jax.random.key(seed)
        k1, k2 = jax.random.split(key)
        node_features = jax.random.normal(k1, (N_NODES, 64), dtype=jnp.float32)
        edge_index = jax.random.randint(k2, (2, 25000), 0, N_NODES, dtype=jnp.int64)
        return {'node_features': node_features, 'edge_index': edge_index}
    _L0_gnn_all = _L0_gnn_setup()
    _L0_gnn_in = {k: v for k, v in _L0_gnn_all.items() if k in ()}
    del _L0_gnn_all

    def _L1_gnn_setup():
        import jax, jax.numpy as jnp
        import numpy as np
        N_NODES = 50000
        N_EDGES = 25000
        N_FEAT = 64
        key = jax.random.key(seed)
        k1, k2, k3 = jax.random.split(key, 3)
        x = jax.random.normal(k1, (N_NODES, N_FEAT), dtype=jnp.float32)
        edge_index = jax.random.randint(k2, (2, N_EDGES), 0, N_NODES, dtype=jnp.int64)
        edge_weights = jax.random.uniform(k3, (N_EDGES,), dtype=jnp.float32)
        return {'x': x, 'edge_index': edge_index, 'edge_weights': edge_weights}
    _L1_gnn_all = _L1_gnn_setup()
    _L1_gnn_in = {k: v for k, v in _L1_gnn_all.items() if k in ()}
    del _L1_gnn_all

    def _L2_gnn_setup():
        import jax, jax.numpy as jnp
        import numpy as np
        N_NODES = 50000
        N_EDGES = 12500
        D_FEAT = 64
        D_HID = 128
        D_OUT = 64
        key = jax.random.key(seed)
        k1, k2, k3, k4 = jax.random.split(key, 4)
        x = jax.random.normal(k1, (N_NODES, D_FEAT), dtype=jnp.float32)
        edge_index = jax.random.randint(k2, (2, N_EDGES), 0, N_NODES, dtype=jnp.int64)
        W1 = jax.random.normal(k3, (2 * D_FEAT, D_HID), dtype=jnp.float32) / np.sqrt(2 * D_FEAT)
        b1 = jnp.zeros((D_HID,), dtype=jnp.float32)
        W2 = jax.random.normal(k4, (D_HID, D_OUT), dtype=jnp.float32) / np.sqrt(D_HID)
        b2 = jnp.zeros((D_OUT,), dtype=jnp.float32)
        return {'x': x, 'edge_index': edge_index, 'W1': W1, 'b1': b1, 'W2': W2, 'b2': b2}
    _L2_gnn_all = _L2_gnn_setup()
    _L2_gnn_in = {k: v for k, v in _L2_gnn_all.items() if k in ('W1', 'b1', 'W2', 'b2')}
    del _L2_gnn_all

    def _L3_gnn_setup():
        import jax, jax.numpy as jnp
        import numpy as np
        N_NODES = 100000
        N_EDGES = 25000
        F_IN = 64
        F_HID = 64

        def gcn_conv(x, src, dst, W, b, n_nodes):
            h = x @ W
            deg = jax.ops.segment_sum(jnp.ones_like(dst, dtype=h.dtype), dst, num_segments=n_nodes)
            dinv = jnp.where(deg > 0, jax.lax.rsqrt(deg), 0.0)
            norm = dinv[src] * dinv[dst]
            msgs = h[src] * norm[:, None]
            out = jax.ops.segment_sum(msgs, dst, num_segments=n_nodes)
            return out + b
        key = jax.random.key(seed)
        k1, k2, k3, k4, k5 = jax.random.split(key, 5)
        x = jax.random.normal(k1, (N_NODES, F_IN), dtype=jnp.float32)
        edge_index = jax.random.randint(k2, (2, N_EDGES), 0, N_NODES, dtype=jnp.int64)
        s1 = float(np.sqrt(6.0 / (F_IN + F_HID)))
        s2 = float(np.sqrt(6.0 / (F_HID + F_HID)))
        W1 = jax.random.uniform(k3, (F_IN, F_HID), dtype=jnp.float32, minval=-s1, maxval=s1)
        b1 = jnp.zeros((F_HID,), dtype=jnp.float32)
        W2 = jax.random.uniform(k4, (F_HID, F_HID), dtype=jnp.float32, minval=-s2, maxval=s2)
        b2 = jnp.zeros((F_HID,), dtype=jnp.float32)
        return {'x': x, 'edge_index': edge_index, 'W1': W1, 'b1': b1, 'W2': W2, 'b2': b2}
    _L3_gnn_all = _L3_gnn_setup()
    _L3_gnn_in = {k: v for k, v in _L3_gnn_all.items() if k in ('W1', 'b1', 'W2', 'b2')}
    del _L3_gnn_all
    return {'x': x, 'src': src, 'dst': dst, 'edge_weight': edge_weight, 'L2_gnn_W1': _L2_gnn_in['W1'], 'L2_gnn_b1': _L2_gnn_in['b1'], 'L2_gnn_W2': _L2_gnn_in['W2'], 'L2_gnn_b2': _L2_gnn_in['b2'], 'L3_gnn_W1': _L3_gnn_in['W1'], 'L3_gnn_b1': _L3_gnn_in['b1'], 'L3_gnn_W2': _L3_gnn_in['W2'], 'L3_gnn_b2': _L3_gnn_in['b2']}

def reference(x, src, dst, edge_weight, L2_gnn_W1, L2_gnn_b1, L2_gnn_W2, L2_gnn_b2, L3_gnn_W1, L3_gnn_b1, L3_gnn_W2, L3_gnn_b2):
    import jax
    import jax.numpy as jnp

    def _L0_gnn_ref(node_features, edge_index):
        import jax, jax.numpy as jnp
        import numpy as np
        N_NODES = 100000
        src = node_features[edge_index[0]]
        dest = node_features[edge_index[1]]
        messages = src + dest
        num_nodes = node_features.shape[0]
        target = edge_index[1]
        aggregated = jax.ops.segment_sum(messages, target, num_segments=num_nodes)
        ones = jnp.ones((messages.shape[0],), dtype=messages.dtype)
        counts = jax.ops.segment_sum(ones, target, num_segments=num_nodes)
        aggregated = aggregated / jnp.clip(counts, 1.0)[:, None]
        return node_features + aggregated

    def _L1_gnn_ref(x, edge_index, edge_weights):
        import jax, jax.numpy as jnp
        import numpy as np
        N_NODES = 50000
        N_EDGES = 25000
        N_FEAT = 64
        src = edge_index[0]
        tgt = edge_index[1]
        messages = x[src] * edge_weights[:, None]
        out = jax.ops.segment_sum(messages, tgt, num_segments=x.shape[0])
        return out

    def _L2_gnn_ref(x, edge_index, W1, b1, W2, b2):
        import jax, jax.numpy as jnp
        import numpy as np
        N_NODES = 50000
        N_EDGES = 12500
        D_FEAT = 64
        D_HID = 128
        D_OUT = 64
        n = x.shape[0]
        loops = jnp.arange(n, dtype=edge_index.dtype)
        src = jnp.concatenate([edge_index[0], loops])
        dst = jnp.concatenate([edge_index[1], loops])
        edge_features = jnp.concatenate([x[src], x[dst]], axis=-1)
        h = jax.nn.relu(edge_features @ W1 + b1)
        edge_out = h @ W2 + b2
        agg = jax.ops.segment_sum(edge_out, dst, num_segments=n)
        counts = jax.ops.segment_sum(jnp.ones_like(dst, dtype=edge_out.dtype), dst, num_segments=n)
        return agg / jnp.clip(counts, 1.0)[:, None]

    def _L3_gnn_ref(x, edge_index, W1, b1, W2, b2):
        import jax, jax.numpy as jnp
        import numpy as np
        N_NODES = 100000
        N_EDGES = 25000
        F_IN = 64
        F_HID = 64

        def gcn_conv(x, src, dst, W, b, n_nodes):
            h = x @ W
            deg = jax.ops.segment_sum(jnp.ones_like(dst, dtype=h.dtype), dst, num_segments=n_nodes)
            dinv = jnp.where(deg > 0, jax.lax.rsqrt(deg), 0.0)
            norm = dinv[src] * dinv[dst]
            msgs = h[src] * norm[:, None]
            out = jax.ops.segment_sum(msgs, dst, num_segments=n_nodes)
            return out + b
        n = x.shape[0]
        loops = jnp.arange(n, dtype=edge_index.dtype)
        src = jnp.concatenate([edge_index[0], loops])
        dst = jnp.concatenate([edge_index[1], loops])
        h = jax.nn.relu(gcn_conv(x, src, dst, W1, b1, n))
        h = jax.nn.relu(gcn_conv(h, src, dst, W2, b2, n))
        return h
    edge_index = jnp.stack([src, dst])
    x = _layernorm(x + _L0_gnn_ref(x, edge_index), axis=-1)
    x = _layernorm(x + _L1_gnn_ref(x, edge_index, edge_weight), axis=-1)
    x = _layernorm(x + _L2_gnn_ref(x, edge_index, L2_gnn_W1, L2_gnn_b1, L2_gnn_W2, L2_gnn_b2), axis=-1)
    x = _layernorm(x + _L3_gnn_ref(x, edge_index, L3_gnn_W1, L3_gnn_b1, L3_gnn_W2, L3_gnn_b2), axis=-1)
    return x

_drawn_inputs = setup_inputs


def setup_inputs(seed=0):
    import zlib

    import numpy as np

    out = dict(_drawn_inputs(seed))
    spreads = {'L2_gnn_b1': (0.0, 0.1),
     'L2_gnn_b2': (0.0, 0.1),
     'L3_gnn_b1': (0.0, 0.1),
     'L3_gnn_b2': (0.0, 0.1)}
    factors = {}
    for name, (base, spread) in spreads.items():
        noise = np.random.default_rng([zlib.crc32(name.encode()), seed]).standard_normal(out[name].shape)
        drawn = base * np.exp(spread * noise) if base else spread * noise
        out[name] = jnp.asarray(drawn.astype(out[name].dtype))
    for name, factor in factors.items():
        out[name] = (out[name] * factor).astype(out[name].dtype)
    return out
```

```python
from contextlib import ExitStack

import concourse.bass as bass
import concourse.mybir as mybir
from concourse.alu_op_type import AluOpType as ALU

F32, I32, U8 = mybir.dt.float32, mybir.dt.int32, mybir.dt.uint8
ACT = mybir.ActivationFunctionType
AX = mybir.AxisListType
P = 128
D = 64
EPS = 1e-5
N = 100000
E = 25000
TB = 4
E_PAD = -(-E // (P * TB)) * P * TB
TILES = E_PAD // P
BATCHES = TILES // TB
PAD_DST = N + 96
MAP_ROWS = N + 352
FAR = 1 << 20
RW = 2 * P
RR = E_PAD // RW
G = 8
BLOCK = P * G
BLOCKS = -(-N // BLOCK)


def bc(ap, *shape):
    return ap.unsqueeze(len(ap.shape)).broadcast_to(list(shape))


def batches(eng, body):
    for b in range(3):
        body(b, b % 2, b // 2)
    with eng.Fori(0, (BATCHES - 5) // 2) as r:
        body(r * 2 + 3, 1, r + 1)
        body(r * 2 + 4, 0, r + 2)
    for b in range(BATCHES - 2, BATCHES):
        body(b, b % 2, b // 2)


def wait(eng, met, sem, value):
    if not isinstance(value, int):
        value = eng.snap(value)
        eng.wait_ge(*met)
    eng.wait_ge(sem, value)


class Links:

    def __init__(self, sem, per):
        self.sem, self.per = sem, per

    def begin(self, eng, n):
        self.eng, self.n, self.k = eng, n, 0

    def __call__(self, instruction):
        self.k += 1
        instruction.then_inc(self.sem, 1)
        self.eng.wait_ge(self.sem, self.n * self.per + self.k)

    def end(self):
        assert self.k == self.per, (self.k, self.per)


class Norm:

    def __init__(self, sb, sem, name, g, scale=1.0 / D, like=None):
        self.g, self.scale = g, scale
        self.mean = sb(f"{name}_mean", [P, g], F32)
        self.mean_d = sb(f"{name}_meand", [P, g], F32)
        self.centred = like.centred if like else sb(f"{name}_centred", [P, g, D], F32)
        self.square = like.square if like else sb(f"{name}_square", [P, g, D], F32)
        self.total = sb(f"{name}_total", [P, g], F32)
        self.root = sb(f"{name}_root", [P, g], F32)
        self.inverse = sb(f"{name}_inverse", [P, g], F32)
        self.s_centred = sem(f"{name}_s_centred")
        self.s_square = sem(f"{name}_s_square")
        self.s_total = sem(f"{name}_s_total")
        self.s_root = sem(f"{name}_s_root")

    LINKS_A, LINKS_C = 2, 1

    def dve_centre(self, nc, link, y):
        link(nc.vector.tensor_reduce(self.mean[:, :], y, AX.X, ALU.add))
        link(nc.vector.tensor_scalar(self.mean_d[:, :], self.mean[:, :], 1.0 / D, None, ALU.mult))
        nc.vector.tensor_tensor(self.centred[:, :, :], y, bc(self.mean_d[:, :], P, self.g, D),
                                ALU.subtract).then_inc(self.s_centred, 1)

    def act_square(self, nc, act, n):
        act.wait_ge(self.s_centred, n + 1)
        nc.scalar.activation(self.square[:, :, :], self.centred[:, :, :], ACT.Square).then_inc(self.s_square, 1)

    def dve_total(self, nc, dve, n):
        dve.wait_ge(self.s_square, n + 1)
        nc.vector.tensor_reduce(self.total[:, :], self.square[:, :, :], AX.X, ALU.add).then_inc(self.s_total, 1)

    def act_root(self, nc, act, n, eps):
        act.wait_ge(self.s_total, n + 1)
        nc.scalar.activation(self.root[:, :], self.total[:, :], ACT.Sqrt, bias=eps,
                             scale=self.scale).then_inc(self.s_root, 1)

    def dve_scale(self, nc, dve, n, link, out):
        dve.wait_ge(self.s_root, n + 1)
        link(nc.vector.reciprocal(self.inverse[:, :], self.root[:, :]))
        return nc.vector.tensor_tensor(out, self.centred[:, :, :], bc(self.inverse[:, :], P, self.g, D), ALU.mult)


def build(nc, x, src, dst, edge_weight, w_21, b_21, w_22, b_22, w_31, b_31, w_32, b_32, out):
    ctx = ExitStack()
    with ctx:
        def sb(name, shape, dt):
            return ctx.enter_context(nc.sbuf_tensor(name, shape, dt))

        def sem(name):
            return ctx.enter_context(nc.semaphore(name))

        slot_map = nc.dram_tensor("slot_map", [MAP_ROWS, 1], I32, kind="Internal").ap()
        dst_dram = nc.dram_tensor("dst_dram", [E_PAD], F32, kind="Internal").ap()
        table = [None] + [nc.dram_tensor(f"table{k}", [2 * E_PAD, D], F32, kind="Internal").ap() for k in (1, 2, 3, 4)]

        ident = sb("ident", [P, P], F32)
        one_row = sb("one_row", [P, P], F32)
        w_src_dst = sb("w_src_dst", [P, P], F32)
        w_self = sb("w_self", [P, P], F32)
        w_part = sb("w_part", [P, P], F32)
        w_out = sb("w_out", [P, D], F32)
        w_conv = [sb(f"w_conv{k}", [P, P], F32) for k in (0, 1)]
        hid_bias = sb("hid_bias", [P, 1], F32)
        out_bias = sb("out_bias", [P, G, D], F32)
        conv_bias_col = sb("conv_bias_col", [P, 1], F32)
        conv_bias = [sb(f"conv_bias{k}", [P, G, D], F32) for k in (0, 1)]
        eps = sb("eps", [P, 1], F32)
        eps_x1 = sb("eps_x1", [P, 1], F32)
        eps_x2 = sb("eps_x2", [P, 1], F32)

        src_r = sb("src_r", [RR, RW], I32)
        dst_r = sb("dst_r", [RR, RW], I32)
        nxt_r = sb("nxt_r", [RR, RW], I32)
        rows_f = sb("rows_f", [RR, 5, RW], F32)
        same_r = sb("same_r", [RR, RW], F32)
        cols = sb("cols", [P, 4, TILES], F32)
        src_i = sb("src_i", [P, TILES], I32)
        dst_i = sb("dst_i", [P, TILES], I32)
        scat_i = sb("scat_i", [P, TILES], I32)
        slot_i = sb("slot_i", [P, TILES], I32)
        own_i = sb("own_i", [P, TILES], I32)
        own_f = sb("own_f", [P, TILES], F32)
        look_i = sb("look_i", [P, TILES], I32)
        prev_f = sb("prev_f", [P, TILES], F32)
        key_r = sb("key_r", [RR, 2], F32)
        key_i = sb("key_i", [RR, 2], I32)
        tail_slot = sb("tail_slot", [RR, 2], I32)
        tail_key = sb("tail_key", [P, TILES], F32)
        tail = sb("tail", [P, 2, D + 2], F32)
        count = sb("count", [P, TILES], F32)
        inv_deg = sb("inv_deg", [P, TILES], F32)
        inv_root = sb("inv_root", [P, TILES], F32)
        same8 = sb("same8", [P, TILES, P], U8)
        carry8 = sb("carry8", [P, TILES, P], U8)
        dst_row = sb("dst_row", [P, 2, TB * P], F32)
        node = sb("node", [P, TILES, D], F32)
        far_map = sb("far_map", [P, MAP_ROWS // P], I32)

        st_src = sb("st_src", [P, 2, TB], I32)
        st_dst = sb("st_dst", [P, 2, TB], I32)
        st_val = sb("st_val", [P, 2, TB], I32)
        msg = sb("msg", [P, 2, TB, D + 2], F32)
        x_dst = sb("x_dst", [P, 2, TB, D], F32)
        own_row = sb("own_row", [P, 2, TB, D], F32)
        got_slot = sb("got_slot", [P, 2, TB], I32)
        slot_d = sb("slot_d", [P, 2, TB], F32)
        same_f = sb("same_f", [P, TB, P], F32)
        carry_f = sb("carry_f", [P, TB, P], F32)
        tail_f = sb("tail_f", [P, TB, P], F32)
        sums = sb("sums", [P, 2, TB, D + 2], F32)
        inv_count = sb("inv_count", [P, TB], F32)
        pair = sb("pair", [P, 2, TB, 2 * D], F32)
        keep = sb("keep", [P, TB], F32)
        feat = sb("feat", [P, TB * P], F32)
        hid = sb("hid", [P, 2, TB * P], F32)
        edge_y = sb("edge_y", [P, TB, D], F32)
        edge_z = sb("edge_z", [P, TB, D], F32)
        new_row = sb("new_row", [P, 2, TB, D], F32)
        en = [Norm(sb, sem, f"en{k}", TB) if k == 0 else None for k in range(1)][0]

        psum = [ctx.enter_context(nc.psum_tensor(f"ps{k}", [P, 512], F32)) for k in range(8)]
        DA, DB, DC, DD, EA, EB, EC, ED = psum
        sums_ps = EB[:, :].rearrange("p (j d) -> p j d", j=TB)

        s_zero = sem("s_zero"); s_load_e = sem("s_load_e"); s_load_w = sem("s_load_w"); s_prep = sem("s_prep")
        s_sel = sem("s_sel"); s_rows = sem("s_rows"); s_ct = sem("s_ct"); s_cc = sem("s_cc"); s_wself = sem("s_wself")
        s_map0 = sem("s_map0"); s_dstd = sem("s_dstd"); s_cols = sem("s_cols"); s_psel = sem("s_psel")
        s_tails = sem("s_tails"); s_tailr = sem("s_tailr"); s_pmem = sem("s_pmem")

        class Rows:

            def __init__(self, name, g, banks, hid=None):
                self.g, self.name = g, name
                self.n0 = Norm(sb, sem, f"{name}0", g, (1.0 + EPS) / D)
                self.n1 = Norm(sb, sem, f"{name}1", g, like=self.n0)
                self.x2 = sb(f"{name}_x2", [P, g, D], F32)
                self.x2t = sb(f"{name}_x2t", [P, g * D], F32)
                self.hid = hid if hid is not None else sb(f"{name}_hid", [P, 2, g * D], F32)
                self.x3 = sb(f"{name}_x3", [P, g, D], F32)
                self.h1 = sb(f"{name}_h1", [P, g * D], F32)
                self.turn, self.hid_ps, self.res = banks
                self.s_x2, self.s_turn, self.s_x2t = sem(f"{name}_s_x2"), sem(f"{name}_s_turn"), sem(f"{name}_s_x2t")
                self.s_hidp, self.s_hid, self.s_y = sem(f"{name}_s_hidp"), sem(f"{name}_s_hid"), sem(f"{name}_s_y")
                self.s_x3, self.s_turn3, self.s_x3t = sem(f"{name}_s_x3"), sem(f"{name}_s_turn3"), sem(f"{name}_s_x3t")
                self.s_h1p, self.s_h1, self.s_h2 = sem(f"{name}_s_h1p"), sem(f"{name}_s_h1"), sem(f"{name}_s_h2")

            def y(self):
                return self.res[:, 0:self.g * D].rearrange("p (g d) -> p g d", d=D)

            def pe_turn(self, pe, n, rows, ready, done):
                pe.wait_ge(ready, n + 1)
                for k in range(self.g // 2):
                    last = nc.tensor.transpose(self.turn[:, k * P:(k + 1) * P],
                                               rows[:, 2 * k:2 * k + 2, :].rearrange("p a d -> p (a d)"), ident[:, :])
                last.then_inc(done, 1)

            def pe_hidden(self, pe, n):
                pe.wait_ge(self.s_x2t, n + 1)
                for h in range(2):
                    last = nc.tensor.matmul(self.hid_ps[h], w_self[64 * h:64 * h + 64, :],
                                            self.x2t[64 * h:64 * h + 64, :], start=True, stop=True)
                last.then_inc(self.s_hidp, 1)

            def act_hidden(self, act, n):
                act.wait_ge(self.s_hidp, n + 1)
                for h in range(2):
                    last = nc.scalar.activation(self.hid[:, h, :], self.hid_ps[h], ACT.Relu, bias=hid_bias[:, :])
                last.then_inc(self.s_hid, 1)

            def pe_out(self, pe, n):
                pe.wait_ge(self.s_hid, n + 1)
                nc.tensor.matmul(self.res[:, 0:self.g * D], one_row[:, :],
                                 out_bias[:, 0:self.g, :].rearrange("p g d -> p (g d)"), start=True, stop=True)
                for k in range(self.g):
                    last = nc.tensor.matmul(self.res[:, k * D:(k + 1) * D],
                                            self.hid[:, k % 2, (k // 2) * P:(k // 2 + 1) * P], w_out[:, :],
                                            start=False, stop=True, skip_group_check=True)
                last.then_inc(self.s_y, 1)

            def act_copy(self, act, n, to, ready, done):
                act.wait_ge(ready, n + 1)
                nc.scalar.activation(to, self.turn[:, 0:self.g * D], ACT.Copy).then_inc(done, 1)

            def pe_conv1(self, pe, n):
                pe.wait_ge(self.s_x3t, n + 1)
                nc.tensor.matmul(self.hid_ps[0], w_conv[0][:, :], self.x2t[:, :], start=True,
                                 stop=True).then_inc(self.s_h1p, 1)

            def act_conv1(self, act, n):
                act.wait_ge(self.s_h1p, n + 1)
                nc.scalar.activation(self.h1[:, :], self.hid_ps[0], ACT.Relu, bias=conv_bias_col[:, :]).then_inc(self.s_h1, 1)

        dense = Rows("dense", G, (DA, [DB[:, :], DC[:, :]], DD))
        dense.n2 = Norm(sb, sem, "dense2", G, like=dense.n0)
        x_in = sb("x_in", [P, 2, G, D], F32)
        x_out = sb("x_out", [P, 2, G, D], F32)
        s_xin = [sem("s_xin0"), sem("s_xin1")]
        s_xout = sem("s_xout")
        s_stored = [sem("s_stored0"), sem("s_stored1")]
        link_d = Links(sem("s_link_d"), 3 * 3 + 2)
        s_dadd = sem("s_dadd")

        srows = Rows("srows", TB, (EA[:, 0:TB * D], [EC[:, 0:TB * D], ED[:, 0:TB * D]], EA[:, TB * D:2 * TB * D]), hid[:, :, 0:TB * D])
        src_x1 = sb("src_x1", [P, TB, D], F32)
        src_root = sb("src_root", [P, TB], F32)
        src_inv = sb("src_inv", [P, TB], F32)
        src_h1 = sb("src_h1", [P, TB, D], F32)
        s_root1 = sem("s_root1")
        s_x1s = sem("s_x1s")
        s_h1t = sem("s_h1t")
        s_h1o = sem("s_h1o")
        s_sst = [sem(f"s_sst{k}") for k in range(4)]
        link_s = Links(sem("s_link_s"), 2 * 3 + 2)

        s_stage = sem("s_stage")
        s_row = [sem("s_row0"), sem("s_row1")]
        s_row3 = [sem("s_row3_0"), sem("s_row3_1")]
        s_mask = sem("s_mask")
        s_scat = [sem("s_scat0"), sem("s_scat1")]
        s_msgin = [sem("s_msgin0"), sem("s_msgin1")]
        s_dstin = [sem("s_dstin0"), sem("s_dstin1")]
        s_slotin = [sem("s_slotin0"), sem("s_slotin1")]
        s_msg = sem("s_msg")
        s_same = sem("s_same")
        s_sum = sem("s_sum")
        s_sums = sem("s_sums")
        s_new = sem("s_new")
        s_put = [sem("s_put0"), sem("s_put1")]
        s_scattered = [sem("s_scattered0"), sem("s_scattered1")]
        s_ownin = [sem("s_ownin0"), sem("s_ownin1")]
        link_e = {1: Links(sem("s_link_e1"), 9), 2: Links(sem("s_link_e2"), 4), 3: Links(sem("s_link_e3"), 8),
                  4: Links(sem("s_link_e4"), 1), 5: Links(sem("s_link_e5"), 6)}
        s_look = sem("s_look")
        s_tailf = sem("s_tailf"); s_tailp = sem("s_tailp"); s_pair = sem("s_pair"); s_pairt = sem("s_pairt")
        s_feat = sem("s_feat"); s_hidp = sem("s_hidp"); s_hide = sem("s_hide"); s_mp = sem("s_mp")
        s_agg = [sem("s_agg4"), sem("s_agg5")]
        s_aggt = [sem("s_aggt4"), sem("s_aggt5")]
        s_aggc = [sem("s_aggc4"), sem("s_aggc5")]
        s_conv = [sem("s_conv4"), sem("s_conv5")]
        s_deg = sem("s_deg"); s_deg2 = sem("s_deg2"); s_deg3 = sem("s_deg3")

        NORM = {1: 0, 2: 1, 3: 2, 5: 3}

        def before(ph):
            return (ph - 1) * BATCHES

        def before_par(ph, par):
            return (ph - 1) * ((BATCHES + 1 - par) // 2)

        def norms(ph, n):
            return n + NORM[ph] * BATCHES

        x_blocks = x[0:(BLOCKS - 1) * BLOCK, :].rearrange("(b p g) d -> b p g d", p=P, g=G)
        out_blocks = out[0:(BLOCKS - 1) * BLOCK, :].rearrange("(b p g) d -> b p g d", p=P, g=G)

        def dense_rows(blocks, whole, b):
            if isinstance(b, int) and b == BLOCKS - 1:
                return whole[N - BLOCK:N, :].rearrange("(p g) d -> p g d", g=G)
            return blocks[b]

        def table_rows(k, b, half):
            t = table[k][half * E_PAD:(half + 1) * E_PAD, :].rearrange("(b j p) d -> b p j d", j=TB, p=P)
            return t[b]

        block = ctx.enter_context(nc.Block())

        @block.sync
        def _(sp):
            sp.wait_ge(s_zero, 1)
            full = E // RW
            rest = E - full * RW
            sp.dma_start(src_r[0:full, :], src[0:full * RW].rearrange("(r c) -> r c", c=RW)).then_inc(s_load_e, 16)
            sp.dma_start(src_r[full:full + 1, 0:rest], src[full * RW:E].rearrange("(r c) -> r c", r=1)).then_inc(s_load_e, 16)
            sp.dma_start(dst_r[0:full, :], dst[0:full * RW].rearrange("(r c) -> r c", c=RW)).then_inc(s_load_e, 16)
            sp.dma_start(dst_r[full:full + 1, 0:rest], dst[full * RW:E].rearrange("(r c) -> r c", r=1)).then_inc(s_load_e, 16)
            sp.dma_start(nxt_r[0:full, :], dst[1:full * RW + 1].rearrange("(r c) -> r c", c=RW)).then_inc(s_load_e, 16)
            sp.dma_start(nxt_r[full:full + 1, 0:rest - 1], dst[full * RW + 1:E].rearrange("(r c) -> r c", r=1)).then_inc(s_load_e, 16)
            sp.dma_start(rows_f[0:full, 4, :], edge_weight[0:full * RW].rearrange("(r c) -> r c", c=RW)).then_inc(s_load_e, 16)
            sp.dma_start(rows_f[full:full + 1, 4, 0:rest], edge_weight[full * RW:E].rearrange("(r c) -> r c", r=1)).then_inc(s_load_e, 16)
            sp.dma_start(slot_map.rearrange("(p c) a -> p (c a)", p=P), far_map[:, :]).then_inc(s_map0, 16)
            sp.wait_ge(s_rows, 1)
            sp.dma_start(dst_dram.rearrange("(r c) -> r c", c=RW), rows_f[:, 1, :]).then_inc(s_dstd, 16)
            sp.wait_ge(s_dstd, 16)

            dst_rows = dst_dram.rearrange("(b a c) -> b a c", a=1, c=TB * P)

            def dense_io(b, par, k, first=False):
                if not first:
                    if not isinstance(b, int) or b >= 2:
                        wait(sp, (s_dstd, 16), dense.n0.s_centred, b - 1)
                sp.dma_start(x_in[:, par, :, :], dense_rows(x_blocks, x, b)).then_inc(s_xin[par], 16)
                if not first:
                    wait(sp, (s_dstd, 16), s_xout, b)
                    sp.dma_start(dense_rows(out_blocks, out, b - 1), x_out[:, 1 - par, :, :]).then_inc(s_stored[1 - par], 16)

            def phase0(i, par, k):
                if not isinstance(i, int) or i >= 2:
                    wait(sp, (s_dstd, 16), s_mask, i - 1)
                sp.dma_start(dst_row[:, par, :], dst_rows[i].broadcast_to([P, TB * P])).then_inc(s_row[par], 16)
                dense_io(i, par, k, first=isinstance(i, int) and i == 0)
            batches(sp, phase0)

            def phase1(i, par, k):
                dense_io(i + BATCHES, 1 - par, None)
                wait(sp, (s_dstd, 16), s_x1s, i + 1)
                sp.dma_start(table_rows(1, i, 1), src_x1[:, :, :]).then_inc(s_sst[0], 16)
                wait(sp, (s_dstd, 16), srows.s_x2, i + 1)
                sp.dma_start(table_rows(2, i, 1), srows.x2[:, :, :]).then_inc(s_sst[1], 16)
                wait(sp, (s_dstd, 16), srows.s_x3, i + 1)
                sp.dma_start(table_rows(3, i, 1), srows.x3[:, :, :]).then_inc(s_sst[2], 16)
                wait(sp, (s_dstd, 16), s_h1o, i + 1)
                sp.dma_start(table_rows(4, i, 1), src_h1[:, :, :]).then_inc(s_sst[3], 16)
                wait(sp, (s_dstd, 16), s_new, i + 1 + before(1))
                sp.dma_start(table_rows(1, i, 0), new_row[:, par, :, :]).then_inc(s_put[par], 16)
            batches(sp, phase1)
            last = BLOCKS - 1
            sp.wait_ge(s_xout, last + 1)
            sp.wait_ge(s_stored[(last - 1) % 2], 16 * (BLOCKS // 2))
            sp.dma_start(dense_rows(out_blocks, out, last), x_out[:, last % 2, :, :]).then_inc(s_stored[last % 2], 16)

            for ph in (2, 3, 4):
                def phase(i, par, k, ph=ph):
                    if ph == 3:
                        if not isinstance(i, int) or i >= 2:
                            wait(sp, (s_dstd, 16), s_tailf, i - 1)
                        sp.dma_start(dst_row[:, par, :], dst_rows[i].broadcast_to([P, TB * P])).then_inc(s_row3[par], 16)
                    wait(sp, (s_dstd, 16), s_new, i + 1 + before(ph))
                    sp.dma_start(table_rows(ph, i, 0), new_row[:, par, :, :]).then_inc(s_put[par], 16)
                batches(sp, phase)

            def phase5(i, par, k):
                if not isinstance(i, int) or i >= 2:
                    wait(sp, (s_dstd, 16), s_agg[1], i - 1)
                if isinstance(i, int) and i == 0:
                    sp.wait_ge(s_put[0], 16 * before_par(5, 0))
                    sp.wait_ge(s_put[1], 16 * before_par(5, 1))
                sp.dma_start(own_row[:, par, :, :], table_rows(4, i, 0)).then_inc(s_ownin[par], 16)
            batches(sp, phase5)

        @block.gpsimd
        def _(pool):
            nc.gpsimd.memset(far_map[:, :], FAR)
            nc.gpsimd.memset(src_r[:, :], 0)
            nc.gpsimd.memset(dst_r[:, :], PAD_DST)
            nc.gpsimd.memset(nxt_r[:, :], PAD_DST)
            nc.gpsimd.memset(rows_f[:, :, :], 0.0)
            nc.gpsimd.memset(w_conv[0][:, :], 0.0)
            nc.gpsimd.memset(w_conv[1][:, :], 0.0)
            nc.gpsimd.memset(out_bias[:, :, :], 0.0)
            nc.gpsimd.memset(conv_bias[0][:, :, :], 0.0)
            nc.gpsimd.memset(conv_bias[1][:, :, :], 0.0)
            nc.gpsimd.memset(ident[:, :], 0.0).then_inc(s_zero, 1)
            pool.wait_ge(s_zero, 1)
            nc.gpsimd.affine_select(out=ident[:, :], in_=ident[:, :], compare_op=ALU.not_equal, fill=1.0, base=0,
                                    pattern=[[-1, P]], channel_multiplier=1).then_inc(s_psel, 1)
            for h in range(2):
                pool.dma_start(w_self[64 * h:64 * h + 64, :], w_21[0:D, :]).then_inc(s_load_w, 16)
                pool.dma_start(w_part[64 * h:64 * h + 64, :], w_21[D:2 * D, :]).then_inc(s_load_w, 16)
                pool.dma_start(w_conv[0][64 * h:64 * h + 64, 64 * h:64 * h + 64], w_31).then_inc(s_load_w, 16)
                pool.dma_start(w_conv[1][64 * h:64 * h + 64, 64 * h:64 * h + 64], w_32).then_inc(s_load_w, 16)
                pool.dma_start(conv_bias_col[64 * h:64 * h + 64, :], b_31.rearrange("(d a) -> d a", a=1)).then_inc(s_load_w, 16)
            pool.dma_start(w_src_dst[:, :], w_21).then_inc(s_load_w, 16)
            pool.dma_start(w_out[:, :], w_22).then_inc(s_load_w, 16)
            pool.dma_start(hid_bias[:, :], b_21.rearrange("(d a) -> d a", a=1)).then_inc(s_load_w, 16)
            for to, b in ((out_bias, b_22), (conv_bias[0], b_31), (conv_bias[1], b_32)):
                for g in range(G):
                    pool.dma_start(to[0:1, g, :], b.rearrange("(a d) -> a d", a=1)).then_inc(s_load_w, 16)
            nc.gpsimd.iota(slot_i[:, :], pattern=[[P, TILES]], base=0, channel_multiplier=1).then_inc(s_psel, 1)
            nc.gpsimd.iota(own_i[:, :], pattern=[[P, TILES]], base=E_PAD, channel_multiplier=1).then_inc(s_psel, 1)
            pool.wait_ge(s_cols, 1)
            nc.gpsimd.affine_select(out=prev_f[:, :], in_=prev_f[:, :], compare_op=ALU.is_ge, fill=-1.0, base=-(P - 1),
                                    pattern=[[0, TILES]], channel_multiplier=1).then_inc(s_psel, 1)
            nc.gpsimd.affine_select(out=tail_key[:, :], in_=tail_key[:, :], compare_op=ALU.is_equal, fill=-1.0, base=0,
                                    pattern=[[1, RR], [0, 2]], channel_multiplier=-1).then_inc(s_psel, 1)
            pool.wait_ge(s_psel, 5)
            pool.wait_ge(s_map0, 16)

            def stage(pieces):
                for to, frm in pieces:
                    last = nc.gpsimd.tensor_copy(to, frm)
                last.then_inc(s_stage, 1)
                pool.wait_ge(s_stage, 1)

            def cols_of(t, i):
                return t[:, bass.ts(i, TB)]

            def phase0(i, par, k):
                pool.sem_clear(s_stage)
                if not isinstance(i, int) or i >= 2:
                    wait(pool, (s_psel, 5), s_scat[par], 16 * TB * k)
                stage([(st_src[:, par, :], cols_of(scat_i, i)), (st_val[:, par, :], cols_of(slot_i, i))])
                for j in range(TB):
                    pool.indirect_dma_start(out=slot_map, out_offset=bass.IndirectOffsetOnAxis(ap=st_src[:, par, j:j + 1], axis=0),
                                            in_=st_val[:, par, j:j + 1], in_offset=None,
                                            bounds_check=MAP_ROWS - 1, oob_is_err=False).then_inc(s_scat[par], 16)
            batches(pool, phase0)
            pool.wait_ge(s_scat[0], 16 * TB * ((BATCHES + 1) // 2))
            pool.wait_ge(s_scat[1], 16 * TB * (BATCHES // 2))

            def gather(to, rows, idx, done):
                return pool.indirect_dma_start(out=to, out_offset=None, in_=rows,
                                               in_offset=bass.IndirectOffsetOnAxis(ap=idx, axis=0)).then_inc(done, 16)

            def phase1(i, par, k):
                pool.sem_clear(s_stage)
                if not isinstance(i, int) or i >= 2:
                    wait(pool, (s_psel, 5), s_new, i - 1 + before(1))
                stage([(st_src[:, par, :], cols_of(src_i, i)), (st_dst[:, par, :], cols_of(dst_i, i))])
                for j in range(TB):
                    gather(msg[:, par, j, 0:D], x, st_src[:, par, j:j + 1], s_msgin[par])
                for j in range(TB):
                    gather(x_dst[:, par, j, :], x, st_dst[:, par, j:j + 1], s_dstin[par])
                for j in range(TB):
                    gather(got_slot[:, par, j:j + 1], slot_map, st_src[:, par, j:j + 1], s_slotin[par])
            batches(pool, phase1)
            for h in range(2):
                gather(tail_slot[:, h:h + 1], slot_map, key_i[:, h:h + 1], s_tails)

            for ph in (2, 3, 4, 5):
                pool.wait_ge(s_put[0], 16 * before_par(ph, 0))
                pool.wait_ge(s_put[1], 16 * before_par(ph, 1))
                pool.wait_ge(s_sst[ph - 2], 16 * BATCHES)
                if ph == 2:
                    pool.wait_ge(s_look, BATCHES)
                if ph == 3:
                    pool.wait_ge(s_tails, 32)
                    for h in range(2):
                        pool.indirect_dma_start(out=tail[0:RR, h, 0:D], out_offset=None, in_=table[2],
                                                in_offset=bass.IndirectOffsetOnAxis(ap=tail_slot[:, h:h + 1], axis=0),
                                                bounds_check=2 * E_PAD - 1, oob_is_err=False).then_inc(s_tailr, 16)
                if ph == 5:
                    pool.wait_ge(s_stored[0], 16 * (BLOCKS // 2))
                    pool.wait_ge(s_stored[1], 16 * (BLOCKS // 2))

                def phase(i, par, k, ph=ph):
                    pool.sem_clear(s_stage)
                    to = pair[:, par, :, 0:D] if ph == 3 else msg[:, par, :, 0:D]
                    if not isinstance(i, int) or i >= 2:
                        wait(pool, (s_psel, 5), s_new, i - 1 + before(ph))
                    stage([(st_src[:, par, :], cols_of(look_i, i))])
                    for j in range(TB):
                        gather(to[:, j, :], table[ph - 1], st_src[:, par, j:j + 1], s_msgin[par])
                    if ph == 5 and not (isinstance(i, int) and i == 0):
                        scatter(i - 1, 1 - par, k if par == 1 else k - 1)

                def scatter(i, par, k):
                    pool.sem_clear(s_stage)
                    if not isinstance(i, int) or i >= 2:
                        wait(pool, (s_psel, 5), s_scattered[par], 16 * TB * k)
                    wait(pool, (s_psel, 5), s_new, i + 1 + before(5))
                    stage([(st_dst[:, par, :], cols_of(scat_i, i))])
                    for j in range(TB):
                        pool.indirect_dma_start(out=out, out_offset=bass.IndirectOffsetOnAxis(ap=st_dst[:, par, j:j + 1], axis=0),
                                                in_=new_row[:, par, j, :], in_offset=None,
                                                bounds_check=N - 1, oob_is_err=False).then_inc(s_scattered[par], 16)
                batches(pool, phase)
            scatter(BATCHES - 1, (BATCHES - 1) % 2, (BATCHES - 1) // 2)
            pool.wait_ge(s_scattered[0], 16 * TB * ((BATCHES + 1) // 2))
            pool.wait_ge(s_scattered[1], 16 * TB * (BATCHES // 2))

        @block.scalar
        def _(act):
            act.wait_ge(s_prep, 1)

            def dense_head(b):
                dense.n0.act_square(nc, act, b)
                dense.n0.act_root(nc, act, b, eps_x2[:, :])

            def rows_mid(c, n):
                c.act_copy(act, n, c.x2t[:, :], c.s_turn, c.s_x2t)
                c.act_hidden(act, n)

            def rows_low(c, n):
                c.act_copy(act, n, c.x2t[:, :], c.s_turn3, c.s_x3t)
                c.act_conv1(act, n)

            def norm(m, n, e):
                m.act_square(nc, act, n)
                m.act_root(nc, act, n, e)

            def dense_block(b):
                norm(dense.n0, b, eps_x2[:, :])
                rows_mid(dense, b)
                norm(dense.n1, b, eps[:, :])
                rows_low(dense, b)
                norm(dense.n2, b, eps[:, :])

            act.wait_ge(s_load_w, 16 * 37)

            def expand(ph, i):
                if ph > 1 or not isinstance(i, int) or i >= 1:
                    act.wait_ge(s_sum, TB * i + TB * before(ph))
                nc.scalar.activation(same_f[:, :, :], same8[:, bass.ts(i, TB), :], ACT.Copy)
                nc.scalar.activation(carry_f[:, :, :], carry8[:, bass.ts(i, TB), :], ACT.Copy).then_inc(s_same, 1)

            def take_sums(ph, i, par):
                for j in range(TB):
                    act.wait_ge(s_sum, TB * i + j + 1 + TB * before(ph))
                    nc.scalar.activation(sums[:, par, j, :], sums_ps[:, j, 0:D + 2], ACT.Copy).then_inc(s_sums, 1)

            def phase0(i, par, k):
                dense_block(i)
            batches(act, phase0)

            act.wait_ge(s_mask, BATCHES)

            def phase1(i, par, k):
                b = i + BATCHES
                expand(1, i)
                norm(dense.n0, b, eps_x2[:, :])
                srows.n0.act_square(nc, act, i)
                srows.n0.act_root(nc, act, i, eps_x2[:, :])
                nc.scalar.activation(src_root[:, :], srows.n0.total[:, :], ACT.Sqrt, bias=eps_x1[:, :],
                                     scale=1.0 / D).then_inc(s_root1, 1)
                rows_mid(dense, b)
                take_sums(1, i, par)
                rows_mid(srows, i)
                norm(dense.n1, b, eps[:, :])
                norm(srows.n1, i, eps[:, :])
                norm(en, norms(1, i), eps[:, :])
                rows_low(dense, b)
                rows_low(srows, i)
                act.wait_ge(s_h1t, i + 1)
                if not isinstance(i, int) or i >= 1:
                    act.wait_ge(s_sst[3], 16 * i)
                nc.scalar.activation(src_h1[:, :, :], EA[:, 0:TB * D].rearrange("p (j d) -> p j d", d=D), ACT.Copy).then_inc(s_h1o, 1)
                norm(dense.n2, b, eps[:, :])
            batches(act, phase1)

            def phase2(i, par, k):
                expand(2, i)
                take_sums(2, i, par)
                norm(en, norms(2, i), eps[:, :])
            batches(act, phase2)

            act.wait_ge(s_deg, 1)
            nc.scalar.activation(inv_root[:, :], inv_deg[:, :], ACT.Sqrt).then_inc(s_deg2, 1)

            def phase3(i, par, k):
                expand(3, i)
                act.wait_ge(s_pairt, i + 1)
                nc.scalar.activation(feat[:, :], EB[:, :], ACT.Copy).then_inc(s_feat, 1)
                act.wait_ge(s_hidp, i + 1)
                nc.scalar.activation(hid[:, 0, :], EC[:, :], ACT.Relu, bias=hid_bias[:, :])
                nc.scalar.activation(hid[:, 1, :], ED[:, :], ACT.Relu, bias=hid_bias[:, :]).then_inc(s_hide, 1)
                act.wait_ge(s_mp, i + 1)
                nc.scalar.activation(msg[:, par, :, 0:D], EA[:, 0:TB * D].rearrange("p (j d) -> p j d", d=D), ACT.Copy).then_inc(s_msg, 1)
                take_sums(3, i, par)
                norm(en, norms(3, i), eps[:, :])
            batches(act, phase3)

            for ph in (4, 5):
                def phase(i, par, k, ph=ph):
                    expand(ph, i)
                    take_sums(ph, i, par)
                    act.wait_ge(s_aggt[ph - 4], i + 1)
                    nc.scalar.activation(feat[:, 0:TB * D], EA[:, 0:TB * D], ACT.Copy).then_inc(s_aggc[ph - 4], 1)
                    if ph == 5:
                        norm(en, norms(5, i), eps[:, :])
                batches(act, phase)

        @block.tensor
        def _(pe):
            pe.wait_ge(s_psel, 1)
            pe.wait_ge(s_rows, 1)
            for q, r in enumerate((1, 0, 3, 4)):
                for h in range(2):
                    last = nc.tensor.transpose(psum[q][:, h * P:h * P + RR], rows_f[:, r, h * P:(h + 1) * P], ident[0:RR, 0:RR])
            last.then_inc(s_ct, 1)
            pe.wait_ge(s_cc, 1)
            pe.wait_ge(s_wself, 1)

            def rows_mid(c, n):
                c.pe_turn(pe, n, c.x2, c.s_x2, c.s_turn)
                c.pe_hidden(pe, n)
                c.pe_out(pe, n)

            def rows_low(c, n):
                c.pe_turn(pe, n, c.x3, c.s_x3, c.s_turn3)
                c.pe_conv1(pe, n)

            def dense_conv2(n):
                pe.wait_ge(dense.s_h1, n + 1)
                nc.tensor.matmul(DD[:, :], one_row[:, :], conv_bias[1][:, :, :].rearrange("p g d -> p (g d)"), start=True, stop=True)
                for q in range(G // 2):
                    last = nc.tensor.matmul(DD[:, q * P:(q + 1) * P], dense.h1[:, q * P:(q + 1) * P], w_conv[1][:, :],
                                            start=False, stop=True, skip_group_check=True)
                last.then_inc(dense.s_h2, 1)

            def sum_by_target(ph, i, par, width, message_ready):
                pe.wait_ge(s_same, i + 1 + before(ph))
                message_ready()
                if ph > 1 or not isinstance(i, int) or i >= 1:
                    pe.wait_ge(s_sums, TB * i + TB * before(ph))
                for j in range(TB):
                    nc.tensor.matmul(sums_ps[:, j, 0:width], same_f[:, j, :], msg[:, par, j, 0:width], start=j == 0, stop=True,
                                     skip_group_check=True)
                for j in range(TB):
                    carried = sums[:, par, j - 1, 0:width] if j else sums[:, 1 - par, TB - 1, 0:width]
                    if j:
                        pe.wait_ge(s_sums, TB * i + j + TB * before(ph))
                    nc.tensor.matmul(sums_ps[:, j, 0:width], carry_f[:, j, :], carried, start=False, stop=True,
                                     skip_group_check=True).then_inc(s_sum, 1)

            def phase0(i, par, k):
                rows_mid(dense, i)
                rows_low(dense, i)
                dense_conv2(i)
            batches(pe, phase0)

            def phase1(i, par, k):
                b = i + BATCHES
                rows_mid(dense, b)
                sum_by_target(1, i, par, D + 2, lambda: pe.wait_ge(s_msgin[par], 16 * TB * (k + 1 + before_par(1, par))))
                rows_mid(srows, i)
                rows_low(dense, b)
                rows_low(srows, i)
                pe.wait_ge(srows.s_h1, i + 1)
                for q in range(TB // 2):
                    last = nc.tensor.transpose(EA[:, q * P:(q + 1) * P], srows.h1[:, q * P:(q + 1) * P], ident[:, :])
                last.then_inc(s_h1t, 1)
                dense_conv2(b)
            batches(pe, phase1)

            def phase2(i, par, k):
                sum_by_target(2, i, par, D + 2, lambda: pe.wait_ge(s_msg, i + 1 + 0))
            batches(pe, phase2)

            pe.wait_ge(s_tailr, 32)

            def phase3(i, par, k):
                pe.wait_ge(s_tailf, i + 1)
                for j in range(TB):
                    last = nc.tensor.matmul(EA[:, j * P:j * P + D + 2], tail_f[:, j, :], tail[:, j % 2, :], start=True, stop=True)
                last.then_inc(s_tailp, 1)
                pe.wait_ge(s_pair, i + 1)
                for j in range(TB):
                    last = nc.tensor.transpose(EB[:, j * P:(j + 1) * P], pair[:, par, j, :], ident[:, :])
                last.then_inc(s_pairt, 1)
                pe.wait_ge(s_feat, i + 1)
                nc.tensor.matmul(EC[:, :], w_src_dst[:, :], feat[:, :], start=True, stop=True)
                nc.tensor.matmul(ED[:, :], w_self[D:2 * D, :], feat[D:2 * D, :], start=True, stop=True).then_inc(s_hidp, 1)
                pe.wait_ge(s_hide, i + 1)
                nc.tensor.matmul(EA[:, :], one_row[:, :], out_bias[:, :, :].rearrange("p g d -> p (g d)"), start=True, stop=True)
                for h in range(2):
                    for j in range(TB):
                        last = nc.tensor.matmul(EA[:, (h * TB + j) * D:(h * TB + j + 1) * D], hid[:, h, j * P:(j + 1) * P], w_out[:, :],
                                                start=False, stop=True, skip_group_check=True)
                last.then_inc(s_mp, 1)
                sum_by_target(3, i, par, D + 2, lambda: pe.wait_ge(s_msg, i + 1 + BATCHES))
            batches(pe, phase3)

            for ph in (4, 5):
                def phase(i, par, k, ph=ph):
                    sum_by_target(ph, i, par, D + 2, lambda: pe.wait_ge(s_msgin[par], 16 * TB * (k + 1 + before_par(ph, par))))
                    pe.wait_ge(s_agg[ph - 4], i + 1)
                    for q in range(TB // 2):
                        last = nc.tensor.transpose(EA[:, q * P:(q + 1) * P],
                                                   edge_y[:, 2 * q:2 * q + 2, :].rearrange("p a d -> p (a d)"), ident[:, :])
                    last.then_inc(s_aggt[ph - 4], 1)
                    pe.wait_ge(s_aggc[ph - 4], i + 1)
                    nc.tensor.matmul(EC[:, 0:TB * D], one_row[:, :], conv_bias[ph - 4][:, 0:TB, :].rearrange("p g d -> p (g d)"),
                                     start=True, stop=True)
                    for q in range(TB // 2):
                        last = nc.tensor.matmul(EC[:, q * P:(q + 1) * P], feat[:, q * P:(q + 1) * P], w_conv[ph - 4][:, :],
                                                start=False, stop=True, skip_group_check=True)
                    last.then_inc(s_conv[ph - 4], 1)
                batches(pe, phase)

        @block.vector
        def _(dve):
            nc.vector.memset(eps[:, :], EPS)
            nc.vector.memset(eps_x1[:, :], EPS / 4)
            nc.vector.memset(eps_x2[:, :], EPS * EPS / 4)
            nc.vector.memset(msg[:, :, :, :], 1.0)
            nc.vector.memset(sums[:, :, :, :], 0.0)
            nc.vector.memset(tail[:, :, 0:D], 0.0)
            nc.vector.memset(tail[:, :, D:D + 2], 1.0)
            nc.vector.memset(tail_key[:, :], -1.0)
            nc.vector.memset(one_row[:, :], 0.0).then_inc(s_pmem, 1)
            dve.wait_ge(s_pmem, 1)
            nc.vector.memset(prev_f[:, 0:1], -1.0)
            nc.vector.memset(one_row[0:1, :], 1.0).then_inc(s_prep, 1)
            dve.wait_ge(s_load_e, 16 * 8)
            link = Links(sem("s_link_p"), 19)
            link.begin(dve, 0)
            nc.vector.tensor_copy(rows_f[:, 0, :], src_r[:, :])
            nc.vector.tensor_copy(rows_f[:, 1, :], dst_r[:, :])
            link(nc.vector.tensor_copy(rows_f[:, 2, :], nxt_r[:, :]))
            link(nc.vector.tensor_tensor(same_r[:, :], rows_f[:, 1, :], rows_f[:, 2, :], ALU.is_equal))
            nc.vector.scalar_tensor_tensor(rows_f[:, 3, :], same_r[:, :], float(FAR), rows_f[:, 1, :], ALU.mult,
                                           ALU.add).then_inc(s_rows, 1)
            ends = rows_f[:, 1, :].rearrange("r (h c) -> r h c", h=2)[:, :, P - 1]
            goes = same_r[:, :].rearrange("r (h c) -> r h c", h=2)[:, :, P - 1]
            link(nc.vector.scalar_tensor_tensor(key_r[:, :], ends, 1.0, goes, ALU.add, ALU.mult))
            link(nc.vector.tensor_scalar(key_r[:, :], key_r[:, :], -1.0, None, ALU.add))
            nc.vector.tensor_copy(key_i[:, :], ends)
            nc.vector.tensor_copy(tail_key[0:RR, :].rearrange("k (r h) -> k r h", h=2),
                                  key_r[:, :].unsqueeze(1).broadcast_to([RR, RR, 2]))
            dve.wait_ge(s_ct, 1)
            for q in range(4):
                last = nc.vector.tensor_copy(cols[:, q, :].rearrange("p (r h) -> p h r", h=2),
                                             psum[q][:, 0:2 * P].rearrange("p (h r) -> p h r", h=2)[:, :, 0:RR])
            link(last)
            nc.vector.tensor_copy(src_i[:, :], cols[:, 1, :])
            nc.vector.tensor_scalar(dst_i[:, :], cols[:, 0, :], float(N - 1), None, ALU.min)
            nc.vector.tensor_copy(scat_i[:, :], cols[:, 2, :])
            nc.vector.tensor_copy(prev_f[:, 1:TILES], cols[:, 0, 0:TILES - 1]).then_inc(s_cc, 1)
            dve.wait_ge(s_cc, 1)
            nc.vector.tensor_copy(key_r[:, :], key_r[:, :]).then_inc(s_cols, 1)
            dve.wait_ge(s_psel, 5)
            nc.vector.tensor_copy(own_f[:, :], own_i[:, :])
            dve.wait_ge(s_load_w, 16 * 37)
            nc.vector.tensor_tensor(w_self[:, :], w_self[:, :], w_part[:, :], ALU.add).then_inc(s_wself, 1)

            def dense_1(b, par, k):
                dve.wait_ge(s_xin[par], 16 * (k + 1))
                dense.n0.dve_centre(nc, link_d, x_in[:, par, :, :])

            def dense_2(b):
                dense.n0.dve_total(nc, dve, b)

            def dense_3(b):
                dense.n0.dve_scale(nc, dve, b, link_d, dense.x2[:, :, :]).then_inc(dense.s_x2, 1)

            def dense_4(b):
                dve.wait_ge(dense.s_y, b + 1)
                link_d(nc.vector.tensor_tensor(dense.x3[:, :, :], dense.y(), dense.x2[:, :, :], ALU.add))
                dense.n1.dve_centre(nc, link_d, dense.x3[:, :, :])

            def dense_5(b):
                dense.n1.dve_total(nc, dve, b)

            def dense_6(b):
                dense.n1.dve_scale(nc, dve, b, link_d, dense.x3[:, :, :]).then_inc(dense.s_x3, 1)

            def dense_7(b):
                dve.wait_ge(dense.s_h2, b + 1)
                link_d(nc.vector.scalar_tensor_tensor(dense.x2[:, :, :], dense.y(), 0.0, dense.x3[:, :, :], ALU.max, ALU.add))
                dense.n2.dve_centre(nc, link_d, dense.x2[:, :, :])

            def dense_8(b):
                dense.n2.dve_total(nc, dve, b)

            def dense_9(b, par, k):
                if not isinstance(b, int) or b >= 2:
                    dve.wait_ge(s_stored[par], 16 * k)
                dense.n2.dve_scale(nc, dve, b, link_d, x_out[:, par, :, :]).then_inc(s_xout, 1)

            def phase0(i, par, k):
                link_d.begin(dve, i)
                dense_1(i, par, k)
                dve.wait_ge(s_row[par], 16 * (k + 1))
                for j in range(TB):
                    row = dst_row[:, par, j * P:(j + 1) * P]
                    t = i * TB + j
                    for to, key in ((same8, cols[:, 0, bass.ds(t, 1)]), (carry8, prev_f[:, bass.ds(t, 1)])):
                        last = nc.vector.tensor_scalar(to[:, bass.ds(t, 1), :].rearrange("p a e -> p (a e)"), row, key, None, ALU.is_equal)
                last.then_inc(s_mask, 1)
                dense_2(i)
                dense_3(i)
                dense_4(i); dense_5(i); dense_6(i); dense_7(i); dense_8(i); dense_9(i, par, k)
                link_d.end()
            batches(dve, phase0)

            def edge_norm_1(ph, y):
                en.dve_centre(nc, link_e[ph], y)

            def edge_norm_2(ph, i):
                en.dve_total(nc, dve, norms(ph, i))

            def phase1(i, par, k):
                b = i + BATCHES
                link_d.begin(dve, b)
                link_s.begin(dve, i)
                le = link_e[1]
                le.begin(dve, i)
                kd = k + BATCHES // 2 + par
                dense_1(b, 1 - par, kd)
                dve.wait_ge(s_msgin[par], 16 * TB * (k + 1 + before_par(1, par)))
                srows.n0.dve_centre(nc, link_s, msg[:, par, :, 0:D])
                dense_2(b)
                srows.n0.dve_total(nc, dve, i)
                dense_3(b)
                if not isinstance(i, int) or i >= 1:
                    dve.wait_ge(s_sst[1], 16 * i)
                    dve.wait_ge(s_sst[0], 16 * i)
                srows.n0.dve_scale(nc, dve, i, link_s, srows.x2[:, :, :]).then_inc(srows.s_x2, 1)
                dve.wait_ge(s_root1, i + 1)
                link_s(nc.vector.reciprocal(src_inv[:, :], src_root[:, :]))
                nc.vector.tensor_tensor(src_x1[:, :, :], srows.n0.centred[:, :, :], bc(src_inv[:, :], P, TB, D), ALU.mult).then_inc(s_x1s, 1)
                dve.wait_ge(s_slotin[par], 16 * TB * (k + 1))
                own = own_f[:, bass.ts(i, TB)]
                le(nc.vector.tensor_tensor(slot_d[:, 0, :], got_slot[:, par, :], own, ALU.subtract))
                le(nc.vector.scalar_tensor_tensor(slot_d[:, 1, :], got_slot[:, par, :], float(FAR), slot_d[:, 0, :], ALU.is_lt, ALU.mult))
                nc.vector.tensor_tensor(look_i[:, bass.ts(i, TB)], slot_d[:, 1, :], own, ALU.add).then_inc(s_look, 1)
                dense_4(b)
                dve.wait_ge(s_dstin[par], 16 * TB * (k + 1))
                wait(dve, (s_wself, 1), s_sums, TB * (i + 1 + before(1)))
                nc.vector.tensor_copy(count[:, bass.ts(i, TB)], sums[:, par, :, D])
                le(nc.vector.reciprocal(inv_count[:, :], sums[:, par, :, D]))
                le(nc.vector.tensor_tensor(edge_z[:, :, :], sums[:, par, :, 0:D], bc(inv_count[:, :], P, TB, D), ALU.mult))
                le(nc.vector.scalar_tensor_tensor(edge_y[:, :, :], x_dst[:, par, :, :], 3.0, edge_z[:, :, :], ALU.mult, ALU.add))
                edge_norm_1(1, edge_y[:, :, :])
                dve.wait_ge(srows.s_y, i + 1)
                if not isinstance(i, int) or i >= 1:
                    dve.wait_ge(s_sst[2], 16 * i)
                link_s(nc.vector.tensor_tensor(srows.x3[:, :, :], srows.y(), srows.x2[:, :, :], ALU.add))
                srows.n1.dve_centre(nc, link_s, srows.x3[:, :, :])
                dense_5(b)
                srows.n1.dve_total(nc, dve, i)
                edge_norm_2(1, i)
                dense_6(b)
                srows.n1.dve_scale(nc, dve, i, link_s, srows.x3[:, :, :]).then_inc(srows.s_x3, 1)
                if not isinstance(i, int) or i >= 2:
                    dve.wait_ge(s_put[par], 16 * (k + before_par(1, par)))
                le(en.dve_scale(nc, dve, norms(1, i), le, new_row[:, par, :, :]))
                nc.vector.tensor_copy(node[:, bass.ts(i, TB), :], new_row[:, par, :, :]).then_inc(s_new, 1)
                dense_7(b); dense_8(b)
                dense_9(b, 1 - par, kd)
                link_d.end(); link_s.end(); le.end()
            batches(dve, phase1)

            def phase2(i, par, k):
                le = link_e[2]
                le.begin(dve, i)
                dve.wait_ge(s_msgin[par], 16 * TB * (k + 1 + before_par(2, par)))
                m = msg[:, par, :, 0:D]
                nc.vector.tensor_tensor(m, m, bc(cols[:, 3, bass.ts(i, TB)], P, TB, D), ALU.mult).then_inc(s_msg, 1)
                dve.wait_ge(s_sums, TB * (i + 1 + before(2)))
                le(nc.vector.tensor_tensor(edge_y[:, :, :], sums[:, par, :, 0:D], node[:, bass.ts(i, TB), :], ALU.add))
                edge_norm_1(2, edge_y[:, :, :])
                edge_norm_2(2, i)
                if not isinstance(i, int) or i >= 2:
                    dve.wait_ge(s_put[par], 16 * (k + before_par(2, par)))
                en.dve_scale(nc, dve, norms(2, i), le, new_row[:, par, :, :]).then_inc(s_new, 1)
                wait(dve, (s_wself, 1), s_new, i + 1 + before(2))
                nc.vector.tensor_copy(node[:, bass.ts(i, TB), :], new_row[:, par, :, :])
                le.end()
            batches(dve, phase2)

            lp = Links(sem("s_link_q"), 1)
            lp.begin(dve, 0)
            lp(nc.vector.tensor_scalar(inv_deg[:, :], count[:, :], 1.0, None, ALU.add))
            nc.vector.reciprocal(inv_deg[:, :], inv_deg[:, :]).then_inc(s_deg, 1)
            dve.wait_ge(s_deg2, 1)

            def phase3(i, par, k):
                le = link_e[3]
                le.begin(dve, i)
                own = node[:, bass.ts(i, TB), :]
                dve.wait_ge(s_row3[par], 16 * (k + 1))
                for j in range(TB):
                    last = nc.vector.tensor_scalar(tail_f[:, j, :], dst_row[:, par, j * P:(j + 1) * P],
                                                   tail_key[:, bass.ds(i * TB + j, 1)], None, ALU.is_equal)
                last.then_inc(s_tailf, 1)
                dve.wait_ge(s_tailp, i + 1)
                tails = EA[:, :].rearrange("p (j d) -> p j d", j=TB)
                le(nc.vector.tensor_scalar(keep[:, :], tails[:, :, D], -1.0, 1.0, ALU.mult, ALU.add))
                le(nc.vector.tensor_tensor(edge_z[:, :, :], own, bc(keep[:, :], P, TB, D), ALU.mult))
                nc.vector.tensor_tensor(pair[:, par, :, D:2 * D], edge_z[:, :, :], tails[:, :, 0:D], ALU.add)
                dve.wait_ge(s_msgin[par], 16 * TB * (k + 1 + before_par(3, par)))
                nc.vector.tensor_copy(keep[:, :], inv_deg[:, bass.ts(i, TB)]).then_inc(s_pair, 1)
                dve.wait_ge(s_sums, TB * (i + 1 + before(3)))
                selfs = EA[:, TB * D:2 * TB * D].rearrange("p (j d) -> p j d", d=D)
                le(nc.vector.tensor_tensor(edge_z[:, :, :], sums[:, par, :, 0:D], selfs, ALU.add))
                le(nc.vector.tensor_tensor(edge_z[:, :, :], edge_z[:, :, :], bc(keep[:, :], P, TB, D), ALU.mult))
                le(nc.vector.tensor_tensor(edge_y[:, :, :], edge_z[:, :, :], own, ALU.add))
                edge_norm_1(3, edge_y[:, :, :])
                edge_norm_2(3, i)
                if not isinstance(i, int) or i >= 2:
                    dve.wait_ge(s_put[par], 16 * (k + before_par(3, par)))
                en.dve_scale(nc, dve, norms(3, i), le, own).then_inc(s_deg3, 1)
                dve.wait_ge(s_deg3, i + 1)
                nc.vector.tensor_tensor(new_row[:, par, :, :], own, bc(inv_root[:, bass.ts(i, TB)], P, TB, D), ALU.mult).then_inc(s_new, 1)
                le.end()
            batches(dve, phase3)

            def phase4(i, par, k):
                le = link_e[4]
                le.begin(dve, i)
                scale = bc(inv_root[:, bass.ts(i, TB)], P, TB, D)
                dve.wait_ge(s_sums, TB * (i + 1 + before(4)))
                le(nc.vector.tensor_tensor(edge_z[:, :, :], node[:, bass.ts(i, TB), :], scale, ALU.mult))
                nc.vector.tensor_tensor(edge_z[:, :, :], edge_z[:, :, :], sums[:, par, :, 0:D], ALU.add).then_inc(s_dadd, 1)
                dve.wait_ge(s_dadd, i + 1)
                nc.vector.tensor_tensor(edge_y[:, :, :], edge_z[:, :, :], scale, ALU.mult).then_inc(s_agg[0], 1)
                dve.wait_ge(s_conv[0], i + 1)
                if not isinstance(i, int) or i >= 2:
                    dve.wait_ge(s_put[par], 16 * (k + before_par(4, par)))
                nc.vector.scalar_tensor_tensor(new_row[:, par, :, :], EC[:, 0:TB * D].rearrange("p (j d) -> p j d", d=D), 0.0,
                                               scale, ALU.max, ALU.mult).then_inc(s_new, 1)
                le.end()
            batches(dve, phase4)

            def phase5(i, par, k):
                le = link_e[5]
                le.begin(dve, i)
                scale = bc(inv_root[:, bass.ts(i, TB)], P, TB, D)
                dve.wait_ge(s_sums, TB * (i + 1 + before(5)))
                dve.wait_ge(s_ownin[par], 16 * (k + 1))
                le(nc.vector.tensor_tensor(edge_z[:, :, :], own_row[:, par, :, :], sums[:, par, :, 0:D], ALU.add))
                nc.vector.tensor_tensor(edge_y[:, :, :], edge_z[:, :, :], scale, ALU.mult).then_inc(s_agg[1], 1)
                dve.wait_ge(s_conv[1], i + 1)
                le(nc.vector.scalar_tensor_tensor(edge_z[:, :, :], EC[:, 0:TB * D].rearrange("p (j d) -> p j d", d=D), 0.0,
                                                  node[:, bass.ts(i, TB), :], ALU.max, ALU.add))
                edge_norm_1(5, edge_z[:, :, :])
                edge_norm_2(5, i)
                if not isinstance(i, int) or i >= 2:
                    dve.wait_ge(s_scattered[par], 16 * TB * k)
                le(en.dve_scale(nc, dve, norms(5, i), le, new_row[:, par, :, :]))
                nc.vector.tensor_copy(keep[:, :], keep[:, :]).then_inc(s_new, 1)
                le.end()
            batches(dve, phase5)


_INS = ["x", "src", "dst", "edge_weight", "L2_gnn_W1", "L2_gnn_b1", "L2_gnn_W2", "L2_gnn_b2",
        "L3_gnn_W1", "L3_gnn_b1", "L3_gnn_W2", "L3_gnn_b2"]


def kernel(**inputs):
    import numpy as np
    import concourse.bacc as bacc
    from concourse.bass_utils import run_bass_kernel_spmd

    nc = bacc.Bacc("TRN2", target_bir_lowering=False, num_devices=1)
    arrays, args = {}, []
    for name in _INS:
        a = np.ascontiguousarray(inputs[name])
        arrays[f"in_{name}"] = a
        args.append(nc.dram_tensor(f"in_{name}", a.shape, mybir.dt.from_np(a.dtype), kind="ExternalInput").ap())
    args.append(nc.dram_tensor("out_rows", (N, D), F32, kind="ExternalOutput").ap())
    build(nc, *args)
    got = run_bass_kernel_spmd(nc, [arrays], core_ids=[0])
    return got.results[0]["out_rows"]
```

```python
from contextlib import ExitStack

import concourse.bass as bass
import concourse.mybir as mybir
from concourse.alu_op_type import AluOpType as ALU

F32, I32, U8 = mybir.dt.float32, mybir.dt.int32, mybir.dt.uint8
ACT = mybir.ActivationFunctionType
AX = mybir.AxisListType
P = 128
D = 64
EPS = 1e-5
N = 100000
E = 25000
TB = 4
E_PAD = -(-E // (P * TB)) * P * TB
TILES = E_PAD // P
BATCHES = TILES // TB
HEAD = 5
PAD_DST = N + 96
MAP_ROWS = N + 352
FAR = 1 << 20
RW = 2 * P
RR = E_PAD // RW
G = 8
BLOCK = P * G
BLOCKS = -(-N // BLOCK)


def bc(ap, *shape):
    return ap.unsqueeze(len(ap.shape)).broadcast_to(list(shape))


def batches(eng, body):
    for b in range(HEAD):
        body(b, b % 2, b // 2)
    with eng.Fori(0, (BATCHES - HEAD - 2) // 2) as r:
        body(r * 2 + HEAD, 1, r + HEAD // 2)
        body(r * 2 + HEAD + 1, 0, r + HEAD // 2 + 1)
    for b in range(BATCHES - 2, BATCHES):
        body(b, b % 2, b // 2)


def at_least(i, least):
    return not isinstance(i, int) or i >= least


def back(par, k, by):
    return (par, k - 1) if by == 2 else (1 - par, k - 1 + par)


def wait(eng, met, sem, value):
    if not isinstance(value, int):
        value = eng.snap(value)
        eng.wait_ge(*met)
    eng.wait_ge(sem, value)


class Links:

    def __init__(self, sem, per):
        self.sem, self.per = sem, per

    def begin(self, eng, n):
        self.eng, self.n, self.k = eng, n, 0

    def __call__(self, instruction):
        self.k += 1
        instruction.then_inc(self.sem, 1)
        self.eng.wait_ge(self.sem, self.n * self.per + self.k)

    def end(self):
        assert self.k == self.per, (self.k, self.per)


class Norm:

    LINKS_CENTRE, LINKS_SCALE = 2, 1

    def __init__(self, sb, sem, name, g, scale=1.0 / D, centred=None, square=None):
        self.g, self.scale = g, scale
        self.sum = sb(f"{name}_sum", [P, g], F32)
        self.mean = sb(f"{name}_mean", [P, g], F32)
        self.centred = centred if centred is not None else sb(f"{name}_centred", [P, g, D], F32)[:, :, :]
        self.square = square if square is not None else sb(f"{name}_square", [P, g, D], F32)
        self.total = sb(f"{name}_total", [P, g], F32)
        self.root = sb(f"{name}_root", [P, g], F32)
        self.inverse = sb(f"{name}_inverse", [P, g], F32)
        self.s_centred = None if centred is not None else sem(f"{name}_s_centred")
        self.s_square = sem(f"{name}_s_square")
        self.s_total = sem(f"{name}_s_total")
        self.s_root = sem(f"{name}_s_root")

    def dve_centre(self, nc, link, y):
        link(nc.vector.tensor_reduce(self.sum[:, :], y, AX.X, ALU.add))
        link(nc.vector.tensor_scalar(self.mean[:, :], self.sum[:, :], 1.0 / D, None, ALU.mult))
        nc.vector.tensor_tensor(self.centred, y, bc(self.mean[:, :], P, self.g, D),
                                ALU.subtract).then_inc(self.s_centred, 1)

    def act_square(self, nc, act, n, ready=None):
        act.wait_ge(self.s_centred if ready is None else ready, n + 1)
        nc.scalar.activation(self.square[:, :, :], self.centred, ACT.Square).then_inc(self.s_square, 1)

    def dve_total(self, nc, dve, n):
        dve.wait_ge(self.s_square, n + 1)
        nc.vector.tensor_reduce(self.total[:, :], self.square[:, :, :], AX.X, ALU.add).then_inc(self.s_total, 1)

    def act_root(self, nc, act, n, eps):
        act.wait_ge(self.s_total, n + 1)
        nc.scalar.activation(self.root[:, :], self.total[:, :], ACT.Sqrt, bias=eps,
                             scale=self.scale).then_inc(self.s_root, 1)

    def dve_scale(self, nc, dve, n, link, out):
        dve.wait_ge(self.s_root, n + 1)
        link(nc.vector.reciprocal(self.inverse[:, :], self.root[:, :]))
        return nc.vector.tensor_tensor(out, self.centred, bc(self.inverse[:, :], P, self.g, D), ALU.mult)


def build(nc, x, src, dst, edge_weight, w_21, b_21, w_22, b_22, w_31, b_31, w_32, b_32, out):
    ctx = ExitStack()
    with ctx:
        def sb(name, shape, dt):
            return ctx.enter_context(nc.sbuf_tensor(name, shape, dt))

        def sem(name):
            return ctx.enter_context(nc.semaphore(name))

        slot_map = nc.dram_tensor("slot_map", [MAP_ROWS, 1], I32, kind="Internal").ap()
        dst_dram = nc.dram_tensor("dst_dram", [E_PAD], F32, kind="Internal").ap()
        table = [None] + [nc.dram_tensor(f"table{k}", [2 * E_PAD, D], F32, kind="Internal").ap() for k in (1, 2, 3, 4)]

        ident = sb("ident", [P, P], F32)
        one_row = sb("one_row", [P, P], F32)
        w_src_dst = sb("w_src_dst", [P, P], F32)
        w_self = sb("w_self", [P, P], F32)
        w_part = sb("w_part", [P, P], F32)
        w_out = sb("w_out", [P, D], F32)
        w_out_c = sb("w_out_c", [P, D], F32)
        w_mean = sb("w_mean", [P, 2], F32)
        centring = sb("centring", [P, P], F32)
        out_bias_c = sb("out_bias_c", [P, G, D], F32)
        bias_mean = sb("bias_mean", [P, 2, G], F32)
        w_conv = [sb(f"w_conv{k}", [P, P], F32) for k in (0, 1)]
        hid_bias = sb("hid_bias", [P, 1], F32)
        out_bias = sb("out_bias", [P, G, D], F32)
        conv_bias_col = sb("conv_bias_col", [P, 1], F32)
        conv_bias = [sb(f"conv_bias{k}", [P, G, D], F32) for k in (0, 1)]
        eps = sb("eps", [P, 1], F32)
        eps_x1 = sb("eps_x1", [P, 1], F32)
        eps_x2 = sb("eps_x2", [P, 1], F32)

        src_r = sb("src_r", [RR, RW], I32)
        dst_r = sb("dst_r", [RR, RW], I32)
        nxt_r = sb("nxt_r", [RR, RW], I32)
        weight_r = sb("weight_r", [RR, RW], F32)
        same_r = sb("same_r", [RR, RW], F32)
        cols = sb("cols", [P, 4, TILES], F32)
        src_i = sb("src_i", [P, TILES], I32)
        dst_i = sb("dst_i", [P, TILES], I32)
        scat_i = sb("scat_i", [P, TILES], I32)
        slot_i = sb("slot_i", [P, TILES], I32)
        own_i = sb("own_i", [P, TILES], I32)
        own_f = sb("own_f", [P, TILES], F32)
        look_i = sb("look_i", [P, TILES], I32)
        prev_f = sb("prev_f", [P, TILES], F32)
        key_r = sb("key_r", [RR, 2], F32)
        key_i = sb("key_i", [RR, 2], I32)
        tail_slot = sb("tail_slot", [RR, 2], I32)
        tail_key = sb("tail_key", [P, TILES], F32)
        tail = sb("tail", [P, 2, D + 2], F32)
        count = sb("count", [P, TILES], F32)
        inv_deg = sb("inv_deg", [P, TILES], F32)
        inv_root = sb("inv_root", [P, TILES], F32)
        same8 = sb("same8", [P, TILES, P], U8)
        carry8 = sb("carry8", [P, TILES, P], U8)
        dst_row = sb("dst_row", [P, 2, TB * P], F32)
        x_out = sb("x_out", [P, 2, G, D], F32)
        rows_f = x_out[0:RR, :, :, :].rearrange("p a g d -> p (a g d)").rearrange("p (q c) -> p q c", c=RW)
        node = sb("node", [P, TILES, D], F32)
        far_map = sb("far_map", [P, MAP_ROWS // P], I32)

        st_src = sb("st_src", [P, 2, TB], I32)
        st_dst = sb("st_dst", [P, 2, TB], I32)
        st_val = sb("st_val", [P, 2, TB], I32)
        msg = sb("msg", [P, 2, TB, D + 2], F32)
        x_dst = sb("x_dst", [P, 2, TB, D], F32)
        own_row = x_dst
        got_slot = sb("got_slot", [P, 2, TB], I32)
        slot_d = sb("slot_d", [P, 2, TB], F32)
        same_f = sb("same_f", [P, TB, P], F32)
        carry_f = sb("carry_f", [P, TB, P], F32)
        tail_f = sb("tail_f", [P, TB, P], F32)
        sums = sb("sums", [P, 2, TB, D + 2], F32)
        inv_count = sb("inv_count", [P, TB], F32)
        pair = sb("pair", [P, 2, TB, 2 * D], F32)
        keep = sb("keep", [P, TB], F32)
        feat = sb("feat", [P, TB * P], F32)
        hid = sb("hid", [P, 2, TB * P], F32)
        edge_y = sb("edge_y", [P, TB, D], F32)
        edge_z = sb("edge_z", [P, TB, D], F32)
        new_row = sb("new_row", [P, 2, TB, D], F32)
        en = Norm(sb, sem, "edge_norm", TB)

        psum = [ctx.enter_context(nc.psum_tensor(f"ps{k}", [P, 512], F32)) for k in range(8)]
        DA, DB, DC, DD, EA, EB, EC, ED = psum
        sums_ps = EB[:, :].rearrange("p (j d) -> p j d", j=TB)

        s_zero = sem("s_zero"); s_load_e = sem("s_load_e"); s_load_w = sem("s_load_w"); s_prep = sem("s_prep")
        s_sel = sem("s_sel"); s_rows = sem("s_rows"); s_ct = sem("s_ct"); s_cc = sem("s_cc"); s_wself = sem("s_wself")
        s_map0 = sem("s_map0"); s_dstd = sem("s_dstd"); s_cols = sem("s_cols"); s_psel = sem("s_psel")
        s_tails = sem("s_tails"); s_tailr = sem("s_tailr"); s_pmem = sem("s_pmem")

        class Rows:

            def __init__(self, name, g, turn, hid_ps, res, hid=None, spare=None, squares=(None, None)):
                self.g = g
                self.turn, self.hid_ps, self.res = turn, hid_ps, res
                self.n0 = Norm(sb, sem, f"{name}_n0", g, (1.0 + EPS) / D, square=squares[0])
                self.n1 = Norm(sb, sem, f"{name}_n1", g, centred=res.rearrange("p (g d) -> p g d", d=D), square=squares[1])
                self.x2 = sb(f"{name}_x2", [P, g, D], F32)
                self.x2t, self.x3t, self.h1 = spare or [sb(f"{name}_{part}", [P, g * D], F32) for part in ("x2t", "x3t", "h1")]
                self.hid = hid if hid is not None else sb(f"{name}_hid", [P, 2, g * D], F32)
                self.x3 = sb(f"{name}_x3", [P, g, D], F32)
                self.s_x2, self.s_turn, self.s_x2t = sem(f"{name}_s_x2"), sem(f"{name}_s_turn"), sem(f"{name}_s_x2t")
                self.s_hidp, self.s_hid, self.s_y = sem(f"{name}_s_hidp"), sem(f"{name}_s_hid"), sem(f"{name}_s_y")
                self.s_x3, self.s_turn3, self.s_x3t = sem(f"{name}_s_x3"), sem(f"{name}_s_turn3"), sem(f"{name}_s_x3t")
                self.s_h1p, self.s_h1 = sem(f"{name}_s_h1p"), sem(f"{name}_s_h1")

            def transposes(self, rows, done):
                for k in range(self.g // 2):
                    last = nc.tensor.transpose(self.turn[:, k * P:(k + 1) * P],
                                               rows[:, 2 * k:2 * k + 2, :].rearrange("p a d -> p (a d)"), ident[:, :])
                last.then_inc(done, 1)

            def pe_middle(self, pe, n):
                pe.wait_ge(self.s_x2, n + 1)
                if at_least(n, 1):
                    pe.wait_ge(self.s_x3t, n)
                self.transposes(self.x2, self.s_turn)
                pe.wait_ge(self.s_x2t, n + 1)
                if at_least(n, 1):
                    pe.wait_ge(self.s_h1, n)
                for h in range(2):
                    last = nc.tensor.matmul(self.hid_ps[h], w_self[64 * h:64 * h + 64, :],
                                            self.x2t[64 * h:64 * h + 64, :], start=True, stop=True)
                last.then_inc(self.s_hidp, 1)
                nc.tensor.matmul(self.res, one_row[:, :], out_bias_c[:, 0:self.g, :].rearrange("p g d -> p (g d)"),
                                 start=True, stop=True)
                for q in range(self.g // 2):
                    nc.tensor.matmul(self.res[:, q * P:(q + 1) * P], self.x2t[:, q * P:(q + 1) * P], centring[:, :],
                                     start=False, stop=True, skip_group_check=True)
                pe.wait_ge(self.s_hid, n + 1)
                for k in range(self.g):
                    last = nc.tensor.matmul(self.res[:, k * D:(k + 1) * D],
                                            self.hid[:, k % 2, (k // 2) * P:(k // 2 + 1) * P], w_out_c[:, :],
                                            start=False, stop=True, skip_group_check=True)
                last.then_inc(self.s_y, 1)

            def act_middle(self, act, n):
                act.wait_ge(self.s_turn, n + 1)
                nc.scalar.activation(self.x2t[:, :], self.turn, ACT.Copy).then_inc(self.s_x2t, 1)
                act.wait_ge(self.s_hidp, n + 1)
                for h in range(2):
                    last = nc.scalar.activation(self.hid[:, h, :], self.hid_ps[h], ACT.Relu, bias=hid_bias[:, :])
                last.then_inc(self.s_hid, 1)

            def pe_low(self, pe, n, middles):
                pe.wait_ge(self.s_x3, n + 1)
                pe.wait_ge(self.s_x2t, middles)
                self.transposes(self.x3, self.s_turn3)
                pe.wait_ge(self.s_x3t, n + 1)
                pe.wait_ge(self.s_hid, middles)
                nc.tensor.matmul(self.hid_ps[0], w_conv[0][:, :], self.x3t[:, :], start=True,
                                 stop=True).then_inc(self.s_h1p, 1)

            def act_low(self, act, n):
                act.wait_ge(self.s_turn3, n + 1)
                nc.scalar.activation(self.x3t[:, :], self.turn, ACT.Copy).then_inc(self.s_x3t, 1)
                act.wait_ge(self.s_h1p, n + 1)
                nc.scalar.activation(self.h1[:, :], self.hid_ps[0], ACT.Relu, bias=conv_bias_col[:, :]).then_inc(self.s_h1, 1)

        dense = Rows("dense", G, DA[:, :], [DB[:, :], DC[:, :]], DD[:, :])
        dense_n2 = Norm(sb, sem, "dense_n2", G)
        dense_y = sb("dense_y", [P, G, D], F32)
        x_in = sb("x_in", [P, 2, G, D], F32)
        s_xin = [sem("s_xin0"), sem("s_xin1")]
        s_xout = sem("s_xout")
        s_stored = [sem("s_stored0"), sem("s_stored1")]
        s_h2 = sem("s_h2")
        link_d0, link_d1, link_d2 = Links(sem("s_link_d0"), 3), Links(sem("s_link_d1"), 1), Links(sem("s_link_d2"), 4)

        srows = Rows("source", TB, DA[:, 0:TB * D], [DB[:, 0:TB * D], DC[:, 0:TB * D]], EA[:, 0:TB * D], hid[:, :, 0:TB * D],
                     spare=[pair[:, k // 2, :, :].rearrange("p j d -> p (j d)")[:, k % 2 * TB * D:(k % 2 + 1) * TB * D] for k in range(3)],
                     squares=[tail_f[:, :, :].rearrange("p j d -> p (j d)")[:, k * TB * D:(k + 1) * TB * D]
                              .rearrange("p (g d) -> p g d", d=D) for k in range(2)])
        src_x1 = sb("src_x1", [P, TB, D], F32)
        src_root = sb("src_root", [P, TB], F32)
        src_inv = sb("src_inv", [P, TB], F32)
        src_h1 = sb("src_h1", [P, TB, D], F32)
        s_root1 = sem("s_root1")
        s_x1s = sem("s_x1s")
        s_h1t = sem("s_h1t")
        s_h1o = sem("s_h1o")
        s_sst = [sem(f"s_sst{k}") for k in range(4)]
        link_s0, link_s1 = Links(sem("s_link_s0"), 4), Links(sem("s_link_s1"), 1)

        s_stage = sem("s_stage")
        s_row = [sem("s_row0"), sem("s_row1")]
        s_row3 = [sem("s_row3_0"), sem("s_row3_1")]
        s_mask = sem("s_mask")
        s_scat = [sem("s_scat0"), sem("s_scat1")]
        s_msgin = [sem("s_msgin0"), sem("s_msgin1")]
        s_dstin = [sem("s_dstin0"), sem("s_dstin1")]
        s_node = sem("s_node")
        s_slotin = [sem("s_slotin0"), sem("s_slotin1")]
        s_msg = sem("s_msg")
        s_same = sem("s_same")
        s_sum = sem("s_sum")
        s_sums = sem("s_sums")
        s_new = sem("s_new")
        s_put = [sem("s_put0"), sem("s_put1")]
        s_scattered = [sem("s_scattered0"), sem("s_scattered1")]
        s_ownin = [sem("s_ownin0"), sem("s_ownin1")]
        link_l = Links(sem("s_link_look"), 2)
        link_b = {1: Links(sem("s_link_b1"), 6), 2: Links(sem("s_link_b2"), 4), 3: Links(sem("s_link_b3"), 7),
                  5: Links(sem("s_link_b5"), 4)}
        link_f = {3: Links(sem("s_link_f3"), 2), 4: Links(sem("s_link_f4"), 2), 5: Links(sem("s_link_f5"), 1)}
        s_look = sem("s_look")
        s_tailf = sem("s_tailf"); s_tailp = sem("s_tailp"); s_pair = sem("s_pair"); s_pairt = sem("s_pairt")
        s_feat = sem("s_feat"); s_hidp = sem("s_hidp"); s_hide = sem("s_hide"); s_mp = sem("s_mp")
        s_agg = [sem("s_agg4"), sem("s_agg5")]
        s_aggt = [sem("s_aggt4"), sem("s_aggt5")]
        s_aggc = [sem("s_aggc4"), sem("s_aggc5")]
        s_conv = [sem("s_conv4"), sem("s_conv5")]
        s_deg = sem("s_deg"); s_deg2 = sem("s_deg2"); s_x3e = sem("s_x3e")

        NORM = {1: 0, 2: 1, 3: 2, 5: 3}

        def before(ph):
            return (ph - 1) * BATCHES

        def before_par(ph, par):
            return (ph - 1) * ((BATCHES + 1 - par) // 2)

        def past(b, lag):
            return isinstance(b, int) and b - lag >= BLOCKS

        def norms(ph, n):
            return n + NORM[ph] * BATCHES

        x_blocks = x[0:(BLOCKS - 1) * BLOCK, :].rearrange("(b p g) d -> b p g d", p=P, g=G)
        out_blocks = out[0:(BLOCKS - 1) * BLOCK, :].rearrange("(b p g) d -> b p g d", p=P, g=G)

        def dense_rows(blocks, whole, b):
            if isinstance(b, int) and b == BLOCKS - 1:
                return whole[N - BLOCK:N, :].rearrange("(p g) d -> p g d", g=G)
            return blocks[b]

        def table_rows(k, b, half):
            t = table[k][half * E_PAD:(half + 1) * E_PAD, :].rearrange("(b j p) d -> b p j d", j=TB, p=P)
            return t[b]

        block = ctx.enter_context(nc.Block())

        @block.sync
        def _(sp):
            sp.wait_ge(s_zero, 1)
            full = E // RW
            rest = E - full * RW
            sp.dma_start(src_r[0:full, :], src[0:full * RW].rearrange("(r c) -> r c", c=RW)).then_inc(s_load_e, 16)
            sp.dma_start(src_r[full:full + 1, 0:rest], src[full * RW:E].rearrange("(r c) -> r c", r=1)).then_inc(s_load_e, 16)
            sp.dma_start(dst_r[0:full, :], dst[0:full * RW].rearrange("(r c) -> r c", c=RW)).then_inc(s_load_e, 16)
            sp.dma_start(dst_r[full:full + 1, 0:rest], dst[full * RW:E].rearrange("(r c) -> r c", r=1)).then_inc(s_load_e, 16)
            sp.dma_start(nxt_r[0:full, :], dst[1:full * RW + 1].rearrange("(r c) -> r c", c=RW)).then_inc(s_load_e, 16)
            sp.dma_start(nxt_r[full:full + 1, 0:rest - 1], dst[full * RW + 1:E].rearrange("(r c) -> r c", r=1)).then_inc(s_load_e, 16)
            sp.dma_start(weight_r[0:full, :], edge_weight[0:full * RW].rearrange("(r c) -> r c", c=RW)).then_inc(s_load_e, 16)
            sp.dma_start(weight_r[full:full + 1, 0:rest], edge_weight[full * RW:E].rearrange("(r c) -> r c", r=1)).then_inc(s_load_e, 16)
            sp.dma_start(slot_map.rearrange("(p c) a -> p (c a)", p=P), far_map[:, :]).then_inc(s_map0, 16)
            sp.wait_ge(s_rows, 1)
            sp.dma_start(dst_dram.rearrange("(r c) -> r c", c=RW), rows_f[:, 1, :]).then_inc(s_dstd, 16)
            sp.wait_ge(s_dstd, 16)

            dst_rows = dst_dram.rearrange("(b a c) -> b a c", a=1, c=TB * P)

            def dense_load(b, par):
                if at_least(b, 2):
                    wait(sp, (s_dstd, 16), dense.n0.s_centred, b - 1)
                sp.dma_start(x_in[:, par, :, :], dense_rows(x_blocks, x, b)).then_inc(s_xin[par], 16)

            def dense_store(b, par):
                wait(sp, (s_dstd, 16), s_xout, b + 1)
                if isinstance(b, int) and b == BLOCKS - 1:
                    sp.wait_ge(s_stored[1 - par], 16 * (BLOCKS // 2))
                sp.dma_start(dense_rows(out_blocks, out, b), x_out[:, par, :, :]).then_inc(s_stored[par], 16)

            def phase0(i, par, k):
                if at_least(i, 2):
                    wait(sp, (s_dstd, 16), s_mask, i - 1)
                sp.dma_start(dst_row[:, par, :], dst_rows[i].broadcast_to([P, TB * P])).then_inc(s_row[par], 16)
                dense_load(i, par)
                if at_least(i, 3):
                    dense_store(i - 3, 1 - par)
            batches(sp, phase0)

            def phase1(i, par, k):
                if at_least(i, 1):
                    wait(sp, (s_dstd, 16), srows.s_x3, i)
                    sp.dma_start(table_rows(3, i - 1, 1), srows.x3[:, :, :]).then_inc(s_sst[2], 16)
                    wait(sp, (s_dstd, 16), s_h1o, i)
                    sp.dma_start(table_rows(4, i - 1, 1), src_h1[:, :, :]).then_inc(s_sst[3], 16)
                if isinstance(i, int) and i == BATCHES:
                    return
                wait(sp, (s_dstd, 16), s_x1s, i + 1)
                sp.dma_start(table_rows(2, i, 1), srows.x2[:, :, :]).then_inc(s_sst[1], 16)
                sp.dma_start(table_rows(1, i, 1), src_x1[:, :, :]).then_inc(s_sst[0], 16)
                if at_least(i, 1):
                    put(1, i - 1, *back(par, k, 1))

            def put(ph, i, par, k):
                wait(sp, (s_dstd, 16), s_new, i + 1 + before(ph))
                if ph > 1 or at_least(i, 2):
                    wait(sp, (s_dstd, 16), s_put[par], 16 * (k + before_par(ph, par)))
                rows = node[:, bass.ts(i, TB), :] if ph < 3 else new_row[:, par, :, :]
                sp.dma_start(table_rows(ph, i, 0), rows).then_inc(s_put[par], 16)

            batches(sp, phase1)
            put(1, BATCHES - 1, (BATCHES - 1) % 2, (BATCHES - 1) // 2)
            phase1(BATCHES, BATCHES % 2, BATCHES // 2)

            def phase2(i, par, k):
                put(2, i, par, k)
            batches(sp, phase2)

            def phase3(i, par, k):
                if at_least(i, 2):
                    wait(sp, (s_dstd, 16), s_tailf, i - 1)
                sp.dma_start(dst_row[:, par, :], dst_rows[i].broadcast_to([P, TB * P])).then_inc(s_row3[par], 16)
                if at_least(i, 1):
                    put(3, i - 1, *back(par, k, 1))
            batches(sp, phase3)
            put(3, BATCHES - 1, (BATCHES - 1) % 2, (BATCHES - 1) // 2)

            def phase4(i, par, k):
                dense_load(i + BATCHES, 1 - par)
                dense_store(i + BATCHES - 3, par)
                if at_least(i, 1):
                    put(4, i - 1, *back(par, k, 1))
            batches(sp, phase4)
            put(4, BATCHES - 1, (BATCHES - 1) % 2, (BATCHES - 1) // 2)
            for b in range(BLOCKS - 3, BLOCKS):
                dense_store(b, b % 2)

            sp.wait_ge(s_put[0], 16 * before_par(5, 0))
            sp.wait_ge(s_put[1], 16 * before_par(5, 1))

            def phase5(i, par, k):
                if at_least(i, 2):
                    wait(sp, (s_dstd, 16), s_agg[1], i - 1)
                sp.dma_start(own_row[:, par, :, :], table_rows(4, i, 0)).then_inc(s_ownin[par], 16)
            batches(sp, phase5)

        @block.gpsimd
        def _(pool):
            nc.gpsimd.memset(far_map[:, :], FAR)
            nc.gpsimd.memset(src_r[:, :], 0)
            nc.gpsimd.memset(dst_r[:, :], PAD_DST)
            nc.gpsimd.memset(nxt_r[:, :], PAD_DST)
            nc.gpsimd.memset(weight_r[:, :], 0.0)
            nc.gpsimd.memset(w_conv[0][:, :], 0.0)
            nc.gpsimd.memset(w_conv[1][:, :], 0.0)
            nc.gpsimd.memset(out_bias[:, :, :], 0.0)
            nc.gpsimd.memset(conv_bias[0][:, :, :], 0.0)
            nc.gpsimd.memset(conv_bias[1][:, :, :], 0.0)
            nc.gpsimd.memset(ident[:, :], 0.0).then_inc(s_zero, 1)
            pool.wait_ge(s_zero, 1)
            nc.gpsimd.affine_select(out=ident[:, :], in_=ident[:, :], compare_op=ALU.not_equal, fill=1.0, base=0,
                                    pattern=[[-1, P]], channel_multiplier=1).then_inc(s_psel, 1)
            for h in range(2):
                pool.dma_start(w_self[64 * h:64 * h + 64, :], w_21[0:D, :]).then_inc(s_load_w, 16)
                pool.dma_start(w_part[64 * h:64 * h + 64, :], w_21[D:2 * D, :]).then_inc(s_load_w, 16)
                pool.dma_start(w_conv[0][64 * h:64 * h + 64, 64 * h:64 * h + 64], w_31).then_inc(s_load_w, 16)
                pool.dma_start(w_conv[1][64 * h:64 * h + 64, 64 * h:64 * h + 64], w_32).then_inc(s_load_w, 16)
                pool.dma_start(conv_bias_col[64 * h:64 * h + 64, :], b_31.rearrange("(d a) -> d a", a=1)).then_inc(s_load_w, 16)
            pool.dma_start(w_src_dst[:, :], w_21).then_inc(s_load_w, 16)
            pool.dma_start(w_out[:, :], w_22).then_inc(s_load_w, 16)
            pool.dma_start(hid_bias[:, :], b_21.rearrange("(d a) -> d a", a=1)).then_inc(s_load_w, 16)
            for to, b in ((out_bias, b_22), (conv_bias[0], b_31), (conv_bias[1], b_32)):
                for g in range(G):
                    pool.dma_start(to[0:1, g, :], b.rearrange("(a d) -> a d", a=1)).then_inc(s_load_w, 16)
            nc.gpsimd.iota(slot_i[:, :], pattern=[[P, TILES]], base=0, channel_multiplier=1).then_inc(s_psel, 1)
            nc.gpsimd.iota(own_i[:, :], pattern=[[P, TILES]], base=E_PAD, channel_multiplier=1).then_inc(s_psel, 1)
            pool.wait_ge(s_cols, 1)
            nc.gpsimd.affine_select(out=prev_f[:, :], in_=prev_f[:, :], compare_op=ALU.is_ge, fill=-1.0, base=-(P - 1),
                                    pattern=[[0, TILES]], channel_multiplier=1).then_inc(s_psel, 1)
            nc.gpsimd.affine_select(out=tail_key[:, :], in_=tail_key[:, :], compare_op=ALU.is_equal, fill=-1.0, base=0,
                                    pattern=[[1, RR], [0, 2]], channel_multiplier=-1).then_inc(s_psel, 1)
            pool.wait_ge(s_psel, 5)
            pool.wait_ge(s_map0, 16)

            def stage(pieces):
                for to, frm in pieces:
                    last = nc.gpsimd.tensor_copy(to, frm)
                last.then_inc(s_stage, 1)
                pool.wait_ge(s_stage, 1)

            def cols_of(t, i):
                return t[:, bass.ts(i, TB)]

            def gather(to, rows, idx, done):
                return pool.indirect_dma_start(out=to, out_offset=None, in_=rows,
                                               in_offset=bass.IndirectOffsetOnAxis(ap=idx, axis=0)).then_inc(done, 16)

            def phase0(i, par, k):
                pool.sem_clear(s_stage)
                if at_least(i, 2):
                    wait(pool, (s_psel, 5), s_scat[par], 16 * TB * k)
                    wait(pool, (s_psel, 5), s_node, i - 1)
                stage([(st_src[:, par, :], cols_of(scat_i, i)), (st_val[:, par, :], cols_of(slot_i, i)),
                       (st_dst[:, par, :], cols_of(dst_i, i))])
                for j in range(TB):
                    pool.indirect_dma_start(out=slot_map, out_offset=bass.IndirectOffsetOnAxis(ap=st_src[:, par, j:j + 1], axis=0),
                                            in_=st_val[:, par, j:j + 1], in_offset=None,
                                            bounds_check=MAP_ROWS - 1, oob_is_err=False).then_inc(s_scat[par], 16)
                for j in range(TB):
                    gather(x_dst[:, par, j, :], x, st_dst[:, par, j:j + 1], s_dstin[par])
            batches(pool, phase0)
            pool.wait_ge(s_scat[0], 16 * TB * ((BATCHES + 1) // 2))
            pool.wait_ge(s_scat[1], 16 * TB * (BATCHES // 2))

            def phase1(i, par, k):
                pool.sem_clear(s_stage)
                if at_least(i, 2):
                    wait(pool, (s_psel, 5), s_sum, TB * (i - 1) + TB * before(1))
                    wait(pool, (s_psel, 5), srows.n0.s_centred, i - 1)
                    wait(pool, (s_psel, 5), s_look, i - 1)
                stage([(st_src[:, par, :], cols_of(src_i, i))])
                for j in range(TB):
                    gather(msg[:, par, j, 0:D], x, st_src[:, par, j:j + 1], s_msgin[par])
                for j in range(TB):
                    gather(got_slot[:, par, j:j + 1], slot_map, st_src[:, par, j:j + 1], s_slotin[par])
            batches(pool, phase1)
            for h in range(2):
                gather(tail_slot[:, h:h + 1], slot_map, key_i[:, h:h + 1], s_tails)

            for ph in (2, 3, 4, 5):
                pool.wait_ge(s_put[0], 16 * before_par(ph, 0))
                pool.wait_ge(s_put[1], 16 * before_par(ph, 1))
                pool.wait_ge(s_sst[ph - 2], 16 * BATCHES)
                if ph == 2:
                    pool.wait_ge(s_look, BATCHES)
                if ph == 3:
                    pool.wait_ge(s_tails, 32)
                    for h in range(2):
                        pool.indirect_dma_start(out=tail[0:RR, h, 0:D], out_offset=None, in_=table[2],
                                                in_offset=bass.IndirectOffsetOnAxis(ap=tail_slot[:, h:h + 1], axis=0),
                                                bounds_check=2 * E_PAD - 1, oob_is_err=False).then_inc(s_tailr, 16)
                if ph == 5:
                    pool.wait_ge(s_stored[0], 16 * (BLOCKS // 2))
                    pool.wait_ge(s_stored[1], 16 * (BLOCKS // 2))

                def phase(i, par, k, ph=ph):
                    pool.sem_clear(s_stage)
                    to = pair[:, par, :, 0:D] if ph == 3 else msg[:, par, :, 0:D]
                    if at_least(i, 2):
                        if ph == 3:
                            wait(pool, (s_psel, 5), s_pairt, i - 1)
                        else:
                            wait(pool, (s_psel, 5), s_sum, TB * (i - 1) + TB * before(ph))
                    stage([(st_src[:, par, :], cols_of(look_i, i))])
                    for j in range(TB):
                        gather(to[:, j, :], table[ph - 1], st_src[:, par, j:j + 1], s_msgin[par])
                    if ph == 5 and at_least(i, 2):
                        scatter(i - 2, par, k - 1)

                def scatter(i, par, k):
                    pool.sem_clear(s_stage)
                    if at_least(i, 2):
                        wait(pool, (s_psel, 5), s_scattered[par], 16 * TB * k)
                    wait(pool, (s_psel, 5), s_new, i + 1 + before(5))
                    stage([(st_dst[:, par, :], cols_of(scat_i, i))])
                    for j in range(TB):
                        pool.indirect_dma_start(out=out, out_offset=bass.IndirectOffsetOnAxis(ap=st_dst[:, par, j:j + 1], axis=0),
                                                in_=new_row[:, par, j, :], in_offset=None,
                                                bounds_check=N - 1, oob_is_err=False).then_inc(s_scattered[par], 16)
                batches(pool, phase)
            for b in range(BATCHES - 2, BATCHES):
                scatter(b, b % 2, b // 2)
            pool.wait_ge(s_scattered[0], 16 * TB * ((BATCHES + 1) // 2))
            pool.wait_ge(s_scattered[1], 16 * TB * (BATCHES // 2))

        @block.scalar
        def _(act):
            act.wait_ge(s_prep, 1)

            act.wait_ge(s_load_w, 16 * 37)

            def expand(ph, i):
                if ph > 1 or at_least(i, 1):
                    act.wait_ge(s_sum, TB * i + TB * before(ph))
                nc.scalar.activation(same_f[:, :, :], same8[:, bass.ts(i, TB), :], ACT.Copy)
                nc.scalar.activation(carry_f[:, :, :], carry8[:, bass.ts(i, TB), :], ACT.Copy).then_inc(s_same, 1)

            def take_sums(ph, i, par, tiles):
                for j in tiles:
                    act.wait_ge(s_sum, TB * i + j + 1 + TB * before(ph))
                    nc.scalar.activation(sums[:, par, j, :], sums_ps[:, j, 0:D + 2], ACT.Copy).then_inc(s_sums, 1)

            def dense_squares(b):
                if at_least(b, 1) and not past(b, 1):
                    dense.n1.act_square(nc, act, b - 1, dense.s_y)
                if not past(b, 0):
                    dense.n0.act_square(nc, act, b)
                if at_least(b, 2):
                    dense_n2.act_square(nc, act, b - 2)

            def dense_roots(b):
                if at_least(b, 1) and not past(b, 1):
                    dense.n1.act_root(nc, act, b - 1, eps[:, :])
                if not past(b, 0):
                    dense.n0.act_root(nc, act, b, eps_x2[:, :])
                if at_least(b, 2):
                    dense_n2.act_root(nc, act, b - 2, eps[:, :])

            def dense_products(b):
                if at_least(b, 1) and not past(b, 1):
                    dense.act_low(act, b - 1)
                if not past(b, 0):
                    dense.act_middle(act, b)

            def phase0(i, par, k):
                dense_squares(i)
                dense_roots(i)
                act.wait_ge(s_dstin[par], 16 * TB * (k + 1))
                nc.scalar.activation(node[:, bass.ts(i, TB), :], x_dst[:, par, :, :], ACT.Copy).then_inc(s_node, 1)
                dense_products(i)
            batches(act, phase0)

            act.wait_ge(s_mask, BATCHES)

            def edge_square(ph, i):
                en.act_square(nc, act, norms(ph, i))

            def edge_root(ph, i):
                en.act_root(nc, act, norms(ph, i), eps[:, :])

            def phase1(i, par, k):
                pb, kb = back(par, k, 1)
                live = not (isinstance(i, int) and i == BATCHES)
                lag = at_least(i, 1)
                if live:
                    expand(1, i)
                if lag:
                    srows.n1.act_square(nc, act, i - 1, srows.s_y)
                if live:
                    srows.n0.act_square(nc, act, i)
                    take_sums(1, i, par, (0,))
                if lag:
                    srows.n1.act_root(nc, act, i - 1, eps[:, :])
                    edge_square(1, i - 1)
                if live:
                    take_sums(1, i, par, (1,))
                    srows.n0.act_root(nc, act, i, eps_x2[:, :])
                    nc.scalar.activation(src_root[:, :], srows.n0.total[:, :], ACT.Sqrt, bias=eps_x1[:, :],
                                         scale=1.0 / D).then_inc(s_root1, 1)
                    take_sums(1, i, par, (2,))
                if lag:
                    edge_root(1, i - 1)
                if live:
                    take_sums(1, i, par, (3,))
                if lag:
                    srows.act_low(act, i - 1)
                    act.wait_ge(s_h1t, i)
                    if at_least(i, 2):
                        act.wait_ge(s_sst[3], 16 * (i - 1))
                    nc.scalar.activation(src_h1[:, :, :], EC[:, 0:TB * D].rearrange("p (j d) -> p j d", d=D), ACT.Copy).then_inc(s_h1o, 1)
                if live:
                    srows.act_middle(act, i)
            batches(act, phase1)
            phase1(BATCHES, BATCHES % 2, BATCHES // 2)

            def phase2(i, par, k):
                expand(2, i)
                take_sums(2, i, par, (0, 1))
                if at_least(i, 1):
                    edge_square(2, i - 1)
                    edge_root(2, i - 1)
                take_sums(2, i, par, (2, 3))
            batches(act, phase2)
            edge_square(2, BATCHES - 1)
            edge_root(2, BATCHES - 1)

            act.wait_ge(s_deg, 1)
            nc.scalar.activation(inv_root[:, :], inv_deg[:, :], ACT.Sqrt).then_inc(s_deg2, 1)

            def phase3(i, par, k):
                expand(3, i)
                if at_least(i, 1):
                    edge_square(3, i - 1)
                act.wait_ge(s_pairt, i + 1)
                nc.scalar.activation(feat[:, :], EC[:, :], ACT.Copy).then_inc(s_feat, 1)
                if at_least(i, 1):
                    edge_root(3, i - 1)
                act.wait_ge(s_hidp, i + 1)
                nc.scalar.activation(hid[:, 0, :], DB[:, :], ACT.Relu, bias=hid_bias[:, :])
                nc.scalar.activation(hid[:, 1, :], DC[:, :], ACT.Relu, bias=hid_bias[:, :]).then_inc(s_hide, 1)
                act.wait_ge(s_mp, i + 1)
                nc.scalar.activation(msg[:, par, :, 0:D], EA[:, 0:TB * D].rearrange("p (j d) -> p j d", d=D), ACT.Copy).then_inc(s_msg, 1)
                take_sums(3, i, par, range(TB))
            batches(act, phase3)
            edge_square(3, BATCHES - 1)
            edge_root(3, BATCHES - 1)

            def aggregate(ph, i):
                act.wait_ge(s_aggt[ph - 4], i + 1)
                nc.scalar.activation(feat[:, 0:TB * D], EA[:, 0:TB * D], ACT.Copy).then_inc(s_aggc[ph - 4], 1)

            def phase4(i, par, k):
                b = i + BATCHES
                expand(4, i)
                dense_squares(b)
                take_sums(4, i, par, (0,))
                dense_roots(b)
                take_sums(4, i, par, (1, 2, 3))
                aggregate(4, i)
                dense_products(b)
            batches(act, phase4)
            for b in (BLOCKS, BLOCKS + 1):
                dense_squares(b)
                dense_roots(b)
                dense_products(b)

            def phase5(i, par, k):
                expand(5, i)
                take_sums(5, i, par, (0, 1))
                if at_least(i, 1):
                    edge_square(5, i - 1)
                take_sums(5, i, par, (2, 3))
                if at_least(i, 1):
                    edge_root(5, i - 1)
                aggregate(5, i)
            batches(act, phase5)
            edge_square(5, BATCHES - 1)
            edge_root(5, BATCHES - 1)

        @block.tensor
        def _(pe):
            pe.wait_ge(s_psel, 1)
            pe.wait_ge(s_rows, 1)
            for q, row in enumerate((rows_f[:, 1, :], rows_f[:, 0, :], rows_f[:, 3, :], weight_r[:, :])):
                for h in range(2):
                    last = nc.tensor.transpose(psum[q][:, h * P:h * P + RR], row[:, h * P:(h + 1) * P], ident[0:RR, 0:RR])
            last.then_inc(s_ct, 1)
            pe.wait_ge(s_cc, 1)
            pe.wait_ge(s_wself, 1)

            def dense_products(b):
                if at_least(b, 1) and not past(b, 1):
                    n = b - 1
                    dense.pe_low(pe, n, b)
                    pe.wait_ge(dense.s_h1, n + 1)
                    if at_least(n, 1):
                        pe.wait_ge(dense_n2.s_centred, n)
                    nc.tensor.matmul(ED[:, :], one_row[:, :], conv_bias[1][:, :, :].rearrange("p g d -> p (g d)"),
                                     start=True, stop=True)
                    for q in range(G // 2):
                        last = nc.tensor.matmul(ED[:, q * P:(q + 1) * P], dense.h1[:, q * P:(q + 1) * P], w_conv[1][:, :],
                                                start=False, stop=True, skip_group_check=True)
                    last.then_inc(s_h2, 1)
                if not past(b, 0):
                    dense.pe_middle(pe, b)

            def sum_by_target(ph, i, par, width, message_ready):
                pe.wait_ge(s_same, i + 1 + before(ph))
                message_ready()
                if ph > 1 or not isinstance(i, int) or i >= 1:
                    pe.wait_ge(s_sums, TB * i + TB * before(ph))
                for j in range(TB):
                    nc.tensor.matmul(sums_ps[:, j, 0:width], same_f[:, j, :], msg[:, par, j, 0:width], start=j == 0, stop=True,
                                     skip_group_check=True)
                for j in range(TB):
                    carried = sums[:, par, j - 1, 0:width] if j else sums[:, 1 - par, TB - 1, 0:width]
                    if j:
                        pe.wait_ge(s_sums, TB * i + j + TB * before(ph))
                    nc.tensor.matmul(sums_ps[:, j, 0:width], carry_f[:, j, :], carried, start=False, stop=True,
                                     skip_group_check=True).then_inc(s_sum, 1)

            def phase0(i, par, k):
                dense_products(i)
            batches(pe, phase0)

            def phase1(i, par, k):
                live = not (isinstance(i, int) and i == BATCHES)
                if live:
                    sum_by_target(1, i, par, D + 2, lambda: pe.wait_ge(s_msgin[par], 16 * TB * (k + 1 + before_par(1, par))))
                if at_least(i, 1):
                    srows.pe_low(pe, i - 1, i)
                    pe.wait_ge(srows.s_h1, i)
                    if at_least(i, 2):
                        pe.wait_ge(s_h1o, i - 1)
                    for q in range(TB // 2):
                        last = nc.tensor.transpose(EC[:, q * P:(q + 1) * P], srows.h1[:, q * P:(q + 1) * P], ident[:, :])
                    last.then_inc(s_h1t, 1)
                if live:
                    srows.pe_middle(pe, i)
            batches(pe, phase1)
            phase1(BATCHES, BATCHES % 2, BATCHES // 2)

            def phase2(i, par, k):
                sum_by_target(2, i, par, D + 2, lambda: pe.wait_ge(s_msg, i + 1))
            batches(pe, phase2)

            pe.wait_ge(s_tailr, 32)

            def phase3(i, par, k):
                pe.wait_ge(s_tailf, i + 1)
                for j in range(TB):
                    last = nc.tensor.matmul(DA[:, j * P:j * P + D + 2], tail_f[:, j, :], tail[:, j % 2, :], start=True, stop=True)
                last.then_inc(s_tailp, 1)
                pe.wait_ge(s_pair, i + 1)
                for j in range(TB):
                    last = nc.tensor.transpose(EC[:, j * P:(j + 1) * P], pair[:, par, j, :], ident[:, :])
                last.then_inc(s_pairt, 1)
                pe.wait_ge(s_feat, i + 1)
                nc.tensor.matmul(DB[:, :], w_src_dst[:, :], feat[:, :], start=True, stop=True)
                nc.tensor.matmul(DC[:, :], w_self[D:2 * D, :], feat[D:2 * D, :], start=True, stop=True).then_inc(s_hidp, 1)
                nc.tensor.matmul(EA[:, :], one_row[:, :], out_bias[:, :, :].rearrange("p g d -> p (g d)"), start=True, stop=True)
                pe.wait_ge(s_hide, i + 1)
                for h in range(2):
                    for j in range(TB):
                        last = nc.tensor.matmul(EA[:, (h * TB + j) * D:(h * TB + j + 1) * D], hid[:, h, j * P:(j + 1) * P], w_out[:, :],
                                                start=False, stop=True, skip_group_check=True)
                last.then_inc(s_mp, 1)
                sum_by_target(3, i, par, D + 2, lambda: pe.wait_ge(s_msg, i + 1 + BATCHES))
            batches(pe, phase3)

            def aggregate(ph, i):
                pe.wait_ge(s_agg[ph - 4], i + 1)
                for q in range(TB // 2):
                    last = nc.tensor.transpose(EA[:, q * P:(q + 1) * P],
                                               edge_y[:, 2 * q:2 * q + 2, :].rearrange("p a d -> p (a d)"), ident[:, :])
                last.then_inc(s_aggt[ph - 4], 1)
                nc.tensor.matmul(EC[:, 0:TB * D], one_row[:, :], conv_bias[ph - 4][:, 0:TB, :].rearrange("p g d -> p (g d)"),
                                 start=True, stop=True)
                pe.wait_ge(s_aggc[ph - 4], i + 1)
                for q in range(TB // 2):
                    last = nc.tensor.matmul(EC[:, q * P:(q + 1) * P], feat[:, q * P:(q + 1) * P], w_conv[ph - 4][:, :],
                                            start=False, stop=True, skip_group_check=True)
                last.then_inc(s_conv[ph - 4], 1)

            def phase4(i, par, k):
                sum_by_target(4, i, par, D + 2, lambda: pe.wait_ge(s_msgin[par], 16 * TB * (k + 1 + before_par(4, par))))
                aggregate(4, i)
                dense_products(i + BATCHES)
            batches(pe, phase4)
            for b in (BLOCKS, BLOCKS + 1):
                dense_products(b)

            def phase5(i, par, k):
                sum_by_target(5, i, par, D + 2, lambda: pe.wait_ge(s_msgin[par], 16 * TB * (k + 1 + before_par(5, par))))
                aggregate(5, i)
            batches(pe, phase5)

        @block.vector
        def _(dve):
            nc.vector.memset(eps[:, :], EPS)
            nc.vector.memset(eps_x1[:, :], EPS / 4)
            nc.vector.memset(eps_x2[:, :], EPS * EPS / 4)
            nc.vector.memset(msg[:, :, :, :], 1.0)
            nc.vector.memset(sums[:, :, :, :], 0.0)
            nc.vector.memset(tail[:, :, 0:D], 0.0)
            nc.vector.memset(tail[:, :, D:D + 2], 1.0)
            nc.vector.memset(tail_key[:, :], -1.0)
            nc.vector.memset(one_row[:, :], 0.0).then_inc(s_pmem, 1)
            dve.wait_ge(s_pmem, 1)
            nc.vector.memset(prev_f[:, 0:1], -1.0)
            nc.vector.memset(one_row[0:1, :], 1.0).then_inc(s_prep, 1)
            dve.wait_ge(s_load_e, 16 * 8)
            link = Links(sem("s_link_p"), 19)
            link.begin(dve, 0)
            nc.vector.tensor_copy(rows_f[:, 0, :], src_r[:, :])
            nc.vector.tensor_copy(rows_f[:, 1, :], dst_r[:, :])
            link(nc.vector.tensor_copy(rows_f[:, 2, :], nxt_r[:, :]))
            link(nc.vector.tensor_tensor(same_r[:, :], rows_f[:, 1, :], rows_f[:, 2, :], ALU.is_equal))
            nc.vector.scalar_tensor_tensor(rows_f[:, 3, :], same_r[:, :], float(FAR), rows_f[:, 1, :], ALU.mult,
                                           ALU.add).then_inc(s_rows, 1)
            ends = rows_f[:, 1, :].rearrange("r (h c) -> r h c", h=2)[:, :, P - 1]
            goes = same_r[:, :].rearrange("r (h c) -> r h c", h=2)[:, :, P - 1]
            link(nc.vector.scalar_tensor_tensor(key_r[:, :], ends, 1.0, goes, ALU.add, ALU.mult))
            link(nc.vector.tensor_scalar(key_r[:, :], key_r[:, :], -1.0, None, ALU.add))
            nc.vector.tensor_copy(key_i[:, :], ends)
            nc.vector.tensor_copy(tail_key[0:RR, :].rearrange("k (r h) -> k r h", h=2),
                                  key_r[:, :].unsqueeze(1).broadcast_to([RR, RR, 2]))
            dve.wait_ge(s_ct, 1)
            for q in range(4):
                last = nc.vector.tensor_copy(cols[:, q, :].rearrange("p (r h) -> p h r", h=2),
                                             psum[q][:, 0:2 * P].rearrange("p (h r) -> p h r", h=2)[:, :, 0:RR])
            link(last)
            nc.vector.tensor_copy(src_i[:, :], cols[:, 1, :])
            nc.vector.tensor_scalar(dst_i[:, :], cols[:, 0, :], float(N - 1), None, ALU.min)
            nc.vector.tensor_copy(scat_i[:, :], cols[:, 2, :])
            nc.vector.tensor_copy(prev_f[:, 1:TILES], cols[:, 0, 0:TILES - 1]).then_inc(s_cc, 1)
            dve.wait_ge(s_cc, 1)
            nc.vector.tensor_copy(key_r[:, :], key_r[:, :]).then_inc(s_cols, 1)
            dve.wait_ge(s_psel, 5)
            nc.vector.tensor_copy(own_f[:, :], own_i[:, :])
            dve.wait_ge(s_load_w, 16 * 37)
            nc.vector.tensor_tensor(w_self[:, :], w_self[:, :], w_part[:, :], ALU.add)
            lw = Links(sem("s_link_w"), 4)
            lw.begin(dve, 0)
            nc.vector.memset(centring[:, :], 0.0)
            nc.vector.tensor_reduce(w_mean[:, 0:1], w_out[:, :], AX.X, ALU.add)
            lw(nc.vector.tensor_reduce(bias_mean[:, 0, :], out_bias[:, :, :], AX.X, ALU.add))
            nc.vector.memset(centring[0:D, 0:D], -1.0 / D)
            nc.vector.memset(centring[D:2 * D, D:2 * D], -1.0 / D)
            nc.vector.tensor_scalar(w_mean[:, 1:2], w_mean[:, 0:1], 1.0 / D, None, ALU.mult)
            lw(nc.vector.tensor_scalar(bias_mean[:, 1, :], bias_mean[:, 0, :], 1.0 / D, None, ALU.mult))
            nc.vector.tensor_scalar(w_out_c[:, :], w_out[:, :], w_mean[:, 1:2], None, ALU.subtract)
            lw(nc.vector.tensor_tensor(out_bias_c[:, :, :], out_bias[:, :, :], bc(bias_mean[:, 1, :], P, G, D), ALU.subtract))
            lw(nc.vector.tensor_tensor(centring[:, :], centring[:, :], ident[:, :], ALU.add))
            nc.vector.tensor_copy(w_mean[:, 0:1], w_mean[:, 1:2]).then_inc(s_wself, 1)

            def dense_centre(b, par, k):
                link_d0.begin(dve, b)
                dve.wait_ge(s_xin[par], 16 * (k + 1))
                dense.n0.dve_centre(nc, link_d0, x_in[:, par, :, :])

            def dense_x3(b):
                link_d1.begin(dve, b)
                if at_least(b, 1):
                    dve.wait_ge(dense.s_turn3, b)
                dense.n1.dve_scale(nc, dve, b, link_d1, dense.x3[:, :, :]).then_inc(dense.s_x3, 1)
                link_d1.end()

            def dense_x2(b):
                if at_least(b, 1):
                    dve.wait_ge(dense.s_turn, b)
                dense.n0.dve_scale(nc, dve, b, link_d0, dense.x2[:, :, :]).then_inc(dense.s_x2, 1)
                link_d0.end()

            def dense_y4(b):
                link_d2.begin(dve, b)
                dve.wait_ge(s_h2, b + 1)
                link_d2(nc.vector.scalar_tensor_tensor(dense_y[:, :, :], ED[:, :].rearrange("p (g d) -> p g d", d=D), 0.0,
                                                       dense.x3[:, :, :], ALU.max, ALU.add))
                dense_n2.dve_centre(nc, link_d2, dense_y[:, :, :])

            def dense_out(b, par, k):
                if at_least(b, 2):
                    dve.wait_ge(s_stored[par], 16 * k)
                dense_n2.dve_scale(nc, dve, b, link_d2, x_out[:, par, :, :]).then_inc(s_xout, 1)
                link_d2.end()

            def dense_first(b, par, k):
                if at_least(b, 2):
                    dense_y4(b - 2)
                if not past(b, 0):
                    dense_centre(b, par, k)
                if at_least(b, 1) and not past(b, 1):
                    dense.n1.dve_total(nc, dve, b - 1)

            def dense_second(b, par, k):
                if at_least(b, 2):
                    dense_n2.dve_total(nc, dve, b - 2)
                if not past(b, 0):
                    dense.n0.dve_total(nc, dve, b)
                if at_least(b, 1) and not past(b, 1):
                    dense_x3(b - 1)

            def dense_third(b, par, k):
                if not past(b, 0):
                    dense_x2(b)
                if at_least(b, 2):
                    dense_out(b - 2, par, k - 1)

            def phase0(i, par, k):
                dense_first(i, par, k)
                dve.wait_ge(s_row[par], 16 * (k + 1))
                for j in range(TB):
                    row = dst_row[:, par, j * P:(j + 1) * P]
                    t = i * TB + j
                    for to, key in ((same8, cols[:, 0, bass.ds(t, 1)]), (carry8, prev_f[:, bass.ds(t, 1)])):
                        last = nc.vector.tensor_scalar(to[:, bass.ds(t, 1), :].rearrange("p a e -> p (a e)"), row, key, None, ALU.is_equal)
                    if j == 1:
                        dense_second(i, par, k)
                last.then_inc(s_mask, 1)
                dense_third(i, par, k)
            batches(dve, phase0)

            def edge_centre(ph, y):
                en.dve_centre(nc, link_b[ph], y)

            def edge_total(ph, i):
                en.dve_total(nc, dve, norms(ph, i))

            def phase1(i, par, k):
                pb, kb = back(par, k, 1)
                live = not (isinstance(i, int) and i == BATCHES)
                lag = at_least(i, 1)
                lb = link_b[1]
                if lag:
                    srows.n1.dve_total(nc, dve, i - 1)
                if live:
                    link_s0.begin(dve, i)
                    dve.wait_ge(s_msgin[par], 16 * TB * (k + 1 + before_par(1, par)))
                    srows.n0.dve_centre(nc, link_s0, msg[:, par, :, 0:D])
                if lag:
                    lb.begin(dve, i - 1)
                    wait(dve, (s_wself, 1), s_sums, TB * i + TB * before(1))
                    nc.vector.tensor_copy(count[:, bass.ts(i - 1, TB)], sums[:, pb, :, D])
                    lb(nc.vector.reciprocal(inv_count[:, :], sums[:, pb, :, D]))
                    lb(nc.vector.tensor_tensor(edge_z[:, :, :], sums[:, pb, :, 0:D], bc(inv_count[:, :], P, TB, D), ALU.mult))
                    lb(nc.vector.scalar_tensor_tensor(edge_y[:, :, :], node[:, bass.ts(i - 1, TB), :], 3.0, edge_z[:, :, :], ALU.mult, ALU.add))
                    edge_centre(1, edge_y[:, :, :])
                if live:
                    srows.n0.dve_total(nc, dve, i)
                if lag:
                    link_s1.begin(dve, i - 1)
                    if at_least(i, 2):
                        dve.wait_ge(s_sst[2], 16 * (i - 1))
                    srows.n1.dve_scale(nc, dve, i - 1, link_s1, srows.x3[:, :, :]).then_inc(srows.s_x3, 1)
                    link_s1.end()
                    edge_total(1, i - 1)
                if live:
                    link_l.begin(dve, i)
                    dve.wait_ge(s_slotin[par], 16 * TB * (k + 1))
                    own = own_f[:, bass.ts(i, TB)]
                    link_l(nc.vector.tensor_tensor(slot_d[:, 0, :], got_slot[:, par, :], own, ALU.subtract))
                    link_l(nc.vector.scalar_tensor_tensor(slot_d[:, 1, :], got_slot[:, par, :], float(FAR), slot_d[:, 0, :], ALU.is_lt, ALU.mult))
                    nc.vector.tensor_tensor(look_i[:, bass.ts(i, TB)], slot_d[:, 1, :], own, ALU.add).then_inc(s_look, 1)
                    link_l.end()
                    if at_least(i, 1):
                        dve.wait_ge(s_sst[1], 16 * i)
                        dve.wait_ge(s_sst[0], 16 * i)
                    srows.n0.dve_scale(nc, dve, i, link_s0, srows.x2[:, :, :]).then_inc(srows.s_x2, 1)
                    dve.wait_ge(s_root1, i + 1)
                    link_s0(nc.vector.reciprocal(src_inv[:, :], src_root[:, :]))
                    nc.vector.tensor_tensor(src_x1[:, :, :], srows.n0.centred, bc(src_inv[:, :], P, TB, D), ALU.mult).then_inc(s_x1s, 1)
                    link_s0.end()
                if lag:
                    en.dve_scale(nc, dve, norms(1, i - 1), lb, node[:, bass.ts(i - 1, TB), :]).then_inc(s_new, 1)
                    lb.end()
            batches(dve, phase1)
            phase1(BATCHES, BATCHES % 2, BATCHES // 2)

            def finish2(i, par, k):
                edge_total(2, i)
                en.dve_scale(nc, dve, norms(2, i), link_b[2], node[:, bass.ts(i, TB), :]).then_inc(s_new, 1)
                link_b[2].end()

            def phase2(i, par, k):
                pb, kb = back(par, k, 1)
                if at_least(i, 1):
                    link_b[2].begin(dve, i - 1)
                    dve.wait_ge(s_sums, TB * i + TB * before(2))
                    link_b[2](nc.vector.tensor_tensor(edge_y[:, :, :], sums[:, pb, :, 0:D], node[:, bass.ts(i - 1, TB), :], ALU.add))
                    edge_centre(2, edge_y[:, :, :])
                dve.wait_ge(s_msgin[par], 16 * TB * (k + 1 + before_par(2, par)))
                m = msg[:, par, :, 0:D]
                nc.vector.tensor_tensor(m, m, bc(cols[:, 3, bass.ts(i, TB)], P, TB, D), ALU.mult).then_inc(s_msg, 1)
                if at_least(i, 1):
                    finish2(i - 1, pb, kb)
            batches(dve, phase2)
            last_b = BATCHES - 1
            link_b[2].begin(dve, last_b)
            dve.wait_ge(s_sums, TB * BATCHES + TB * before(2))
            link_b[2](nc.vector.tensor_tensor(edge_y[:, :, :], sums[:, last_b % 2, :, 0:D], node[:, last_b * TB:TILES, :], ALU.add))
            edge_centre(2, edge_y[:, :, :])
            finish2(last_b, last_b % 2, last_b // 2)

            lp = Links(sem("s_link_q"), 1)
            lp.begin(dve, 0)
            lp(nc.vector.tensor_scalar(inv_deg[:, :], count[:, :], 1.0, None, ALU.add))
            nc.vector.reciprocal(inv_deg[:, :], inv_deg[:, :]).then_inc(s_deg, 1)
            dve.wait_ge(s_deg2, 1)

            def tail_masks(i, par, k):
                dve.wait_ge(s_row3[par], 16 * (k + 1))
                if at_least(i, 1):
                    dve.wait_ge(s_tailp, i)
                for j in range(TB):
                    last = nc.vector.tensor_scalar(tail_f[:, j, :], dst_row[:, par, j * P:(j + 1) * P],
                                                   tail_key[:, bass.ds(i * TB + j, 1)], None, ALU.is_equal)
                last.then_inc(s_tailf, 1)

            def pairs(i, par, k):
                link_f[3].begin(dve, i)
                own = node[:, bass.ts(i, TB), :]
                dve.wait_ge(s_tailp, i + 1)
                tails = DA[:, :].rearrange("p (j d) -> p j d", j=TB)
                link_f[3](nc.vector.tensor_scalar(keep[:, :], tails[:, :, D], -1.0, 1.0, ALU.mult, ALU.add))
                link_f[3](nc.vector.tensor_tensor(edge_z[:, :, :], own, bc(keep[:, :], P, TB, D), ALU.mult))
                dve.wait_ge(s_msgin[par], 16 * TB * (k + 1 + before_par(3, par)))
                nc.vector.tensor_tensor(pair[:, par, :, D:2 * D], edge_z[:, :, :], tails[:, :, 0:D], ALU.add).then_inc(s_pair, 1)
                link_f[3].end()

            def targets3(i, par):
                lb = link_b[3]
                lb.begin(dve, i)
                dve.wait_ge(s_sums, TB * (i + 1) + TB * before(3))
                selfs = EA[:, TB * D:2 * TB * D].rearrange("p (j d) -> p j d", d=D)
                lb(nc.vector.tensor_tensor(edge_y[:, :, :], sums[:, par, :, 0:D], selfs, ALU.add))
                lb(nc.vector.tensor_tensor(edge_y[:, :, :], edge_y[:, :, :], bc(inv_deg[:, bass.ts(i, TB)], P, TB, D), ALU.mult))
                lb(nc.vector.tensor_tensor(edge_y[:, :, :], edge_y[:, :, :], node[:, bass.ts(i, TB), :], ALU.add))
                edge_centre(3, edge_y[:, :, :])

            def finish3(i, par, k):
                lb = link_b[3]
                own = node[:, bass.ts(i, TB), :]
                edge_total(3, i)
                if at_least(i, 2):
                    dve.wait_ge(s_put[par], 16 * (k + before_par(3, par)))
                lb(en.dve_scale(nc, dve, norms(3, i), lb, own))
                nc.vector.tensor_tensor(new_row[:, par, :, :], own, bc(inv_root[:, bass.ts(i, TB)], P, TB, D), ALU.mult).then_inc(s_new, 1)
                lb.end()

            def phase3(i, par, k):
                pb, kb = back(par, k, 1)
                tail_masks(i, par, k)
                if at_least(i, 1):
                    targets3(i - 1, pb)
                pairs(i, par, k)
                if at_least(i, 1):
                    finish3(i - 1, pb, kb)
            batches(dve, phase3)
            targets3(last_b, last_b % 2)
            finish3(last_b, last_b % 2, last_b // 2)

            def convolved():
                return EC[:, 0:TB * D].rearrange("p (j d) -> p j d", d=D)

            def hidden4(i, par, k):
                dve.wait_ge(s_conv[0], i + 1)
                if at_least(i, 2):
                    dve.wait_ge(s_put[par], 16 * (k + before_par(4, par)))
                nc.vector.scalar_tensor_tensor(new_row[:, par, :, :], convolved(), 0.0,
                                               bc(inv_root[:, bass.ts(i, TB)], P, TB, D), ALU.max, ALU.mult).then_inc(s_new, 1)

            def phase4(i, par, k):
                b = i + BATCHES
                pd, kd = 1 - par, k + BATCHES // 2 + par
                if at_least(i, 1):
                    hidden4(i - 1, *back(par, k, 1))
                dense_first(b, pd, kd)
                lf = link_f[4]
                lf.begin(dve, i)
                scale = bc(inv_root[:, bass.ts(i, TB)], P, TB, D)
                lf(nc.vector.tensor_tensor(edge_z[:, :, :], node[:, bass.ts(i, TB), :], scale, ALU.mult))
                dense_second(b, pd, kd)
                dve.wait_ge(s_sums, TB * (i + 1) + TB * before(4))
                lf(nc.vector.tensor_tensor(edge_z[:, :, :], edge_z[:, :, :], sums[:, par, :, 0:D], ALU.add))
                nc.vector.tensor_tensor(edge_y[:, :, :], edge_z[:, :, :], scale, ALU.mult).then_inc(s_agg[0], 1)
                lf.end()
                dense_third(b, pd, kd)
            batches(dve, phase4)
            hidden4(last_b, last_b % 2, last_b // 2)
            for b in (BLOCKS, BLOCKS + 1):
                for step in (dense_first, dense_second, dense_third):
                    step(b, b % 2, b // 2)

            def targets5(i):
                link_b[5].begin(dve, i)
                dve.wait_ge(s_conv[1], i + 1)
                link_b[5](nc.vector.scalar_tensor_tensor(edge_z[:, :, :], convolved(), 0.0, node[:, bass.ts(i, TB), :], ALU.max, ALU.add))
                edge_centre(5, edge_z[:, :, :])

            def finish5(i, par, k):
                edge_total(5, i)
                if at_least(i, 2):
                    dve.wait_ge(s_scattered[par], 16 * TB * k)
                en.dve_scale(nc, dve, norms(5, i), link_b[5], new_row[:, par, :, :]).then_inc(s_new, 1)
                link_b[5].end()

            def phase5(i, par, k):
                pb, kb = back(par, k, 1)
                if at_least(i, 1):
                    targets5(i - 1)
                lf = link_f[5]
                lf.begin(dve, i)
                dve.wait_ge(s_sums, TB * (i + 1) + TB * before(5))
                dve.wait_ge(s_ownin[par], 16 * (k + 1))
                lf(nc.vector.tensor_tensor(edge_y[:, :, :], own_row[:, par, :, :], sums[:, par, :, 0:D], ALU.add))
                nc.vector.tensor_tensor(edge_y[:, :, :], edge_y[:, :, :], bc(inv_root[:, bass.ts(i, TB)], P, TB, D), ALU.mult).then_inc(s_agg[1], 1)
                lf.end()
                if at_least(i, 1):
                    finish5(i - 1, pb, kb)
            batches(dve, phase5)
            targets5(last_b)
            finish5(last_b, last_b % 2, last_b // 2)


_INS = ["x", "src", "dst", "edge_weight", "L2_gnn_W1", "L2_gnn_b1", "L2_gnn_W2", "L2_gnn_b2",
        "L3_gnn_W1", "L3_gnn_b1", "L3_gnn_W2", "L3_gnn_b2"]


def kernel(**inputs):
    import numpy as np
    import concourse.bacc as bacc
    from concourse.bass_utils import run_bass_kernel_spmd

    nc = bacc.Bacc("TRN2", target_bir_lowering=False, num_devices=1)
    arrays, args = {}, []
    for name in _INS:
        a = np.ascontiguousarray(inputs[name])
        arrays[f"in_{name}"] = a
        args.append(nc.dram_tensor(f"in_{name}", a.shape, mybir.dt.from_np(a.dtype), kind="ExternalInput").ap())
    args.append(nc.dram_tensor("out_rows", (N, D), F32, kind="ExternalOutput").ap())
    build(nc, *args)
    got = run_bass_kernel_spmd(nc, [arrays], core_ids=[0])
    return got.results[0]["out_rows"]
```

```python
from contextlib import ExitStack

import concourse.bass as bass
import concourse.mybir as mybir
from concourse.alu_op_type import AluOpType as ALU

F32, BF16, I32, U8 = mybir.dt.float32, mybir.dt.bfloat16, mybir.dt.int32, mybir.dt.uint8
ACT = mybir.ActivationFunctionType
AX = mybir.AxisListType
P = 128
D = 64
EPS = 1e-5
N = 100000
E = 25000
TB = 4
E_PAD = -(-E // (P * TB)) * P * TB
TILES = E_PAD // P
BATCHES = TILES // TB
HEAD = 7
TAIL = 4
PAD_DST = N + 96
MAP_ROWS = N + 352
FAR = 1 << 20
RW = 2 * P
RR = E_PAD // RW
G = 8
HALF = G // 2
WHOLE = BATCHES
BLOCKS = WHOLE + -(-(N - WHOLE * P * G) // (P * HALF))
assert BLOCKS == 3 * BATCHES and BATCHES % 2


def bc(ap, *shape):
    return ap.unsqueeze(len(ap.shape)).broadcast_to(list(shape))


def batches(eng, body):
    for b in range(HEAD):
        body(b, b % 2, b // 2)
    with eng.Fori(0, (BATCHES - HEAD - TAIL) // 2) as r:
        body(r * 2 + HEAD, 1, r + HEAD // 2)
        body(r * 2 + HEAD + 1, 0, r + HEAD // 2 + 1)
    for b in range(BATCHES - TAIL, BATCHES):
        body(b, b % 2, b // 2)


def after(body, count):
    for i in range(BATCHES, BATCHES + count):
        body(i, i % 2, i // 2)


def at_least(i, least):
    return not isinstance(i, int) or i >= least


def back(par, k, by):
    return (1 - par, k - (by + 1) // 2 + par) if by % 2 else (par, k - by // 2)


def wait(eng, met, sem, value):
    if not isinstance(value, int):
        value = eng.snap(value)
        eng.wait_ge(*met)
    eng.wait_ge(sem, value)


class Links:

    def __init__(self, sem, per):
        self.sem, self.per = sem, per

    def begin(self, eng, n):
        self.eng, self.n, self.k = eng, n, 0

    def __call__(self, instruction):
        self.k += 1
        instruction.then_inc(self.sem, 1)
        self.eng.wait_ge(self.sem, self.n * self.per + self.k)

    def end(self):
        assert self.k == self.per, (self.k, self.per)


class Norm:

    def __init__(self, sb, sem, name, g, scale=1.0 / D, centring=True, square=None):
        self.g, self.scale = g, scale
        self.sum = sb(f"{name}_sum", [P, g], F32)
        self.centred = None if not centring else sb(f"{name}_centred", [P, g, D], F32)[:, :, :]
        self.square = square if square is not None else sb(f"{name}_square", [P, g, D], F32)
        self.total = sb(f"{name}_total", [P, g], F32)
        self.root = sb(f"{name}_root", [P, g], F32)
        self.inverse = sb(f"{name}_inverse", [P, g], F32)
        self.s_centred = None if not centring else sem(f"{name}_s_centred")
        self.s_square = sem(f"{name}_s_square")
        self.s_total = sem(f"{name}_s_total")
        self.s_root = sem(f"{name}_s_root")

    def dve_centre(self, nc, link, y, g=None):
        g = g or self.g
        link(nc.vector.tensor_reduce(self.sum[:, 0:g], y, AX.X, ALU.add))
        nc.vector.scalar_tensor_tensor(self.centred[:, 0:g, :], bc(self.sum[:, 0:g], P, g, D), -1.0 / D, y, ALU.mult,
                                       ALU.add).then_inc(self.s_centred, 1)

    def act_square(self, nc, act, n, ready=None, centred=None, g=None):
        g = g or self.g
        act.wait_ge(self.s_centred if ready is None else ready, n + 1)
        nc.scalar.activation(self.square[:, 0:g, :], (self.centred if centred is None else centred)[:, 0:g, :],
                             ACT.Square).then_inc(self.s_square, 1)

    def dve_total(self, nc, dve, n, g=None):
        g = g or self.g
        dve.wait_ge(self.s_square, n + 1)
        nc.vector.tensor_reduce(self.total[:, 0:g], self.square[:, 0:g, :], AX.X, ALU.add).then_inc(self.s_total, 1)

    def act_root(self, nc, act, n, eps):
        act.wait_ge(self.s_total, n + 1)
        nc.scalar.activation(self.root[:, :], self.total[:, :], ACT.Sqrt, bias=eps,
                             scale=self.scale).then_inc(self.s_root, 1)

    def dve_scale(self, nc, dve, n, link, out, centred=None, g=None):
        g = g or self.g
        dve.wait_ge(self.s_root, n + 1)
        link(nc.vector.reciprocal(self.inverse[:, 0:g], self.root[:, 0:g]))
        return nc.vector.tensor_tensor(out, (self.centred if centred is None else centred)[:, 0:g, :],
                                       bc(self.inverse[:, 0:g], P, g, D), ALU.mult)


def build(nc, x, src, dst, edge_weight, w_21, b_21, w_22, b_22, w_31, b_31, w_32, b_32, out):
    ctx = ExitStack()
    with ctx:
        def sb(name, shape, dt):
            return ctx.enter_context(nc.sbuf_tensor(name, shape, dt))

        def sem(name):
            return ctx.enter_context(nc.semaphore(name))

        slot_map = nc.dram_tensor("slot_map", [MAP_ROWS, 1], I32, kind="Internal").ap()
        dst_dram = nc.dram_tensor("dst_dram", [E_PAD], F32, kind="Internal").ap()
        table = [None] + [nc.dram_tensor(f"table{k}", [2 * E_PAD, D], F32, kind="Internal").ap() for k in (1, 2, 3, 4)]

        ident = sb("ident", [P, P], F32)
        ones = sb("ones", [P, P], BF16)
        out_bias = sb("out_bias", [P, G * D], BF16)
        conv_bias = [sb(f"conv_bias{k}", [P, G * D], BF16) for k in (0, 1)]
        out_bias_bc = sb("out_bias_bc", [P, D], F32)
        w_src_dst = sb("w_src_dst", [P, P], F32)
        w_self = sb("w_self", [P, P], F32)
        w_part = sb("w_part", [P, P], F32)
        w_out = sb("w_out", [P, D], F32)
        w_out_c = sb("w_out_c", [P, D], F32)
        w_mean = sb("w_mean", [P, 2], F32)
        centring = sb("centring", [P, P], F32)
        bias_mean = sb("bias_mean", [P, 2, G], F32)
        w_conv = [sb(f"w_conv{k}", [P, P], F32) for k in (0, 1)]
        hid_bias = sb("hid_bias", [P, 1], F32)
        conv_bias_col = sb("conv_bias_col", [P, 1], F32)
        eps = sb("eps", [P, 1], F32)
        eps_x1 = sb("eps_x1", [P, 1], F32)
        eps_x2 = sb("eps_x2", [P, 1], F32)

        src_r = sb("src_r", [RR, RW], I32)
        dst_r = sb("dst_r", [RR, RW], I32)
        nxt_r = sb("nxt_r", [RR, RW], I32)
        weight_r = sb("weight_r", [RR, RW], F32)
        same_r = sb("same_r", [RR, RW], F32)
        cols = sb("cols", [P, 4, TILES], F32)
        src_i = sb("src_i", [P, TILES], I32)
        dst_i = sb("dst_i", [P, TILES], I32)
        scat_i = sb("scat_i", [P, TILES], I32)
        slot_i = sb("slot_i", [P, TILES], I32)
        own_i = sb("own_i", [P, TILES], I32)
        own_f = sb("own_f", [P, TILES], F32)
        look_i = sb("look_i", [P, TILES], I32)
        prev_f = sb("prev_f", [P, TILES], F32)
        key_r = sb("key_r", [RR, 2], F32)
        key_i = sb("key_i", [RR, 2], I32)
        tail_slot = sb("tail_slot", [RR, 2], I32)
        tail_key = sb("tail_key", [P, TILES], F32)
        tail = sb("tail", [P, 2, D + 2], F32)
        count = sb("count", [P, TILES], F32)
        inv_deg = sb("inv_deg", [P, TILES], F32)
        inv_root = sb("inv_root", [P, TILES], F32)
        same8 = sb("same8", [P, TILES, P], U8)
        carry8 = sb("carry8", [P, TILES, P], U8)
        dst_row = sb("dst_row", [P, 2, TB * P], F32)
        x_out = sb("x_out", [P, 2, G, D], F32)
        rows_f = x_out[0:RR, :, :, :].rearrange("p a g d -> p (a g d)").rearrange("p (q c) -> p q c", c=RW)
        node = sb("node", [P, TILES, D], F32)
        far_map = sb("far_map", [P, MAP_ROWS // P], I32)

        st_src = sb("st_src", [P, 2, TB], I32)
        st_dst = sb("st_dst", [P, 2, TB], I32)
        st_val = sb("st_val", [P, 2, TB], I32)
        msg = sb("msg", [P, 2, TB, D + 2], F32)
        x_dst = sb("x_dst", [P, 2, TB, D], F32)
        own_row = x_dst
        selfs = x_dst
        got_slot = sb("got_slot", [P, 2, TB], I32)
        slot_d = sb("slot_d", [P, 2, TB], F32)
        same_f = sb("same_f", [P, TB, P], F32)
        carry_f = sb("carry_f", [P, TB, P], F32)
        tail_f = sb("tail_f", [P, TB, P], F32)
        sums = sb("sums", [P, 2, TB, D + 2], F32)
        inv_count = sb("inv_count", [P, TB], F32)
        pair = sb("pair", [P, 2, TB, 2 * D], F32)
        feat = sb("feat", [P, TB * P], F32)
        hid = sb("hid", [P, 2, TB * P], F32)
        edge_y = sb("edge_y", [P, TB, D], F32)
        edge_z = sb("edge_z", [P, TB, D], F32)
        new_row = sb("new_row", [P, 2, TB, D], F32)
        en = Norm(sb, sem, "edge_norm", TB)

        psum = [ctx.enter_context(nc.psum_tensor(f"ps{k}", [P, 512], F32)) for k in range(8)]
        DA, DB, DC, DD, EA, EB, EC, ED = psum
        bias_rows = [feat[:, :].rearrange("p (g d) -> p g d", d=D)] + [hid[:, k, :].rearrange("p (g d) -> p g d", d=D) for k in (0, 1)]
        sums_ps = EB[:, :].rearrange("p (j d) -> p j d", j=TB)

        s_zero = sem("s_zero"); s_load_e = sem("s_load_e"); s_load_w = sem("s_load_w"); s_prep = sem("s_prep")
        s_rows = sem("s_rows"); s_ct = sem("s_ct"); s_cc = sem("s_cc"); s_wself = sem("s_wself")
        s_map0 = sem("s_map0"); s_dstd = sem("s_dstd"); s_cols = sem("s_cols"); s_psel = sem("s_psel")
        s_tails = sem("s_tails"); s_tailr = sem("s_tailr"); s_pmem = sem("s_pmem")

        class Rows:

            def __init__(self, name, g, blocks, turn3, turn, res, x3, hid=None, spare=None, squares=(None, None)):
                self.g, self.blocks = g, blocks
                self.turn3, self.turn, self.res = turn3, turn, res
                self.hid_ps, self.h1_ps = [turn3, turn], turn3
                self.n0 = Norm(sb, sem, f"{name}_n0", g, (1.0 + EPS) / D, square=squares[0])
                self.n1 = Norm(sb, sem, f"{name}_n1", g, centring=False, square=squares[1])
                self.x2 = sb(f"{name}_x2", [P, g, D], F32)
                self.x2t, self.x3t, self.h1 = spare or [sb(f"{name}_{part}", [P, g * D], F32) for part in ("x2t", "x3t", "h1")]
                self.hid = hid if hid is not None else sb(f"{name}_hid", [P, 2, g * D], F32)
                self.x3 = x3
                self.s_x2, self.s_turn, self.s_x2t = sem(f"{name}_s_x2"), sem(f"{name}_s_turn"), sem(f"{name}_s_x2t")
                self.s_hidp, self.s_hid, self.s_y = sem(f"{name}_s_hidp"), sem(f"{name}_s_hid"), sem(f"{name}_s_y")
                self.s_x3, self.s_turn3, self.s_x3t = sem(f"{name}_s_x3"), sem(f"{name}_s_turn3"), sem(f"{name}_s_x3t")
                self.s_h1p, self.s_h1 = sem(f"{name}_s_h1p"), sem(f"{name}_s_h1")

            def has(self, i, step):
                return not isinstance(i, int) or 0 <= i - step < self.blocks

            def size(self, n, g):
                if not isinstance(n, int) or self.g < G:
                    return g
                return G if n < WHOLE else HALF

            def transposes(self, rows, to, done, g):
                for k in range(g // 2):
                    last = nc.tensor.transpose(to[:, k * P:(k + 1) * P],
                                               rows[:, 2 * k:2 * k + 2, :].rearrange("p a d -> p (a d)"), ident[:, :])
                last.then_inc(done, 1)

            def pe(self, pe, i, par, g, second, others):
                n, low = i - 1, i - 3
                middle, convs = self.has(i, 1), self.has(i, 3)
                g_middle, g_low = self.size(n, g), self.size(low, g)
                res = self.res[1 - par]
                if convs:
                    pe.wait_ge(self.s_x3, low + 1)
                    if not isinstance(i, int) or i - 3 >= 1:
                        pe.wait_ge(self.s_hid, i - 1 if middle else self.blocks)
                    self.transposes(self.x3[1 - par], self.turn3, self.s_turn3, g_low)
                if middle:
                    pe.wait_ge(self.s_x2, n + 1)
                    if at_least(n, 1):
                        pe.wait_ge(self.s_hid, n)
                    self.transposes(self.x2, self.turn, self.s_turn, g_middle)
                others[0]()
                if convs:
                    pe.wait_ge(self.s_x3t, low + 1)
                    nc.tensor.matmul(self.h1_ps[:, 0:g_low * D], w_conv[0][:, :], self.x3t[:, 0:g_low * D], start=True,
                                     stop=True).then_inc(self.s_h1p, 1)
                others[1]()
                if middle:
                    if at_least(n, 2):
                        pe.wait_ge(self.s_x3, n - 1)
                    nc.tensor.matmul(res[:, 0:g_middle * D], ones[:, :], out_bias[:, 0:g_middle * D],
                                     start=True, stop=True)
                    pe.wait_ge(self.s_x2t, n + 1)
                    for q in range(g_middle // 2):
                        nc.tensor.matmul(res[:, q * P:(q + 1) * P], self.x2t[:, q * P:(q + 1) * P], centring[:, :],
                                         start=False, stop=True, skip_group_check=True)
                    if convs:
                        pe.wait_ge(self.s_h1, low + 1)
                    for h in range(2):
                        last = nc.tensor.matmul(self.hid_ps[h][:, 0:g_middle * D], w_self[64 * h:64 * h + 64, :],
                                                self.x2t[64 * h:64 * h + 64, 0:g_middle * D], start=True, stop=True)
                    last.then_inc(self.s_hidp, 1)
                others[2]()
                if convs:
                    second(low, g_low)
                others[3]()
                if middle:
                    pe.wait_ge(self.s_hid, n + 1)
                    for k in range(g_middle):
                        last = nc.tensor.matmul(res[:, k * D:(k + 1) * D],
                                                self.hid[:, k % 2, (k // 2) * P:(k // 2 + 1) * P], w_out_c[:, :],
                                                start=False, stop=True, skip_group_check=True)
                    last.then_inc(self.s_y, 1)

            def rows(self, par):
                return self.res[par].rearrange("p (g d) -> p g d", d=D)

            def act_square3(self, act, i, par, g):
                if self.has(i, 2):
                    self.n1.act_square(nc, act, i - 2, self.s_y, self.rows(par), self.size(i - 2, g))

            def act_root3(self, act, i):
                if self.has(i, 2):
                    self.n1.act_root(nc, act, i - 2, eps[:, :])

            def act_turned(self, act, i, g):
                if self.has(i, 3):
                    cols3 = self.size(i - 3, g) * D
                    act.wait_ge(self.s_turn3, i - 2)
                    nc.scalar.activation(self.x3t[:, 0:cols3], self.turn3[:, 0:cols3], ACT.Copy).then_inc(self.s_x3t, 1)
                if self.has(i, 1):
                    cols2 = self.size(i - 1, g) * D
                    act.wait_ge(self.s_turn, i)
                    nc.scalar.activation(self.x2t[:, 0:cols2], self.turn[:, 0:cols2], ACT.Copy).then_inc(self.s_x2t, 1)

            def act_h1(self, act, i, g):
                if self.has(i, 3):
                    width = self.size(i - 3, g) * D
                    act.wait_ge(self.s_h1p, i - 2)
                    nc.scalar.activation(self.h1[:, 0:width], self.h1_ps[:, 0:width], ACT.Relu,
                                         bias=conv_bias_col[:, :]).then_inc(self.s_h1, 1)

            def act_hid(self, act, i, g):
                if self.has(i, 1):
                    width = self.size(i - 1, g) * D
                    act.wait_ge(self.s_hidp, i)
                    for h in range(2):
                        last = nc.scalar.activation(self.hid[:, h, 0:width], self.hid_ps[h][:, 0:width], ACT.Relu, bias=hid_bias[:, :])
                    last.then_inc(self.s_hid, 1)

        dense_x3 = [sb(f"dense_x3_{par}", [P, G, D], F32) for par in (0, 1)]
        dense = Rows("dense", G, BLOCKS, DA[:, :], DC[:, :], [DB[:, :], DD[:, :]], dense_x3)
        dense_n2 = Norm(sb, sem, "dense_n2", G)
        dense_y = sb("dense_y", [P, G, D], F32)
        x_in = sb("x_in", [P, 2, G, D], F32)
        s_xin = [sem("s_xin0"), sem("s_xin1")]
        s_xout = sem("s_xout")
        s_stored = [sem("s_stored0"), sem("s_stored1")]
        s_h2 = sem("s_h2")
        link_d0, link_d1, link_d2 = Links(sem("s_link_d0"), 2), Links(sem("s_link_d1"), 1), Links(sem("s_link_d2"), 3)

        src_x3 = sb("src_x3", [P, TB, D], F32)
        srows = Rows("source", TB, BATCHES, DA[:, 0:TB * D], DC[:, 0:TB * D], [DB[:, 0:TB * D], EA[:, 0:TB * D]],
                     [src_x3, src_x3], hid[:, :, 0:TB * D],
                     spare=[pair[:, k // 2, :, :].rearrange("p j d -> p (j d)")[:, k % 2 * TB * D:(k % 2 + 1) * TB * D] for k in range(3)],
                     squares=[tail_f[:, :, :].rearrange("p j d -> p (j d)")[:, k * TB * D:(k + 1) * TB * D]
                              .rearrange("p (g d) -> p g d", d=D) for k in range(2)])
        src_x1 = sb("src_x1", [P, TB, D], F32)
        src_root = sb("src_root", [P, TB], F32)
        src_inv = sb("src_inv", [P, TB], F32)
        src_h1 = sb("src_h1", [P, TB, D], F32)
        s_root1 = sem("s_root1")
        s_x1s = sem("s_x1s")
        s_h1t = sem("s_h1t")
        s_h1o = sem("s_h1o")
        s_sst = [sem(f"s_sst{k}") for k in range(4)]
        link_s0, link_s1 = Links(sem("s_link_s0"), 3), Links(sem("s_link_s1"), 1)

        s_stage = sem("s_stage")
        s_row = [sem("s_row0"), sem("s_row1")]
        s_row3 = [sem("s_row3_0"), sem("s_row3_1")]
        s_mask = sem("s_mask")
        s_scat = [sem("s_scat0"), sem("s_scat1")]
        s_msgin = [sem("s_msgin0"), sem("s_msgin1")]
        s_dstin = [sem("s_dstin0"), sem("s_dstin1")]
        s_node = sem("s_node")
        s_slotin = [sem("s_slotin0"), sem("s_slotin1")]
        s_msg = sem("s_msg")
        s_same = sem("s_same")
        s_carry = sem("s_carry")
        s_sum = sem("s_sum")
        s_sums = sem("s_sums")
        s_new = sem("s_new")
        s_put = [sem("s_put0"), sem("s_put1")]
        s_scattered = [sem("s_scattered0"), sem("s_scattered1")]
        s_ownin = [sem("s_ownin0"), sem("s_ownin1")]
        link_l = Links(sem("s_link_look"), 2)
        link_b = {1: Links(sem("s_link_b1"), 5), 2: Links(sem("s_link_b2"), 3), 3: Links(sem("s_link_b3"), 6),
                  5: Links(sem("s_link_b5"), 3)}
        link_f = {3: Links(sem("s_link_f3"), 1), 4: Links(sem("s_link_f4"), 2), 5: Links(sem("s_link_f5"), 1)}
        s_look = sem("s_look")
        s_self_used = sem("s_self_used")
        s_tailf = sem("s_tailf"); s_tailp = sem("s_tailp"); s_pair = sem("s_pair"); s_pairt = sem("s_pairt")
        s_feat = sem("s_feat"); s_hidp = sem("s_hidp"); s_hide = sem("s_hide"); s_mp = sem("s_mp")
        s_agg = [sem("s_agg4"), sem("s_agg5")]
        s_aggt = [sem("s_aggt4"), sem("s_aggt5")]
        s_aggc = [sem("s_aggc4"), sem("s_aggc5")]
        s_conv = [sem("s_conv4"), sem("s_conv5")]
        s_deg = sem("s_deg"); s_deg2 = sem("s_deg2")

        NORM = {1: 0, 2: 1, 3: 2, 5: 3}

        def before(ph):
            return (ph - 1) * BATCHES

        def before_par(ph, par):
            return (ph - 1) * ((BATCHES + 1 - par) // 2)

        def has3(i, step):
            return not isinstance(i, int) or 0 <= i - step < BATCHES

        def norms(ph, n):
            return n + NORM[ph] * BATCHES

        def dense_rows(nodes, b, g):
            first = nodes[0:WHOLE * P * G, :].rearrange("(b p g) d -> b p g d", p=P, g=G)
            halves = nodes[WHOLE * P * G:WHOLE * P * G + (BLOCKS - WHOLE - 1) * P * HALF, :].rearrange(
                "(b p g) d -> b p g d", p=P, g=HALF)
            if isinstance(b, int) and b == BLOCKS - 1:
                return nodes[N - P * HALF:N, :].rearrange("(p g) d -> p g d", g=HALF)
            return first[b] if dense.size(b, g) == G else halves[b - WHOLE]

        def table_rows(k, b, half):
            t = table[k][half * E_PAD:(half + 1) * E_PAD, :].rearrange("(b j p) d -> b p j d", j=TB, p=P)
            return t[b]

        block = ctx.enter_context(nc.Block())

        @block.sync
        def _(sp):
            sp.wait_ge(s_zero, 1)
            full = E // RW
            rest = E - full * RW
            sp.dma_start(src_r[0:full, :], src[0:full * RW].rearrange("(r c) -> r c", c=RW)).then_inc(s_load_e, 16)
            sp.dma_start(src_r[full:full + 1, 0:rest], src[full * RW:E].rearrange("(r c) -> r c", r=1)).then_inc(s_load_e, 16)
            sp.dma_start(dst_r[0:full, :], dst[0:full * RW].rearrange("(r c) -> r c", c=RW)).then_inc(s_load_e, 16)
            sp.dma_start(dst_r[full:full + 1, 0:rest], dst[full * RW:E].rearrange("(r c) -> r c", r=1)).then_inc(s_load_e, 16)
            sp.dma_start(nxt_r[0:full, :], dst[1:full * RW + 1].rearrange("(r c) -> r c", c=RW)).then_inc(s_load_e, 16)
            sp.dma_start(nxt_r[full:full + 1, 0:rest - 1], dst[full * RW + 1:E].rearrange("(r c) -> r c", r=1)).then_inc(s_load_e, 16)
            sp.dma_start(weight_r[0:full, :], edge_weight[0:full * RW].rearrange("(r c) -> r c", c=RW)).then_inc(s_load_e, 16)
            sp.dma_start(weight_r[full:full + 1, 0:rest], edge_weight[full * RW:E].rearrange("(r c) -> r c", r=1)).then_inc(s_load_e, 16)
            sp.dma_start(slot_map.rearrange("(p c) a -> p (c a)", p=P), far_map[:, :]).then_inc(s_map0, 16)
            sp.wait_ge(s_rows, 1)
            sp.dma_start(dst_dram.rearrange("(r c) -> r c", c=RW), rows_f[:, 1, :]).then_inc(s_dstd, 16)
            sp.wait_ge(s_dstd, 16)

            dst_rows = dst_dram.rearrange("(b a c) -> b a c", a=1, c=TB * P)

            def dense_load(b, par, g):
                if at_least(b, 2):
                    wait(sp, (s_dstd, 16), dense.n0.s_centred, b - 1)
                sp.dma_start(x_in[:, par, 0:dense.size(b, g), :], dense_rows(x, b, g)).then_inc(s_xin[par], 16)

            def dense_store(b, par, g):
                wait(sp, (s_dstd, 16), s_xout, b + 1)
                if isinstance(b, int) and b == BLOCKS - 1:
                    sp.wait_ge(s_stored[1 - par], 16 * (BLOCKS // 2))
                sp.dma_start(dense_rows(out, b, g), x_out[:, par, 0:dense.size(b, g), :]).then_inc(s_stored[par], 16)

            def phase0(i, par, k):
                if at_least(i, 2):
                    wait(sp, (s_dstd, 16), s_mask, i - 1)
                sp.dma_start(dst_row[:, par, :], dst_rows[i].broadcast_to([P, TB * P])).then_inc(s_row[par], 16)
                dense_load(i, par, G)
                if at_least(i, 5):
                    dense_store(i - 5, 1 - par, G)
            batches(sp, phase0)

            def phase1(i, par, k):
                if srows.has(i, 2):
                    wait(sp, (s_dstd, 16), srows.s_x3, i - 1)
                    sp.dma_start(table_rows(3, i - 2, 1), src_x3[:, :, :]).then_inc(s_sst[2], 16)
                if srows.has(i, 0):
                    wait(sp, (s_dstd, 16), s_x1s, i + 1)
                    sp.dma_start(table_rows(2, i, 1), srows.x2[:, :, :]).then_inc(s_sst[1], 16)
                    sp.dma_start(table_rows(1, i, 1), src_x1[:, :, :]).then_inc(s_sst[0], 16)
                if srows.has(i, 3):
                    wait(sp, (s_dstd, 16), s_h1o, i - 2)
                    sp.dma_start(table_rows(4, i - 3, 1), src_h1[:, :, :]).then_inc(s_sst[3], 16)
                if srows.has(i, 1):
                    put(1, i - 1, *back(par, k, 1))

            def put(ph, i, par, k):
                wait(sp, (s_dstd, 16), s_new, i + 1 + before(ph))
                if ph > 1 or at_least(i, 2):
                    wait(sp, (s_dstd, 16), s_put[par], 16 * (k + before_par(ph, par)))
                rows = node[:, bass.ts(i, TB), :] if ph < 3 else new_row[:, par, :, :]
                sp.dma_start(table_rows(ph, i, 0), rows).then_inc(s_put[par], 16)

            batches(sp, phase1)
            after(phase1, 3)

            def phase2(i, par, k):
                dense_load(i + WHOLE, 1 - par, HALF)
                dense_store(i + WHOLE - 5, par, HALF)
                if at_least(i, 2):
                    put(2, i - 2, *back(par, k, 2))
            batches(sp, phase2)
            for b in range(BATCHES - 2, BATCHES):
                put(2, b, b % 2, b // 2)

            def phase3(i, par, k):
                if at_least(i, 2):
                    wait(sp, (s_dstd, 16), s_tailf, i - 1)
                sp.dma_start(dst_row[:, par, :], dst_rows[i].broadcast_to([P, TB * P])).then_inc(s_row3[par], 16)
                if at_least(i, 4):
                    put(3, i - 4, *back(par, k, 4))
            batches(sp, phase3)
            for b in range(BATCHES - 4, BATCHES):
                put(3, b, b % 2, b // 2)

            def phase4(i, par, k):
                dense_load(i + 2 * BATCHES, par, HALF)
                dense_store(i + 2 * BATCHES - 5, 1 - par, HALF)
                if at_least(i, 2):
                    put(4, i - 2, *back(par, k, 2))
            batches(sp, phase4)
            for b in range(BATCHES - 2, BATCHES):
                put(4, b, b % 2, b // 2)

            sp.wait_ge(s_put[0], 16 * before_par(5, 0))
            sp.wait_ge(s_put[1], 16 * before_par(5, 1))

            def phase5(i, par, k):
                if at_least(i, 2):
                    wait(sp, (s_dstd, 16), s_agg[1], i - 1)
                sp.dma_start(own_row[:, par, :, :], table_rows(4, i, 0)).then_inc(s_ownin[par], 16)
                if isinstance(i, int) and i < 5:
                    dense_store(i + BLOCKS - 5, par, HALF)
            batches(sp, phase5)

        @block.gpsimd
        def _(pool):
            nc.gpsimd.memset(far_map[:, :], FAR)
            nc.gpsimd.memset(src_r[:, :], 0)
            nc.gpsimd.memset(dst_r[:, :], PAD_DST)
            nc.gpsimd.memset(nxt_r[:, :], PAD_DST)
            nc.gpsimd.memset(weight_r[:, :], 0.0)
            nc.gpsimd.memset(w_conv[0][:, :], 0.0)
            nc.gpsimd.memset(w_conv[1][:, :], 0.0)
            for rows in bias_rows:
                nc.gpsimd.memset(rows, 0.0)
            nc.gpsimd.memset(ident[:, :], 0.0).then_inc(s_zero, 1)
            pool.wait_ge(s_zero, 1)
            nc.gpsimd.affine_select(out=ident[:, :], in_=ident[:, :], compare_op=ALU.not_equal, fill=1.0, base=0,
                                    pattern=[[-1, P]], channel_multiplier=1).then_inc(s_psel, 1)
            for h in range(2):
                pool.dma_start(w_self[64 * h:64 * h + 64, :], w_21[0:D, :]).then_inc(s_load_w, 16)
                pool.dma_start(w_part[64 * h:64 * h + 64, :], w_21[D:2 * D, :]).then_inc(s_load_w, 16)
                pool.dma_start(w_conv[0][64 * h:64 * h + 64, 64 * h:64 * h + 64], w_31).then_inc(s_load_w, 16)
                pool.dma_start(w_conv[1][64 * h:64 * h + 64, 64 * h:64 * h + 64], w_32).then_inc(s_load_w, 16)
                pool.dma_start(conv_bias_col[64 * h:64 * h + 64, :], b_31.rearrange("(d a) -> d a", a=1)).then_inc(s_load_w, 16)
            pool.dma_start(w_src_dst[:, :], w_21).then_inc(s_load_w, 16)
            pool.dma_start(w_out[:, :], w_22).then_inc(s_load_w, 16)
            pool.dma_start(hid_bias[:, :], b_21.rearrange("(d a) -> d a", a=1)).then_inc(s_load_w, 16)
            pool.dma_start(out_bias_bc[:, :], b_22.rearrange("(a d) -> a d", a=1).broadcast_to([P, D])).then_inc(s_load_w, 16)
            for rows, b in zip(bias_rows, (b_22, b_31, b_32)):
                for row in (0, 32, 64):
                    pool.dma_start(rows[row:row + 1, :, :], b.rearrange("(a g d) -> a g d", a=1, g=1).broadcast_to([1, G, D])).then_inc(s_load_w, 16)
            nc.gpsimd.iota(slot_i[:, :], pattern=[[P, TILES]], base=0, channel_multiplier=1).then_inc(s_psel, 1)
            nc.gpsimd.iota(own_i[:, :], pattern=[[P, TILES]], base=E_PAD, channel_multiplier=1).then_inc(s_psel, 1)
            pool.wait_ge(s_cols, 1)
            nc.gpsimd.affine_select(out=prev_f[:, :], in_=prev_f[:, :], compare_op=ALU.is_ge, fill=-1.0, base=-(P - 1),
                                    pattern=[[0, TILES]], channel_multiplier=1).then_inc(s_psel, 1)
            nc.gpsimd.affine_select(out=tail_key[:, :], in_=tail_key[:, :], compare_op=ALU.is_equal, fill=-1.0, base=0,
                                    pattern=[[1, RR], [0, 2]], channel_multiplier=-1).then_inc(s_psel, 1)
            pool.wait_ge(s_psel, 5)
            pool.wait_ge(s_map0, 16)

            def stage(pieces):
                for to, frm in pieces:
                    last = nc.gpsimd.tensor_copy(to, frm)
                last.then_inc(s_stage, 1)
                pool.wait_ge(s_stage, 1)

            def cols_of(t, i):
                return t[:, bass.ts(i, TB)]

            def gather(to, rows, idx, done):
                return pool.indirect_dma_start(out=to, out_offset=None, in_=rows,
                                               in_offset=bass.IndirectOffsetOnAxis(ap=idx, axis=0)).then_inc(done, 16)

            def phase0(i, par, k):
                pool.sem_clear(s_stage)
                if at_least(i, 2):
                    wait(pool, (s_psel, 5), s_scat[par], 16 * TB * k)
                    wait(pool, (s_psel, 5), s_node, i - 1)
                stage([(st_src[:, par, :], cols_of(scat_i, i)), (st_val[:, par, :], cols_of(slot_i, i)),
                       (st_dst[:, par, :], cols_of(dst_i, i))])
                for j in range(TB):
                    pool.indirect_dma_start(out=slot_map, out_offset=bass.IndirectOffsetOnAxis(ap=st_src[:, par, j:j + 1], axis=0),
                                            in_=st_val[:, par, j:j + 1], in_offset=None,
                                            bounds_check=MAP_ROWS - 1, oob_is_err=False).then_inc(s_scat[par], 16)
                for j in range(TB):
                    gather(x_dst[:, par, j, :], x, st_dst[:, par, j:j + 1], s_dstin[par])
            batches(pool, phase0)
            pool.wait_ge(s_scat[0], 16 * TB * ((BATCHES + 1) // 2))
            pool.wait_ge(s_scat[1], 16 * TB * (BATCHES // 2))

            def phase1(i, par, k):
                pool.sem_clear(s_stage)
                if at_least(i, 2):
                    wait(pool, (s_psel, 5), s_sum, TB * (i - 2) + 1 + TB * before(1))
                    wait(pool, (s_psel, 5), srows.n0.s_centred, i - 1)
                stage([(st_src[:, par, :], cols_of(src_i, i))])
                for j in range(TB):
                    gather(msg[:, par, j, 0:D], x, st_src[:, par, j:j + 1], s_msgin[par])
            batches(pool, phase1)
            for h in range(2):
                gather(tail_slot[:, h:h + 1], slot_map, key_i[:, h:h + 1], s_tails)

            def look_up(i, par):
                for j in range(TB):
                    gather(got_slot[:, par, j:j + 1], slot_map, st_val[:, par, j:j + 1], s_slotin[par])

            def scatter(i, par, k):
                pool.sem_clear(s_stage)
                if at_least(i, 2):
                    wait(pool, (s_psel, 5), s_scattered[par], 16 * TB * k)
                wait(pool, (s_psel, 5), s_new, i + 1 + before(5))
                stage([(st_dst[:, par, :], cols_of(scat_i, i))])
                for j in range(TB):
                    pool.indirect_dma_start(out=out, out_offset=bass.IndirectOffsetOnAxis(ap=st_dst[:, par, j:j + 1], axis=0),
                                            in_=new_row[:, par, j, :], in_offset=None,
                                            bounds_check=N - 1, oob_is_err=False).then_inc(s_scattered[par], 16)

            for ph in (2, 3, 4, 5):
                pool.wait_ge(s_put[0], 16 * before_par(ph, 0))
                pool.wait_ge(s_put[1], 16 * before_par(ph, 1))
                pool.wait_ge(s_sst[ph - 2], 16 * BATCHES)
                if ph == 2:
                    for b in (0, 1, 2):
                        pool.sem_clear(s_stage)
                        if b == 2:
                            pool.wait_ge(s_look, 1)
                        stage([(st_val[:, b % 2, :], cols_of(src_i, b))])
                        look_up(b, b % 2)
                if ph == 3:
                    pool.wait_ge(s_tails, 32)
                    for h in range(2):
                        pool.indirect_dma_start(out=tail[0:RR, h, 0:D], out_offset=None, in_=table[2],
                                                in_offset=bass.IndirectOffsetOnAxis(ap=tail_slot[:, h:h + 1], axis=0),
                                                bounds_check=2 * E_PAD - 1, oob_is_err=False).then_inc(s_tailr, 16)

                def phase(i, par, k, ph=ph):
                    pool.sem_clear(s_stage)
                    to = pair[:, par, :, 0:D] if ph == 3 else msg[:, par, :, 0:D]
                    places = [(st_src[:, par, :], cols_of(look_i, i))]
                    if at_least(i, 2):
                        if ph == 3:
                            wait(pool, (s_psel, 5), s_pairt, i - 1)
                        else:
                            wait(pool, (s_psel, 5), s_sum, TB * (i - 2) + 1 + TB * before(ph))
                    if ph == 2 and has3(i, -3):
                        wait(pool, (s_psel, 5), s_look, i + 2)
                        places.append((st_val[:, 1 - par, :], cols_of(src_i, i + 3)))
                    elif ph == 2:
                        wait(pool, (s_psel, 5), s_look, i + 1)
                    stage(places)
                    for j in range(TB):
                        gather(to[:, j, :], table[ph - 1], st_src[:, par, j:j + 1], s_msgin[par])
                    if ph == 2 and has3(i, -3):
                        look_up(i + 3, 1 - par)
                    if ph == 5 and isinstance(i, int) and i == 3:
                        pool.wait_ge(s_stored[0], 16 * (BLOCKS // 2 + 1))
                        pool.wait_ge(s_stored[1], 16 * (BLOCKS // 2))
                    if ph == 5 and at_least(i, 3):
                        scatter(i - 3, *back(par, k, 3))
                batches(pool, phase)
            for b in range(BATCHES - 3, BATCHES):
                scatter(b, b % 2, b // 2)
            pool.wait_ge(s_scattered[0], 16 * TB * ((BATCHES + 1) // 2))
            pool.wait_ge(s_scattered[1], 16 * TB * (BATCHES // 2))

        @block.scalar
        def _(act):
            act.wait_ge(s_prep, 1)

            act.wait_ge(s_load_w, 16 * 23)

            def same_mask(ph, i):
                if ph > 1 or at_least(i, 1):
                    act.wait_ge(s_sum, TB * (i - 1) + 1 + TB * before(ph))
                nc.scalar.activation(same_f[:, :, :], same8[:, bass.ts(i, TB), :], ACT.Copy).then_inc(s_same, 1)

            def carry_mask(ph, i):
                if ph > 1 or at_least(i, 1):
                    act.wait_ge(s_sum, TB * i + TB * before(ph))
                nc.scalar.activation(carry_f[:, :, :], carry8[:, bass.ts(i, TB), :], ACT.Copy).then_inc(s_carry, 1)

            def take_sums(ph, i, par, tiles):
                more = not isinstance(i, int) or i + 1 < BATCHES
                for j in tiles:
                    act.wait_ge(s_sum, TB * i + j + 1 + TB * before(ph))
                    nc.scalar.activation(sums[:, par, j, :], sums_ps[:, j, 0:D + 2], ACT.Copy).then_inc(s_sums, 1)
                    if j == 1 and more:
                        same_mask(ph, i + 1)
                    if j == TB - 1 and more:
                        carry_mask(ph, i + 1)

            def first_masks(ph):
                same_mask(ph, 0)
                carry_mask(ph, 0)

            def dense_steps(b, par, g, edge):
                dense.act_square3(act, b, par, g)
                dense.act_turned(act, b, g)
                edge[0]()
                dense.act_h1(act, b, g)
                edge[1]()
                if dense.has(b, 4):
                    dense_n2.act_square(nc, act, b - 4, g=dense.size(b - 4, g))
                dense.act_root3(act, b)
                if dense.has(b, 0):
                    dense.n0.act_square(nc, act, b, g=dense.size(b, g))
                dense.act_hid(act, b, g)
                edge[2]()
                if dense.has(b, 4):
                    dense_n2.act_root(nc, act, b - 4, eps[:, :])
                if dense.has(b, 0):
                    dense.n0.act_root(nc, act, b, eps_x2[:, :])
                edge[3]()

            def nothing():
                pass

            def phase0(i, par, k):
                def targets():
                    act.wait_ge(s_dstin[par], 16 * TB * (k + 1))
                    nc.scalar.activation(node[:, bass.ts(i, TB), :], x_dst[:, par, :, :], ACT.Copy).then_inc(s_node, 1)
                dense_steps(i, par, G, (nothing, nothing, nothing, targets))
            batches(act, phase0)

            act.wait_ge(s_mask, BATCHES)

            def edge_square(ph, i):
                en.act_square(nc, act, norms(ph, i))

            def edge_root(ph, i):
                en.act_root(nc, act, norms(ph, i), eps[:, :])

            def phase1(i, par, k):
                live, lag = srows.has(i, 0), srows.has(i, 1)
                srows.act_square3(act, i, par, TB)
                srows.act_turned(act, i, TB)
                if live:
                    take_sums(1, i, par, (0,))
                srows.act_h1(act, i, TB)
                if live:
                    srows.n0.act_square(nc, act, i)
                    take_sums(1, i, par, (1,))
                if lag:
                    edge_square(1, i - 1)
                srows.act_root3(act, i)
                srows.act_hid(act, i, TB)
                if live:
                    take_sums(1, i, par, (2,))
                    srows.n0.act_root(nc, act, i, eps_x2[:, :])
                    nc.scalar.activation(src_root[:, :], srows.n0.total[:, :], ACT.Sqrt, bias=eps_x1[:, :],
                                         scale=1.0 / D).then_inc(s_root1, 1)
                if lag:
                    edge_root(1, i - 1)
                if live:
                    take_sums(1, i, par, (3,))
                if srows.has(i, 3):
                    act.wait_ge(s_h1t, i - 2)
                    if at_least(i, 4):
                        act.wait_ge(s_sst[3], 16 * (i - 3))
                    nc.scalar.activation(src_h1[:, :, :], EC[:, 0:TB * D].rearrange("p (j d) -> p j d", d=D), ACT.Copy).then_inc(s_h1o, 1)
            first_masks(1)
            batches(act, phase1)
            after(phase1, 3)

            def phase2(i, par, k):
                def third():
                    take_sums(2, i, par, (2,))
                    if at_least(i, 1):
                        edge_square(2, i - 1)

                def fourth():
                    take_sums(2, i, par, (3,))
                    if at_least(i, 1):
                        edge_root(2, i - 1)
                dense_steps(i + WHOLE, 1 - par, HALF, (lambda: take_sums(2, i, par, (0,)),
                                                       lambda: take_sums(2, i, par, (1,)), third, fourth))
            first_masks(2)
            batches(act, phase2)
            edge_square(2, BATCHES - 1)
            edge_root(2, BATCHES - 1)

            act.wait_ge(s_deg, 1)
            nc.scalar.activation(inv_root[:, :], inv_deg[:, :], ACT.Sqrt).then_inc(s_deg2, 1)

            def phase3(i, par, k):
                turned, rest, norm = has3(i, 1), has3(i, 2), has3(i, 3)
                if rest:
                    act.wait_ge(s_mp, i - 1)
                    if at_least(i, 4):
                        act.wait_ge(s_self_used, i - 3)
                    nc.scalar.activation(msg[:, par, :, 0:D], EA[:, 0:TB * D].rearrange("p (j d) -> p j d", d=D), ACT.Copy)
                    nc.scalar.activation(selfs[:, par, :, :], EA[:, TB * D:2 * TB * D].rearrange("p (j d) -> p j d", d=D),
                                         ACT.Copy).then_inc(s_msg, 1)
                if turned:
                    act.wait_ge(s_pairt, i)
                    nc.scalar.activation(feat[:, :], EC[:, :], ACT.Copy).then_inc(s_feat, 1)
                if rest:
                    take_sums(3, i - 2, par, (0,))
                if rest:
                    take_sums(3, i - 2, par, (1,))
                if norm:
                    edge_square(3, i - 3)
                if turned:
                    act.wait_ge(s_hidp, i)
                    nc.scalar.activation(hid[:, 0, :], DD[:, :], ACT.Relu, bias=hid_bias[:, :])
                    nc.scalar.activation(hid[:, 1, :], DC[:, :], ACT.Relu, bias=hid_bias[:, :]).then_inc(s_hide, 1)
                if rest:
                    take_sums(3, i - 2, par, (2,))
                if norm:
                    edge_root(3, i - 3)
                if rest:
                    take_sums(3, i - 2, par, (3,))
            first_masks(3)
            batches(act, phase3)
            after(phase3, 3)

            def aggregate(ph, i):
                act.wait_ge(s_aggt[ph - 4], i + 1)
                nc.scalar.activation(feat[:, 0:TB * D], EA[:, 0:TB * D], ACT.Copy).then_inc(s_aggc[ph - 4], 1)

            def phase4(i, par, k):
                def sums_of(*tiles):
                    return lambda: take_sums(4, i, par, tiles)

                def second():
                    take_sums(4, i, par, (1,))
                    if at_least(i, 1):
                        aggregate(4, i - 1)
                dense_steps(i + 2 * BATCHES, par, HALF, (sums_of(0), second, sums_of(2), sums_of(3)))
            first_masks(4)
            batches(act, phase4)
            aggregate(4, BATCHES - 1)

            def phase5(i, par, k):
                if isinstance(i, int) and i < 5:
                    dense_steps(i + BLOCKS, 1 - par, HALF, (nothing,) * 4)
                live = not isinstance(i, int) or i < BATCHES
                if live:
                    take_sums(5, i, par, (0,))
                if has3(i, 1):
                    aggregate(5, i - 1)
                if live:
                    take_sums(5, i, par, (1,))
                if has3(i, 2):
                    edge_square(5, i - 2)
                if live:
                    take_sums(5, i, par, (2,))
                if has3(i, 2):
                    edge_root(5, i - 2)
                if live:
                    take_sums(5, i, par, (3,))
            first_masks(5)
            batches(act, phase5)
            after(phase5, 2)

        @block.tensor
        def _(pe):
            pe.wait_ge(s_psel, 1)
            pe.wait_ge(s_rows, 1)
            for q, row in enumerate((rows_f[:, 1, :], rows_f[:, 0, :], rows_f[:, 3, :], weight_r[:, :])):
                for h in range(2):
                    last = nc.tensor.transpose(psum[q][:, h * P:h * P + RR], row[:, h * P:(h + 1) * P], ident[0:RR, 0:RR])
            last.then_inc(s_ct, 1)
            pe.wait_ge(s_cc, 1)
            pe.wait_ge(s_wself, 1)

            def dense_products(b, par, g, others):
                def second(n, g):
                    pe.wait_ge(dense.s_h1, n + 1)
                    if at_least(n, 1):
                        pe.wait_ge(dense_n2.s_centred, n)
                    nc.tensor.matmul(ED[:, 0:g * D], ones[:, :], conv_bias[1][:, 0:g * D],
                                     start=True, stop=True)
                    for q in range(g // 2):
                        last = nc.tensor.matmul(ED[:, q * P:(q + 1) * P], dense.h1[:, q * P:(q + 1) * P], w_conv[1][:, :],
                                                start=False, stop=True, skip_group_check=True)
                    last.then_inc(s_h2, 1)
                dense.pe(pe, b, par, g, second, others)

            def nothing():
                pass

            def sum_within(ph, i, par, width, message_ready):
                pe.wait_ge(s_same, i + 1 + before(ph))
                message_ready()
                if ph > 1 or at_least(i, 1):
                    pe.wait_ge(s_sums, TB * i + TB * before(ph))
                for j in range(TB):
                    nc.tensor.matmul(sums_ps[:, j, 0:width], same_f[:, j, :], msg[:, par, j, 0:width], start=j == 0, stop=True,
                                     skip_group_check=True)

            def carry(ph, i, par, width, tiles):
                if 0 in tiles:
                    pe.wait_ge(s_carry, i + 1 + before(ph))
                for j in tiles:
                    carried = sums[:, par, j - 1, 0:width] if j else sums[:, 1 - par, TB - 1, 0:width]
                    if j:
                        pe.wait_ge(s_sums, TB * i + j + TB * before(ph))
                    nc.tensor.matmul(sums_ps[:, j, 0:width], carry_f[:, j, :], carried, start=False, stop=True,
                                     skip_group_check=True).then_inc(s_sum, 1)

            def keep_busy(bank, count):
                for _ in range(count):
                    nc.tensor.matmul(bank[:, :], ones[:, :], out_bias[:, :], start=True, stop=True)

            def phase0(i, par, k):
                dense_products(i, par, G, (nothing,) * 4)
            batches(pe, phase0)

            def gathered(ph, par, k):
                return lambda: pe.wait_ge(s_msgin[par], 16 * TB * (k + 1 + before_par(ph, par)))

            def phase1(i, par, k):
                def carried(*tiles):
                    return (lambda: carry(1, i, par, D + 2, tiles)) if srows.has(i, 0) else nothing

                def start():
                    if srows.has(i, 0):
                        sum_within(1, i, par, D + 2, gathered(1, par, k))
                    carried(0)()

                def rows_back(n, g):
                    pe.wait_ge(srows.s_h1, n + 1)
                    if at_least(n, 1):
                        pe.wait_ge(s_h1o, n)
                    for q in range(TB // 2):
                        last = nc.tensor.transpose(EC[:, q * P:(q + 1) * P], srows.h1[:, q * P:(q + 1) * P], ident[:, :])
                    last.then_inc(s_h1t, 1)
                keep_busy(DA, 4)
                srows.pe(pe, i, par, TB, rows_back, (start, carried(1), carried(2), carried(3)))
            batches(pe, phase1)
            after(phase1, 3)

            def phase2(i, par, k):
                def carried(*tiles):
                    return lambda: carry(2, i, par, D + 2, tiles)

                def start():
                    sum_within(2, i, par, D + 2, lambda: pe.wait_ge(s_msg, i + 1))
                    carried(0)()
                keep_busy(DA, 1)
                dense_products(i + WHOLE, 1 - par, HALF, (start, carried(1), carried(2), carried(3)))
            batches(pe, phase2)

            pe.wait_ge(s_tailr, 32)

            def phase3(i, par, k):
                first, turned, rest = has3(i, 0), has3(i, 1), has3(i, 2)
                if rest:
                    if at_least(i, 3):
                        pe.wait_ge(s_msg, i - 2 + BATCHES)
                    pe.wait_ge(s_hide, i - 1)
                    for h in range(2):
                        for j in range(TB):
                            last = nc.tensor.matmul(EA[:, (h * TB + j) * D:(h * TB + j + 1) * D], hid[:, h, j * P:(j + 1) * P], w_out[:, :],
                                                    start=h == 0 and j == 0, stop=True, skip_group_check=True)
                    last.then_inc(s_mp, 1)
                keep_busy(DD, 2)
                if turned:
                    pe.wait_ge(s_pair, i)
                    if at_least(i, 2):
                        pe.wait_ge(s_feat, i - 1)
                    for j in range(TB):
                        last = nc.tensor.transpose(EC[:, j * P:(j + 1) * P], pair[:, 1 - par, j, :], ident[:, :])
                    last.then_inc(s_pairt, 1)
                keep_busy(DD, 2)
                if rest:
                    sum_within(3, i - 2, par, D + 2, lambda: pe.wait_ge(s_msg, i - 1 + BATCHES))
                    carry(3, i - 2, par, D + 2, (0,))
                if turned:
                    pe.wait_ge(s_feat, i)
                    if at_least(i, 2):
                        pe.wait_ge(s_hide, i - 1)
                    nc.tensor.matmul(DD[:, :], w_src_dst[:, :], feat[:, :], start=True, stop=True)
                if rest:
                    carry(3, i - 2, par, D + 2, (1,))
                if turned:
                    nc.tensor.matmul(DC[:, :], w_self[D:2 * D, :], feat[D:2 * D, :], start=True, stop=True).then_inc(s_hidp, 1)
                if first:
                    pe.wait_ge(s_tailf, i + 1)
                    for j in range(TB):
                        last = nc.tensor.matmul(DA[:, j * P:j * P + D + 2], tail_f[:, j, :], tail[:, j % 2, :], start=True, stop=True)
                    last.then_inc(s_tailp, 1)
                if rest:
                    carry(3, i - 2, par, D + 2, (2, 3))
            batches(pe, phase3)
            after(phase3, 2)

            def aggregate(ph, i):
                pe.wait_ge(s_agg[ph - 4], i + 1)
                for q in range(TB // 2):
                    last = nc.tensor.transpose(EA[:, q * P:(q + 1) * P],
                                               edge_y[:, 2 * q:2 * q + 2, :].rearrange("p a d -> p (a d)"), ident[:, :])
                last.then_inc(s_aggt[ph - 4], 1)

            def convolve(ph, i, out_of_bank):
                if at_least(i, 1):
                    pe.wait_ge(*out_of_bank)
                nc.tensor.matmul(EC[:, 0:TB * D], ones[:, :], conv_bias[ph - 4][:, 0:TB * D],
                                 start=True, stop=True)
                pe.wait_ge(s_aggc[ph - 4], i + 1)
                for q in range(TB // 2):
                    last = nc.tensor.matmul(EC[:, q * P:(q + 1) * P], feat[:, q * P:(q + 1) * P], w_conv[ph - 4][:, :],
                                            start=False, stop=True, skip_group_check=True)
                last.then_inc(s_conv[ph - 4], 1)

            def convolve4(i):
                convolve(4, i, (s_new, i + before(4)))

            def phase4(i, par, k):
                def start():
                    sum_within(4, i, par, D + 2, gathered(4, par, k))
                    carry(4, i, par, D + 2, (0,))

                def turn():
                    carry(4, i, par, D + 2, (1,))
                    if at_least(i, 1):
                        aggregate(4, i - 1)

                def convolution():
                    carry(4, i, par, D + 2, (2,))
                    if at_least(i, 1):
                        convolve4(i - 1)

                dense_products(i + 2 * BATCHES, par, HALF, (start, turn, convolution, lambda: carry(4, i, par, D + 2, (3,))))
            batches(pe, phase4)
            aggregate(4, BATCHES - 1)
            convolve4(BATCHES - 1)

            def phase5(i, par, k):
                if isinstance(i, int) and i < 4:
                    dense_products(i + BLOCKS, 1 - par, HALF, (nothing,) * 4)
                live, rest = not isinstance(i, int) or i < BATCHES, has3(i, 1)
                if live:
                    sum_within(5, i, par, D + 2, gathered(5, par, k))
                    carry(5, i, par, D + 2, (0,))
                if rest:
                    aggregate(5, i - 1)
                if live:
                    carry(5, i, par, D + 2, (1, 2))
                if rest:
                    convolve(5, i - 1, (en.s_centred, norms(5, i - 1)))
                if live:
                    carry(5, i, par, D + 2, (3,))
            batches(pe, phase5)
            after(phase5, 1)

        @block.vector
        def _(dve):
            nc.vector.memset(eps[:, :], EPS)
            nc.vector.memset(eps_x1[:, :], EPS / 4)
            nc.vector.memset(eps_x2[:, :], EPS * EPS / 4)
            nc.vector.memset(msg[:, :, :, :], 1.0)
            nc.vector.memset(sums[:, :, :, :], 0.0)
            nc.vector.memset(tail[:, :, 0:D], 0.0)
            nc.vector.memset(tail[:, :, D:D + 2], 1.0)
            nc.vector.memset(tail_key[:, :], -1.0)
            nc.vector.memset(ones[:, :], 1.0).then_inc(s_pmem, 1)
            dve.wait_ge(s_pmem, 1)
            nc.vector.memset(prev_f[:, 0:1], -1.0).then_inc(s_prep, 1)
            dve.wait_ge(s_load_e, 16 * 8)
            link = Links(sem("s_link_p"), 19)
            link.begin(dve, 0)
            nc.vector.tensor_copy(rows_f[:, 0, :], src_r[:, :])
            nc.vector.tensor_copy(rows_f[:, 1, :], dst_r[:, :])
            link(nc.vector.tensor_copy(rows_f[:, 2, :], nxt_r[:, :]))
            link(nc.vector.tensor_tensor(same_r[:, :], rows_f[:, 1, :], rows_f[:, 2, :], ALU.is_equal))
            nc.vector.scalar_tensor_tensor(rows_f[:, 3, :], same_r[:, :], float(FAR), rows_f[:, 1, :], ALU.mult,
                                           ALU.add).then_inc(s_rows, 1)
            ends = rows_f[:, 1, :].rearrange("r (h c) -> r h c", h=2)[:, :, P - 1]
            goes = same_r[:, :].rearrange("r (h c) -> r h c", h=2)[:, :, P - 1]
            link(nc.vector.scalar_tensor_tensor(key_r[:, :], ends, 1.0, goes, ALU.add, ALU.mult))
            link(nc.vector.tensor_scalar(key_r[:, :], key_r[:, :], -1.0, None, ALU.add))
            nc.vector.tensor_copy(key_i[:, :], ends)
            nc.vector.tensor_copy(tail_key[0:RR, :].rearrange("k (r h) -> k r h", h=2),
                                  key_r[:, :].unsqueeze(1).broadcast_to([RR, RR, 2]))
            dve.wait_ge(s_ct, 1)
            for q in range(4):
                last = nc.vector.tensor_copy(cols[:, q, :].rearrange("p (r h) -> p h r", h=2),
                                             psum[q][:, 0:2 * P].rearrange("p (h r) -> p h r", h=2)[:, :, 0:RR])
            link(last)
            nc.vector.tensor_copy(src_i[:, :], cols[:, 1, :])
            nc.vector.tensor_scalar(dst_i[:, :], cols[:, 0, :], float(N - 1), None, ALU.min)
            nc.vector.tensor_copy(scat_i[:, :], cols[:, 2, :])
            nc.vector.tensor_copy(prev_f[:, 1:TILES], cols[:, 0, 0:TILES - 1]).then_inc(s_cc, 1)
            dve.wait_ge(s_cc, 1)
            nc.vector.tensor_copy(key_r[:, :], key_r[:, :]).then_inc(s_cols, 1)
            dve.wait_ge(s_psel, 5)
            nc.vector.tensor_copy(own_f[:, :], own_i[:, :])
            dve.wait_ge(s_load_w, 16 * 23)
            nc.vector.tensor_tensor(w_self[:, :], w_self[:, :], w_part[:, :], ALU.add)
            lw = Links(sem("s_link_w"), 9)
            lw.begin(dve, 0)
            nc.vector.memset(centring[:, :], 0.0)
            nc.vector.tensor_reduce(w_mean[:, 0:1], w_out[:, :], AX.X, ALU.add)
            lw(nc.vector.tensor_reduce(bias_mean[:, 0, :], bias_rows[0], AX.X, ALU.add))
            nc.vector.memset(centring[0:D, 0:D], -1.0 / D)
            nc.vector.memset(centring[D:2 * D, D:2 * D], -1.0 / D)
            nc.vector.tensor_scalar(w_mean[:, 1:2], w_mean[:, 0:1], 1.0 / D, None, ALU.mult)
            lw(nc.vector.tensor_scalar(bias_mean[:, 1, :], bias_mean[:, 0, :], 1.0 / D, None, ALU.mult))
            nc.vector.tensor_scalar(w_out_c[:, :], w_out[:, :], w_mean[:, 1:2], None, ALU.subtract)
            lw(nc.vector.tensor_tensor(bias_rows[0], bias_rows[0], bc(bias_mean[:, 1, :], P, G, D), ALU.subtract))
            lw(nc.vector.tensor_tensor(centring[:, :], centring[:, :], ident[:, :], ALU.add))
            rest = [part[:, :, :].rearrange("p j e -> p (j e)") for part in (same_f, carry_f, tail_f)]
            biases = [(to[:, :], frm.rearrange("p g d -> p (g d)"), left) for to, frm, left in
                      zip([out_bias] + conv_bias, bias_rows, rest)]
            for to, frm, left in biases:
                last = nc.vector.tensor_copy(to, frm)
            lw(last)
            for to, frm, left in biases:
                last = nc.vector.tensor_tensor(left, frm, to, ALU.subtract)
            lw(last)
            for to, frm, left in biases:
                nc.vector.tensor_copy(to[32:64, :], left[32:64, :])
                last = nc.vector.tensor_copy(to[64:96, :], left[64:96, :])
            lw(last)
            for to, frm, left in biases:
                last = nc.vector.tensor_tensor(left[64:96, :], left[64:96, :], to[64:96, :], ALU.subtract)
            lw(last)
            for to, frm, left in biases:
                last = nc.vector.tensor_copy(to[64:96, :], left[64:96, :])
            lw(last)
            lw.end()
            nc.vector.tensor_copy(w_mean[:, 0:1], w_mean[:, 1:2]).then_inc(s_wself, 1)

            def dense_first(b, par, k, g):
                if dense.has(b, 4):
                    g4 = dense.size(b - 4, g)
                    link_d2.begin(dve, b - 4)
                    dve.wait_ge(s_h2, b - 3)
                    link_d2(nc.vector.scalar_tensor_tensor(dense_y[:, 0:g4, :], ED[:, 0:g4 * D].rearrange("p (g d) -> p g d", d=D), 0.0,
                                                           dense_x3[par][:, 0:g4, :], ALU.max, ALU.add))
                    dense_n2.dve_centre(nc, link_d2, dense_y[:, 0:g4, :], g4)
                if dense.has(b, 2):
                    dense.n1.dve_total(nc, dve, b - 2, dense.size(b - 2, g))
                if dense.has(b, 0):
                    g0 = dense.size(b, g)
                    link_d0.begin(dve, b)
                    dve.wait_ge(s_xin[par], 16 * (k + 1))
                    dense.n0.dve_centre(nc, link_d0, x_in[:, par, 0:g0, :], g0)

            def dense_second(b, par, k, g):
                if dense.has(b, 4):
                    dense_n2.dve_total(nc, dve, b - 4, dense.size(b - 4, g))
                if dense.has(b, 2):
                    g2 = dense.size(b - 2, g)
                    link_d1.begin(dve, b - 2)
                    dense.n1.dve_scale(nc, dve, b - 2, link_d1, dense_x3[par][:, 0:g2, :], dense.rows(par), g2).then_inc(dense.s_x3, 1)
                    link_d1.end()
                if dense.has(b, 0):
                    dense.n0.dve_total(nc, dve, b, dense.size(b, g))

            def dense_third(b, par, k, g):
                if dense.has(b, 4):
                    g4 = dense.size(b - 4, g)
                    if at_least(b, 6):
                        dve.wait_ge(s_stored[par], 16 * (k - 2))
                    dense_n2.dve_scale(nc, dve, b - 4, link_d2, x_out[:, par, 0:g4, :], g=g4).then_inc(s_xout, 1)
                    link_d2.end()
                if dense.has(b, 0):
                    g0 = dense.size(b, g)
                    if at_least(b, 1):
                        dve.wait_ge(dense.s_turn, b)
                    dense.n0.dve_scale(nc, dve, b, link_d0, dense.x2[:, 0:g0, :], g=g0).then_inc(dense.s_x2, 1)
                    link_d0.end()

            def phase0(i, par, k):
                dense_first(i, par, k, G)
                dve.wait_ge(s_row[par], 16 * (k + 1))
                for j in range(TB):
                    row = dst_row[:, par, j * P:(j + 1) * P]
                    t = i * TB + j
                    for to, key in ((same8, cols[:, 0, bass.ds(t, 1)]), (carry8, prev_f[:, bass.ds(t, 1)])):
                        last = nc.vector.tensor_scalar(to[:, bass.ds(t, 1), :].rearrange("p a e -> p (a e)"), row, key, None, ALU.is_equal)
                    if j == 1:
                        dense_second(i, par, k, G)
                last.then_inc(s_mask, 1)
                dense_third(i, par, k, G)
            batches(dve, phase0)

            def edge_centre(ph, y):
                en.dve_centre(nc, link_b[ph], y)

            def edge_total(ph, i):
                en.dve_total(nc, dve, norms(ph, i))

            def phase1(i, par, k):
                pb, kb = back(par, k, 1)
                live, lag = srows.has(i, 0), srows.has(i, 1)
                lb = link_b[1]
                if srows.has(i, 2):
                    srows.n1.dve_total(nc, dve, i - 2)
                if live:
                    link_s0.begin(dve, i)
                    dve.wait_ge(s_msgin[par], 16 * TB * (k + 1 + before_par(1, par)))
                    srows.n0.dve_centre(nc, link_s0, msg[:, par, :, 0:D])
                if lag:
                    lb.begin(dve, i - 1)
                    wait(dve, (s_wself, 1), s_sums, TB * i + TB * before(1))
                    nc.vector.tensor_copy(count[:, bass.ts(i - 1, TB)], sums[:, pb, :, D])
                    lb(nc.vector.reciprocal(inv_count[:, :], sums[:, pb, :, D]))
                    lb(nc.vector.tensor_tensor(edge_z[:, :, :], sums[:, pb, :, 0:D], bc(inv_count[:, :], P, TB, D), ALU.mult))
                    lb(nc.vector.scalar_tensor_tensor(edge_y[:, :, :], node[:, bass.ts(i - 1, TB), :], 3.0, edge_z[:, :, :], ALU.mult, ALU.add))
                    edge_centre(1, edge_y[:, :, :])
                if live:
                    srows.n0.dve_total(nc, dve, i)
                if lag:
                    edge_total(1, i - 1)
                if srows.has(i, 2):
                    link_s1.begin(dve, i - 2)
                    if at_least(i, 3):
                        dve.wait_ge(s_sst[2], 16 * (i - 2))
                        dve.wait_ge(srows.s_turn3, i - 2)
                    srows.n1.dve_scale(nc, dve, i - 2, link_s1, src_x3[:, :, :], srows.rows(par)).then_inc(srows.s_x3, 1)
                    link_s1.end()
                if live:
                    if at_least(i, 1):
                        dve.wait_ge(s_sst[1], 16 * i)
                        dve.wait_ge(s_sst[0], 16 * i)
                        dve.wait_ge(srows.s_turn, i)
                    srows.n0.dve_scale(nc, dve, i, link_s0, srows.x2[:, :, :]).then_inc(srows.s_x2, 1)
                    dve.wait_ge(s_root1, i + 1)
                    link_s0(nc.vector.reciprocal(src_inv[:, :], src_root[:, :]))
                    nc.vector.tensor_tensor(src_x1[:, :, :], srows.n0.centred, bc(src_inv[:, :], P, TB, D), ALU.mult).then_inc(s_x1s, 1)
                    link_s0.end()
                if lag:
                    en.dve_scale(nc, dve, norms(1, i - 1), lb, node[:, bass.ts(i - 1, TB), :]).then_inc(s_new, 1)
                    lb.end()
            batches(dve, phase1)
            after(phase1, 3)

            def look(i, par, k):
                link_l.begin(dve, i)
                dve.wait_ge(s_slotin[par], 16 * TB * (k + 1))
                own = own_f[:, bass.ts(i, TB)]
                link_l(nc.vector.tensor_tensor(slot_d[:, 0, :], got_slot[:, par, :], own, ALU.subtract))
                link_l(nc.vector.scalar_tensor_tensor(slot_d[:, 1, :], got_slot[:, par, :], float(FAR), slot_d[:, 0, :], ALU.is_lt, ALU.mult))
                nc.vector.tensor_tensor(look_i[:, bass.ts(i, TB)], slot_d[:, 1, :], own, ALU.add).then_inc(s_look, 1)
                link_l.end()

            def weigh(i, par, k):
                dve.wait_ge(s_msgin[par], 16 * TB * (k + 1 + before_par(2, par)))
                m = msg[:, par, :, 0:D]
                nc.vector.tensor_tensor(m, m, bc(cols[:, 3, bass.ts(i, TB)], P, TB, D), ALU.mult).then_inc(s_msg, 1)

            def phase2(i, par, k):
                b, pd, kd = i + WHOLE, 1 - par, k + WHOLE // 2 + par
                edge, live = has3(i, 1), has3(i, 0)
                if has3(i, -3):
                    look(i + 3, 1 - par, k + 1 + par)
                if live:
                    dense_first(b, pd, kd, HALF)
                if edge:
                    link_b[2].begin(dve, i - 1)
                    dve.wait_ge(s_sums, TB * i + TB * before(2))
                    link_b[2](nc.vector.tensor_tensor(edge_y[:, :, :], sums[:, 1 - par, :, 0:D], node[:, bass.ts(i - 1, TB), :], ALU.add))
                    edge_centre(2, edge_y[:, :, :])
                if has3(i, -1):
                    weigh(i + 1, 1 - par, k + par)
                if live:
                    dense_second(b, pd, kd, HALF)
                if edge:
                    edge_total(2, i - 1)
                if live:
                    dense_third(b, pd, kd, HALF)
                if edge:
                    en.dve_scale(nc, dve, norms(2, i - 1), link_b[2], node[:, bass.ts(i - 1, TB), :]).then_inc(s_new, 1)
                    link_b[2].end()
            look(0, 0, 0)
            look(1, 1, 0)
            look(2, 0, 1)
            weigh(0, 0, 0)
            batches(dve, phase2)
            after(phase2, 1)

            lp = Links(sem("s_link_q"), 1)
            lp.begin(dve, 0)
            lp(nc.vector.tensor_scalar(inv_deg[:, :], count[:, :], 1.0, None, ALU.add))
            nc.vector.reciprocal(inv_deg[:, :], inv_deg[:, :]).then_inc(s_deg, 1)
            dve.wait_ge(s_deg2, 1)

            def tail_masks(i, par, k):
                dve.wait_ge(s_row3[par], 16 * (k + 1))
                if at_least(i, 1):
                    dve.wait_ge(s_tailp, i)
                for j in range(TB):
                    last = nc.vector.tensor_scalar(tail_f[:, j, :], dst_row[:, par, j * P:(j + 1) * P],
                                                   tail_key[:, bass.ds(i * TB + j, 1)], None, ALU.is_equal)
                last.then_inc(s_tailf, 1)

            def pairs(i, par, k):
                link_f[3].begin(dve, i)
                own = node[:, bass.ts(i, TB), :]
                dve.wait_ge(s_tailp, i + 1)
                tails = DA[:, :].rearrange("p (j d) -> p j d", j=TB)
                link_f[3](nc.vector.scalar_tensor_tensor(edge_z[:, :, :], bc(tails[:, :, D], P, TB, D), -1.0, own, ALU.add, ALU.mult))
                dve.wait_ge(s_msgin[par], 16 * TB * (k + 1 + before_par(3, par)))
                nc.vector.tensor_tensor(pair[:, par, :, D:2 * D], tails[:, :, 0:D], edge_z[:, :, :], ALU.subtract).then_inc(s_pair, 1)
                link_f[3].end()

            def targets3(i, par):
                lb = link_b[3]
                lb.begin(dve, i)
                dve.wait_ge(s_sums, TB * (i + 1) + TB * before(3))
                first = nc.vector.tensor_tensor(edge_y[:, :, :], sums[:, par, :, 0:D], selfs[:, par, :, :], ALU.add)
                first.then_inc(s_self_used, 1)
                dve.wait_ge(s_self_used, i + 1)
                lb(nc.vector.tensor_tensor(edge_y[:, :, :], edge_y[:, :, :], bc(inv_deg[:, bass.ts(i, TB)], P, TB, D), ALU.mult))
                lb(nc.vector.tensor_tensor(edge_y[:, :, :], edge_y[:, :, :], out_bias_bc[:, :].unsqueeze(1).broadcast_to([P, TB, D]), ALU.add))
                lb(nc.vector.tensor_tensor(edge_y[:, :, :], edge_y[:, :, :], node[:, bass.ts(i, TB), :], ALU.add))
                edge_centre(3, edge_y[:, :, :])

            def finish3(i, par, k):
                lb = link_b[3]
                own = node[:, bass.ts(i, TB), :]
                edge_total(3, i)
                if at_least(i, 2):
                    dve.wait_ge(s_put[par], 16 * (k + before_par(3, par)))
                lb(en.dve_scale(nc, dve, norms(3, i), lb, own))
                nc.vector.tensor_tensor(new_row[:, par, :, :], own, bc(inv_root[:, bass.ts(i, TB)], P, TB, D), ALU.mult).then_inc(s_new, 1)
                lb.end()

            def phase3(i, par, k):
                if has3(i, 1):
                    pairs(i - 1, *back(par, k, 1))
                if has3(i, 0):
                    tail_masks(i, par, k)
                if has3(i, 3):
                    targets3(i - 3, 1 - par)
                if has3(i, 3):
                    finish3(i - 3, *back(par, k, 3))
            batches(dve, phase3)
            after(phase3, 3)

            def convolved():
                return EC[:, 0:TB * D].rearrange("p (j d) -> p j d", d=D)

            def hidden4(i, par, k):
                dve.wait_ge(s_conv[0], i + 1)
                if at_least(i, 2):
                    dve.wait_ge(s_put[par], 16 * (k + before_par(4, par)))
                nc.vector.scalar_tensor_tensor(new_row[:, par, :, :], convolved(), 0.0,
                                               bc(inv_root[:, bass.ts(i, TB)], P, TB, D), ALU.max, ALU.mult).then_inc(s_new, 1)

            def phase4(i, par, k):
                b, kd = i + 2 * BATCHES, k + BATCHES
                if at_least(i, 2):
                    hidden4(i - 2, *back(par, k, 2))
                dense_first(b, par, kd, HALF)
                lf = link_f[4]
                lf.begin(dve, i)
                scale = bc(inv_root[:, bass.ts(i, TB)], P, TB, D)
                lf(nc.vector.tensor_tensor(edge_z[:, :, :], node[:, bass.ts(i, TB), :], scale, ALU.mult))
                dense_second(b, par, kd, HALF)
                dense_third(b, par, kd, HALF)
                dve.wait_ge(s_sums, TB * (i + 1) + TB * before(4))
                lf(nc.vector.tensor_tensor(edge_z[:, :, :], edge_z[:, :, :], sums[:, par, :, 0:D], ALU.add))
                if at_least(i, 1):
                    dve.wait_ge(s_aggt[0], i)
                nc.vector.tensor_tensor(edge_y[:, :, :], edge_z[:, :, :], scale, ALU.mult).then_inc(s_agg[0], 1)
                lf.end()
            batches(dve, phase4)
            for b in range(BATCHES - 2, BATCHES):
                hidden4(b, b % 2, b // 2)
            def targets5(i):
                link_b[5].begin(dve, i)
                dve.wait_ge(s_conv[1], i + 1)
                link_b[5](nc.vector.scalar_tensor_tensor(edge_z[:, :, :], convolved(), 0.0, node[:, bass.ts(i, TB), :], ALU.max, ALU.add))
                edge_centre(5, edge_z[:, :, :])

            def finish5(i, par, k):
                if at_least(i, 2):
                    dve.wait_ge(s_scattered[par], 16 * TB * k)
                en.dve_scale(nc, dve, norms(5, i), link_b[5], new_row[:, par, :, :]).then_inc(s_new, 1)
                link_b[5].end()

            def phase5(i, par, k):
                if isinstance(i, int) and i < 5:
                    for step in (dense_first, dense_second, dense_third):
                        step(i + BLOCKS, 1 - par, k + BLOCKS // 2 + par, HALF)
                live, rest = not isinstance(i, int) or i < BATCHES, has3(i, 2)
                if rest:
                    targets5(i - 2)
                    edge_total(5, i - 2)
                if live:
                    lf = link_f[5]
                    lf.begin(dve, i)
                    dve.wait_ge(s_sums, TB * (i + 1) + TB * before(5))
                    dve.wait_ge(s_ownin[par], 16 * (k + 1))
                    if at_least(i, 1):
                        dve.wait_ge(s_aggt[1], i)
                    lf(nc.vector.tensor_tensor(edge_y[:, :, :], own_row[:, par, :, :], sums[:, par, :, 0:D], ALU.add))
                    nc.vector.tensor_tensor(edge_y[:, :, :], edge_y[:, :, :], bc(inv_root[:, bass.ts(i, TB)], P, TB, D), ALU.mult).then_inc(s_agg[1], 1)
                    lf.end()
                if rest:
                    finish5(i - 2, *back(par, k, 2))
            batches(dve, phase5)
            after(phase5, 2)


_INS = ["x", "src", "dst", "edge_weight", "L2_gnn_W1", "L2_gnn_b1", "L2_gnn_W2", "L2_gnn_b2",
        "L3_gnn_W1", "L3_gnn_b1", "L3_gnn_W2", "L3_gnn_b2"]


def kernel(**inputs):
    import numpy as np
    import concourse.bacc as bacc
    from concourse.bass_utils import run_bass_kernel_spmd

    nc = bacc.Bacc("TRN2", target_bir_lowering=False, num_devices=1)
    arrays, args = {}, []
    for name in _INS:
        a = np.ascontiguousarray(inputs[name])
        arrays[f"in_{name}"] = a
        args.append(nc.dram_tensor(f"in_{name}", a.shape, mybir.dt.from_np(a.dtype), kind="ExternalInput").ap())
    args.append(nc.dram_tensor("out_rows", (N, D), F32, kind="ExternalOutput").ap())
    build(nc, *args)
    got = run_bass_kernel_spmd(nc, [arrays], core_ids=[0])
    return got.results[0]["out_rows"]
```
